# Optimizing a Trainium2 kernel written in Bass

```python
import numpy as np
import jax
import jax.numpy as jnp

def _softmax(x, axis=-1):
    return jax.nn.softmax(x, axis=axis)

def _gelu(x):
    return jax.nn.gelu(x, approximate=True)

def _silu(x):
    return jax.nn.silu(x)

def _sigmoid(x):
    return jax.nn.sigmoid(x)

def _layernorm(x, axis=-1, eps=1e-05):
    m = jnp.mean(x, axis=axis, keepdims=True)
    v = jnp.var(x, axis=axis, keepdims=True)
    return (x - m) / jnp.sqrt(v + eps)

def _scatter_add(tgt, idx, src, axis=0):
    return tgt.at[idx].add(src)

def _segment_sum(src, seg, n):
    return jax.ops.segment_sum(src, seg, n)
kernel_name = 'mk_flamingo_gated_d2_seqx_r4_929cd6'

def setup_inputs(seed: int=0):
    np.random.seed(seed)
    _w = jnp.asarray

    def _rec_inputs():
        import jax
        import jax.numpy as jnp
        _rk = jax.random.key(seed)
        x = -0.0002928 + 1 * jax.random.normal(jax.random.fold_in(_rk, 1), (1, 2048, 256), jnp.float32)
        _lenS = 2048 - jax.random.randint(jax.random.fold_in(_rk, 7), (1,), 0, max(1, 2048 // 4) + 1, jnp.int32)
        _lenS2 = 1601 - jax.random.randint(jax.random.fold_in(_rk, 8), (1,), 0, max(1, 1601 // 4) + 1, jnp.int32)
        _ctx_1024P = jax.random.normal(jax.random.fold_in(_rk, 11), (1, 16, 256), jnp.float32)
        _ctx_1024c = jax.random.dirichlet(jax.random.fold_in(_rk, 511), 0.3 * jnp.ones((16,), jnp.float32), (1, 1601))
        _ctx_1024t = jnp.einsum('bsk,bkd->bsd', _ctx_1024c, _ctx_1024P)
        _ctx_1024t = _ctx_1024t * jax.lax.rsqrt(jnp.mean(jnp.square(_ctx_1024t)) + 1e-12) * 0.953939
        ctx_1024 = -1.39393e-06 + 0.999914 * (_ctx_1024t + 0.3 * jax.random.normal(jax.random.fold_in(_rk, 611), (1, 1601, 256), jnp.float32))
        _validS = jnp.arange(2048)[None, :] < _lenS[:, None]
        _validS2 = jnp.arange(1601)[None, :] < _lenS2[:, None]
        _causal = jnp.tril(jnp.ones((2048, 2048), dtype=bool))
        mask_SxS2_ik0 = jnp.where(jnp.broadcast_to(_validS2[0:1, :], (2048, 1601)), 0, 1).astype(jnp.int32)
        _g = jax.random.normal(jax.random.fold_in(_rk, 9001), (2, 2), jnp.float32)
        _g = jnp.sign(_g) * jnp.maximum(jnp.abs(_g), 1.0) + (_g == 0) * 1.0
        g_xattn = _g[0]
        g_ffn = _g[1]
        return (x, ctx_1024, mask_SxS2_ik0, g_xattn, g_ffn)
    x, ctx_1024, mask_SxS2_ik0, g_xattn, g_ffn = _rec_inputs()

    def _L0_xattn_setup():
        import jax, jax.numpy as jnp
        import numpy as np
        import math
        D_MODEL = 256
        N_HEADS = 16
        key = jax.random.key(seed)
        ks = jax.random.split(key, 11)
        N, L, S = (2, 512, 512)
        d = D_MODEL
        s = 1.0 / math.sqrt(d)
        return {'queries': jax.random.normal(ks[0], (N, L, d), dtype=jnp.float32), 'keys': jax.random.normal(ks[1], (N, S, d), dtype=jnp.float32), 'values': jax.random.normal(ks[2], (N, S, d), dtype=jnp.float32), 'Wq': jax.random.normal(ks[3], (d, d), dtype=jnp.float32) * s, 'bq': jax.random.normal(ks[4], (d,), dtype=jnp.float32) * s, 'Wk': jax.random.normal(ks[5], (d, d), dtype=jnp.float32) * s, 'bk': jax.random.normal(ks[6], (d,), dtype=jnp.float32) * s, 'Wv': jax.random.normal(ks[7], (d, d), dtype=jnp.float32) * s, 'bv': jax.random.normal(ks[8], (d,), dtype=jnp.float32) * s, 'Wo': jax.random.normal(ks[9], (d, d), dtype=jnp.float32) * s, 'bo': jax.random.normal(ks[10], (d,), dtype=jnp.float32) * s}
    _L0_xattn_all = _L0_xattn_setup()
    _L0_xattn_in = {k: v for k, v in _L0_xattn_all.items() if k in ('Wq', 'bq', 'Wk', 'bk', 'Wv', 'bv', 'Wo', 'bo')}
    del _L0_xattn_all

    def _L0_ffn_setup():
        import jax, jax.numpy as jnp
        import numpy as np
        DIM = 256
        FF = 1024
        E = 8
        K = 2
        key = jax.random.key(seed)
        ks = jax.random.split(key, 6)
        x = jax.random.normal(ks[0], (4, 512, DIM), dtype=jnp.float32)
        wr = jax.random.normal(ks[1], (E, DIM), dtype=jnp.float32) * 0.02
        w1 = jax.random.normal(ks[2], (E, DIM, 2 * FF), dtype=jnp.float32) * 0.02
        b1 = jax.random.normal(ks[3], (E, 2 * FF), dtype=jnp.float32) * 0.02
        w2 = jax.random.normal(ks[4], (E, FF, DIM), dtype=jnp.float32) * 0.02
        b2 = jax.random.normal(ks[5], (E, DIM), dtype=jnp.float32) * 0.02
        return {'x': x, 'wr': wr, 'w1': w1, 'b1': b1, 'w2': w2, 'b2': b2}
    _L0_ffn_all = _L0_ffn_setup()
    _L0_ffn_in = {k: v for k, v in _L0_ffn_all.items() if k in ('wr', 'w1', 'b1', 'w2', 'b2')}
    del _L0_ffn_all

    def _L1_xattn_setup():
        import jax, jax.numpy as jnp
        import numpy as np
        D_MODEL = 256
        N_HEADS = 16
        D_K = D_MODEL // N_HEADS
        B, L = (4, 512)
        key = jax.random.key(seed)
        ks = jax.random.split(key, 12)
        s_in = 1.0 / np.sqrt(D_MODEL)
        inp = {'Q': jax.random.normal(ks[0], (B, L, D_MODEL), jnp.float32), 'K': jax.random.normal(ks[1], (B, L, D_MODEL), jnp.float32), 'V': jax.random.normal(ks[2], (B, L, D_MODEL), jnp.float32), 'attn_mask': jnp.tril(jnp.ones((L, L), jnp.int32)), 'Wq': jax.random.normal(ks[3], (D_MODEL, D_MODEL), jnp.float32) * s_in, 'bq': jnp.zeros((D_MODEL,), jnp.float32), 'Wk': jax.random.normal(ks[4], (D_MODEL, D_MODEL), jnp.float32) * s_in, 'bk': jnp.zeros((D_MODEL,), jnp.float32), 'Wv': jax.random.normal(ks[5], (D_MODEL, D_MODEL), jnp.float32) * s_in, 'bv': jnp.zeros((D_MODEL,), jnp.float32), 'Wo': jax.random.normal(ks[6], (D_MODEL, D_MODEL), jnp.float32) * s_in, 'bo': jnp.zeros((D_MODEL,), jnp.float32)}
        return inp
    _L1_xattn_all = _L1_xattn_setup()
    _L1_xattn_in = {k: v for k, v in _L1_xattn_all.items() if k in ('Wq', 'bq', 'Wk', 'bk', 'Wv', 'bv', 'Wo', 'bo')}
    del _L1_xattn_all

    def _L1_ffn_setup():
        import jax, jax.numpy as jnp
        import numpy as np
        B, S, D = (1, 512, 256)
        F = 352
        E = 16
        K = 2
        CAP_FACTOR = 1.25

        def _mlp(h, wg, wu, wd):
            return jax.nn.silu(h @ wg) * (h @ wu) @ wd
        key = jax.random.key(seed)
        ks = jax.random.split(key, 10)
        sd = 0.02
        return {'x': jax.random.normal(ks[0], (B, S, D), jnp.float32), 'router_w': jax.random.normal(ks[1], (D, E), jnp.float32) * sd, 'router_b': jnp.zeros((E,), jnp.float32), 'w_gate': jax.random.normal(ks[2], (E, D, F), jnp.float32) * sd, 'w_up': jax.random.normal(ks[3], (E, D, F), jnp.float32) * sd, 'w_down': jax.random.normal(ks[4], (E, F, D), jnp.float32) * sd, 'sw_gate': jax.random.normal(ks[5], (D, F), jnp.float32) * sd, 'sw_up': jax.random.normal(ks[6], (D, F), jnp.float32) * sd, 'sw_down': jax.random.normal(ks[7], (F, D), jnp.float32) * sd}
    _L1_ffn_all = _L1_ffn_setup()
    _L1_ffn_in = {k: v for k, v in _L1_ffn_all.items() if k in ('router_w', 'router_b', 'w_gate', 'w_up', 'w_down', 'sw_gate', 'sw_up', 'sw_down')}
    del _L1_ffn_all
    return {'x': x, 'ctx_1024': ctx_1024, 'mask_SxS2_ik0': mask_SxS2_ik0, 'g_xattn': g_xattn, 'g_ffn': g_ffn, 'L0_xattn_Wq': _L0_xattn_in['Wq'], 'L0_xattn_bq': _L0_xattn_in['bq'], 'L0_xattn_Wk': _L0_xattn_in['Wk'], 'L0_xattn_bk': _L0_xattn_in['bk'], 'L0_xattn_Wv': _L0_xattn_in['Wv'], 'L0_xattn_bv': _L0_xattn_in['bv'], 'L0_xattn_Wo': _L0_xattn_in['Wo'], 'L0_xattn_bo': _L0_xattn_in['bo'], 'L0_ffn_wr': _L0_ffn_in['wr'], 'L0_ffn_w1': _L0_ffn_in['w1'], 'L0_ffn_b1': _L0_ffn_in['b1'], 'L0_ffn_w2': _L0_ffn_in['w2'], 'L0_ffn_b2': _L0_ffn_in['b2'], 'L1_xattn_Wq': _L1_xattn_in['Wq'], 'L1_xattn_bq': _L1_xattn_in['bq'], 'L1_xattn_Wk': _L1_xattn_in['Wk'], 'L1_xattn_bk': _L1_xattn_in['bk'], 'L1_xattn_Wv': _L1_xattn_in['Wv'], 'L1_xattn_bv': _L1_xattn_in['bv'], 'L1_xattn_Wo': _L1_xattn_in['Wo'], 'L1_xattn_bo': _L1_xattn_in['bo'], 'L1_ffn_router_w': _L1_ffn_in['router_w'], 'L1_ffn_router_b': _L1_ffn_in['router_b'], 'L1_ffn_w_gate': _L1_ffn_in['w_gate'], 'L1_ffn_w_up': _L1_ffn_in['w_up'], 'L1_ffn_w_down': _L1_ffn_in['w_down'], 'L1_ffn_sw_gate': _L1_ffn_in['sw_gate'], 'L1_ffn_sw_up': _L1_ffn_in['sw_up'], 'L1_ffn_sw_down': _L1_ffn_in['sw_down']}

def reference(x, ctx_1024, mask_SxS2_ik0, g_xattn, g_ffn, L0_xattn_Wq, L0_xattn_bq, L0_xattn_Wk, L0_xattn_bk, L0_xattn_Wv, L0_xattn_bv, L0_xattn_Wo, L0_xattn_bo, L0_ffn_wr, L0_ffn_w1, L0_ffn_b1, L0_ffn_w2, L0_ffn_b2, L1_xattn_Wq, L1_xattn_bq, L1_xattn_Wk, L1_xattn_bk, L1_xattn_Wv, L1_xattn_bv, L1_xattn_Wo, L1_xattn_bo, L1_ffn_router_w, L1_ffn_router_b, L1_ffn_w_gate, L1_ffn_w_up, L1_ffn_w_down, L1_ffn_sw_gate, L1_ffn_sw_up, L1_ffn_sw_down):
    import jax
    import jax.numpy as jnp

    def _L0_xattn_ref(queries, keys, values, Wq, bq, Wk, bk, Wv, bv, Wo, bo):
        import jax, jax.numpy as jnp
        import numpy as np
        import math
        D_MODEL = 256
        N_HEADS = 16
        N, L, _ = queries.shape
        S = keys.shape[1]
        H = N_HEADS
        q = (queries @ Wq.T + bq).reshape(N, L, H, -1)
        k = (keys @ Wk.T + bk).reshape(N, S, H, -1)
        v = (values @ Wv.T + bv).reshape(N, S, H, -1)
        D = k.shape[-1]
        sm = jnp.einsum('nlhd,nshd->nlhs', q, k) / math.sqrt(D)
        causal_mask = jnp.triu(jnp.ones((L, S), dtype=bool), k=1)
        sm = jnp.where(causal_mask[None, :, None, :], -jnp.inf, sm)
        sm = jax.nn.softmax(sm, axis=-1)
        attn = jnp.einsum('nlhs,nshd->nlhd', sm, v)
        new_values = attn.reshape(N, L, H * D)
        return new_values @ Wo.T + bo

    def _L0_ffn_ref(x, wr, w1, b1, w2, b2):
        import jax, jax.numpy as jnp
        import numpy as np
        DIM = 256
        FF = 1024
        E = 8
        K = 2
        B, T, D = x.shape
        n_experts = wr.shape[0]
        xf = x.reshape(B * T, D)
        logits = xf @ wr.T
        topk_vals, topk_idx = jax.lax.top_k(logits, K)
        gates = jax.nn.softmax(topk_vals, axis=-1)
        out = jnp.zeros_like(xf)
        for e in range(n_experts):
            g_e = jnp.sum(jnp.where(topk_idx == e, gates, 0.0), axis=-1)
            u = xf @ w1[e] + b1[e]
            a, b = jnp.split(u, 2, axis=-1)
            h = jax.nn.silu(a) * b
            y_e = h @ w2[e] + b2[e]
            out = out + g_e[:, None] * y_e
        return out.reshape(B, T, D)

    def _L1_xattn_ref(Q, K, V, Wq, bq, Wk, bk, Wv, bv, Wo, bo, attn_mask):
        import jax, jax.numpy as jnp
        import numpy as np
        D_MODEL = 256
        N_HEADS = 16
        D_K = D_MODEL // N_HEADS
        B, L = (4, 512)
        Bq, Lq, D = Q.shape
        Lk = K.shape[1]
        q = (Q @ Wq.T + bq).reshape(Bq, Lq, N_HEADS, D_K).transpose(0, 2, 1, 3)
        k = (K @ Wk.T + bk).reshape(Bq, Lk, N_HEADS, D_K).transpose(0, 2, 1, 3)
        v = (V @ Wv.T + bv).reshape(Bq, Lk, N_HEADS, D_K).transpose(0, 2, 1, 3)
        scores = jnp.einsum('bhqd,bhkd->bhqk', q, k) / jnp.sqrt(jnp.float32(D_K))
        mask = attn_mask[None, None, :, :]
        scores = jnp.where(mask == 0, jnp.float32(-jnp.inf), scores)
        attn = jax.nn.softmax(scores, axis=-1)
        out = jnp.einsum('bhqk,bhkd->bhqd', attn, v)
        out = out.transpose(0, 2, 1, 3).reshape(Bq, Lq, D)
        return out @ Wo.T + bo

    def _L1_ffn_ref(x, router_w, router_b, w_gate, w_up, w_down, sw_gate, sw_up, sw_down):
        import jax, jax.numpy as jnp
        import numpy as np
        B, S, D = (1, 512, 256)
        F = 352
        E = 16
        K = 2
        CAP_FACTOR = 1.25

        def _mlp(h, wg, wu, wd):
            return jax.nn.silu(h @ wg) * (h @ wu) @ wd
        b, s, d = x.shape
        N = b * s
        NK = N * K
        C = int(np.ceil(CAP_FACTOR * NK / E))
        x_tokens = x.reshape(N, d)
        logits = x_tokens @ router_w + router_b
        probs = jax.nn.softmax(logits, axis=-1)
        vals, idx = jax.lax.top_k(probs, K)
        vals = vals / (jnp.sum(vals, axis=-1, keepdims=True) + 1e-09)
        idx_flat = idx.reshape(NK)
        vals_flat = vals.reshape(NK)
        oh_e = jax.nn.one_hot(idx_flat, E, dtype=x.dtype)
        pos = (jnp.cumsum(oh_e, axis=0) * oh_e).sum(axis=1) - 1
        within = (pos < C).astype(x.dtype)
        pos_c = jnp.clip(pos, 0, C - 1).astype(jnp.int32)
        token_ids = jnp.arange(NK) // K
        x_pair = x_tokens[token_ids] * within[:, None]
        expert_inputs = jnp.zeros((E, C, d), x.dtype).at[idx_flat, pos_c].add(x_pair)
        expert_outputs = jax.vmap(_mlp)(expert_inputs, w_gate, w_up, w_down)
        gathered = expert_outputs[idx_flat, pos_c] * (vals_flat * within)[:, None]
        output_tokens = gathered.reshape(N, K, d).sum(axis=1)
        return x + _mlp(x, sw_gate, sw_up, sw_down) + output_tokens.reshape(b, s, d)
    x = x + jnp.tanh(g_xattn[0]) * _L0_xattn_ref(_layernorm(x, axis=-1), ctx_1024, ctx_1024, L0_xattn_Wq, L0_xattn_bq, L0_xattn_Wk, L0_xattn_bk, L0_xattn_Wv, L0_xattn_bv, L0_xattn_Wo, L0_xattn_bo)
    x = x + jnp.tanh(g_ffn[0]) * _L0_ffn_ref(_layernorm(x, axis=-1), L0_ffn_wr, L0_ffn_w1, L0_ffn_b1, L0_ffn_w2, L0_ffn_b2)
    x = x + jnp.tanh(g_xattn[1]) * _L1_xattn_ref(_layernorm(x, axis=-1), ctx_1024, ctx_1024, L1_xattn_Wq, L1_xattn_bq, L1_xattn_Wk, L1_xattn_bk, L1_xattn_Wv, L1_xattn_bv, L1_xattn_Wo, L1_xattn_bo, mask_SxS2_ik0)
    x = x + jnp.tanh(g_ffn[1]) * _L1_ffn_ref(_layernorm(x, axis=-1), L1_ffn_router_w, L1_ffn_router_b, L1_ffn_w_gate, L1_ffn_w_up, L1_ffn_w_down, L1_ffn_sw_gate, L1_ffn_sw_up, L1_ffn_sw_down)
    return x

_drawn_inputs = setup_inputs


def setup_inputs(seed=0):
    import zlib

    import numpy as np

    out = dict(_drawn_inputs(seed))
    spreads = {'g_ffn': (-1.0, 0.2),
     'L1_xattn_bq': (0.0, 0.485),
     'L1_xattn_bk': (0.0, 2.0),
     'L1_xattn_bv': (0.0, 0.1),
     'L1_xattn_bo': (0.0, 0.1),
     'L1_ffn_router_b': (0.0, 2.0)}
    factors = {'L0_xattn_bq': 6.317,
     'L0_xattn_bk': 64.0,
     'L0_ffn_wr': 3.591,
     'L0_ffn_w1': 3.6,
     'L0_ffn_b1': 8.0,
     'L0_ffn_w2': 3.595,
     'L0_ffn_b2': 5.994,
     'L1_ffn_router_w': 15.111,
     'L1_ffn_w_gate': 5.195,
     'L1_ffn_w_up': 5.176,
     'L1_ffn_w_down': 5.146,
     'L1_ffn_sw_gate': 2.849,
     'L1_ffn_sw_up': 2.883,
     'L1_ffn_sw_down': 2.852}
    for name, (base, spread) in spreads.items():
        noise = np.random.default_rng([zlib.crc32(name.encode()), seed]).standard_normal(out[name].shape)
        drawn = base * np.exp(spread * noise) if base else spread * noise
        out[name] = jnp.asarray(drawn.astype(out[name].dtype))
    for name, factor in factors.items():
        out[name] = (out[name] * factor).astype(out[name].dtype)
    return out
```

```python
from contextlib import ExitStack, contextmanager

import numpy as np

import concourse.bass as bass
from concourse import mybir

F32 = mybir.dt.float32
BF16 = mybir.dt.bfloat16
I32 = mybir.dt.int32
U32 = mybir.dt.uint32
ALU = mybir.AluOpType
ACT = mybir.ActivationFunctionType
AX = mybir.AxisListType

P = 128
T = 2048
D = 256
KD = D // P
S = 1601
NQT = T // P
H = 16
DH = D // H
NKT = -(-S // P)
QC = 512
NC = T // QC
QTC = QC // P
SP_ = S + 1
EPS = 1e-5
MASKED = -1e30
DEAD = -1e29
PAIRS = ((0, 0), (0, 1), (1, 0), (0, 2), (1, 1), (2, 0))
NB = len(PAIRS) * DH
RB = NB
RM = NB + 1
KA = NB + 1
KC = NB + 4
G = 4
NV = DH + 1
SLOTS = 4
LAG = 2

E0, F0 = 8, 1024
E1, F1 = 16, 352
CAP = -(-5 * 2 * T // (4 * E1))
ROWS = E1 * CAP
NT0 = ROWS // P
FAR = 1 << 20
assert NT0 >= 2 * T // P + E0 - 1


def key_tiles(first=0):
    return [(j * P, min(P, S - j * P)) for j in range(first, NKT)]


def groups_of(n, most):
    k = -(-n // most)
    out, at = [], 0
    for i in range(k):
        m = n // k + (i < n % k)
        out.append((at, m))
        at += m
    return out


def build(nc, x_d, ctxT_d, mask_d, maskT_d, gx_d, gf_d, W, F, out_d, stop=None):
    ctx = ExitStack()

    def sb(stack, name, shape, dt=F32):
        return stack.enter_context(nc.sbuf_tensor(name, shape, dt))

    layer_sems = []

    def sem(name):
        layer_sems.append(nc.alloc_semaphore(name=name))
        return layer_sems[-1]

    def free_semaphores():
        nc.clear_and_free_semaphores(layer_sems)
        nc.all_engine_barrier()
        layer_sems.clear()

    def scratch(name, shape, dt):
        return nc.dram_tensor(name, shape, dt, kind="Internal").ap()

    with ctx:
        psA = ctx.enter_context(nc.psum_tensor("psA", [P, 2, 512], F32))
        psC = ctx.enter_context(nc.psum_tensor("psC", [P, 2, 1024], F32))
        psO = ctx.enter_context(nc.psum_tensor("psO", [P, 2, 512], F32))

        def bank(i):
            if i < 2:
                return psA[:, i, :]
            if i < 6:
                return psC[:, (i - 2) // 2, (i % 2) * 512:(i % 2) * 512 + 512]
            return psO[:, i - 6, :]

        xres = sb(ctx, "xres", [P, NQT, D])
        ident = sb(ctx, "ident", [P, P])
        identb = sb(ctx, "identb", [P, P], BF16)
        causb = sb(ctx, "causb", [P, P], BF16)
        gates = sb(ctx, "gates", [P, 4])
        causbT = sb(ctx, "causbT", [P, P], BF16)
        stats = sb(ctx, "stats", [P, NQT, 6])
        lnw = sb(ctx, "lnw", [P, 6, NQT])

        c_ld, c_ms, c_id, c_tanh = sem("const_loaded"), sem("const_memset"), sem("const_made"), sem("tanh_done")
        with nc.Block() as block:
            @block.sync
            def _(sp):
                sp.dma_start(xres[:, :, :], x_d.rearrange("(t p) d -> p t d", p=P)).then_inc(c_ld, 16)
                sp.dma_start(gates[:, 0:2], gx_d.rearrange("(a n) -> a n", a=1).to_broadcast([P, 2])).then_inc(c_ld, 16)
                sp.dma_start(gates[:, 2:4], gf_d.rearrange("(a n) -> a n", a=1).to_broadcast([P, 2])).then_inc(c_ld, 16)
                sp.wait_ge(c_ld, 48)

            @block.scalar
            def _(act):
                act.wait_ge(c_ld, 48)
                act.activation(gates[:, :], gates[:, :], ACT.Tanh).then_inc(c_tanh, 1)

            @block.gpsimd
            def _(pool):
                pool.memset(ident[:, :], 0.0).then_inc(c_ms, 1)
                pool.memset(identb[:, :], 0.0).then_inc(c_ms, 1)
                pool.memset(causb[:, :], 0.0).then_inc(c_ms, 1)
                pool.memset(causbT[:, :], 0.0).then_inc(c_ms, 1)
                pool.wait_ge(c_ms, 4)
                pool.affine_select(out=causbT[:, :], in_=causbT[:, :], compare_op=ALU.is_ge, fill=MASKED,
                                   base=0, pattern=[[1, P]], channel_multiplier=-1).then_inc(c_id, 1)
                for m in (ident, identb):
                    pool.affine_select(out=m[:, :], in_=m[:, :], compare_op=ALU.not_equal, fill=1.0,
                                       base=0, pattern=[[-1, P]], channel_multiplier=1).then_inc(c_id, 1)
                pool.affine_select(out=causb[:, :], in_=causb[:, :], compare_op=ALU.is_ge, fill=MASKED,
                                   base=0, pattern=[[-1, P]], channel_multiplier=1).then_inc(c_id, 1)

        def norm_vector(dve, xn, chain, tag_sqrt, tag_var):
            n = [0]

            def link(ins):
                n[0] += 1
                ins.then_inc(chain, 1)
                dve.wait_ge(chain, n[0])

            with dve.Fori(0, NQT) as t:
                dve.bn_stats(stats[:, bass.ds(t, 1), :].rearrange("p a b -> p (a b)"),
                             xres[:, bass.ds(t, 1), :].rearrange("p a b -> p (a b)")).then_inc(chain, 1)
            n[0] = NQT
            dve.wait_ge(chain, NQT)
            me, ve, mo, vo = (stats[:, :, i] for i in (1, 2, 4, 5))
            mean, diff, var, std, rstd, tmp = (lnw[:, i, :] for i in range(6))
            link(dve.tensor_tensor(mean, me, mo, ALU.add))
            link(dve.tensor_scalar(mean, mean, 0.5, None, ALU.mult))
            link(dve.tensor_tensor(diff, me, mo, ALU.subtract))
            link(dve.tensor_tensor(diff, diff, diff, ALU.mult))
            link(dve.tensor_tensor(var, ve, vo, ALU.add))
            link(dve.tensor_scalar(var, var, 1.0 / D, EPS, ALU.mult, ALU.add))
            dve.scalar_tensor_tensor(out=var, in0=diff, scalar=0.25, in1=var, op0=ALU.mult, op1=ALU.add)\
               .then_inc(tag_var, 1)
            dve.wait_ge(tag_sqrt, 1)
            link(dve.reciprocal(rstd, std))
            with dve.Fori(0, NQT) as t:
                dve.tensor_scalar(xn[:, bass.ds(t, 1), :].rearrange("p a b -> p (a b)"),
                                  xres[:, bass.ds(t, 1), :].rearrange("p a b -> p (a b)"),
                                  lnw[:, 0, bass.ds(t, 1)], lnw[:, 4, bass.ds(t, 1)],
                                  ALU.subtract, ALU.mult).then_inc(chain, 1)
            return n[0] + NQT

        def projections(L, Kst, Vaug, Qs, Ks):
            with ExitStack() as st:
                w = W[L]
                xn = sb(st, f"xn{L}", [P, NQT, D])
                xT = sb(st, f"xT{L}", [P, KD, T])
                cT = sb(st, f"cT{L}", [P, KD, S])
                wq, wk, wv = (sb(st, f"w{n}{L}", [P, KD, D]) for n in "qkv")
                bqk = sb(st, f"bqk{L}", [P, 2, KD])
                bvb = sb(st, f"bvb{L}", [P, D])
                kf = sb(st, f"kf{L}", [P, T])
                rest = sb(st, f"rest{L}", [P, T])
                parts = sb(st, f"parts{L}", [P, 3, T], BF16)
                ld, ldv, ldx = sem(f"p{L}_k_loaded"), sem(f"p{L}_v_loaded"), sem(f"p{L}_q_loaded")
                vones = sem(f"p{L}_v_ones")
                mm, ev = sem(f"p{L}_kq_done"), sem(f"p{L}_kq_evacuated")
                vmm, vev = sem(f"p{L}_v_done"), sem(f"p{L}_v_evacuated")
                spl, sto = sem(f"p{L}_split"), sem(f"p{L}_stored")
                lnc, lns, lnv = sem(f"p{L}_ln"), sem(f"p{L}_ln_sqrt"), sem(f"p{L}_ln_var")
                bq4, tr, tre = sem(f"p{L}_bq_scaled"), sem(f"p{L}_transposed"), sem(f"p{L}_xT")
                chain = sem(f"p{L}_chain")
                kload = sem(f"p{L}_kstack")
                kcols = [(a, n) for a, n in groups_of(S, 512)]
                NKP = len(kcols)
                xn_done = 2 * NQT + 7

                with nc.Block() as block:
                    @block.sync
                    def _(sp):
                        for dst, src in ((cT[:, :, :], ctxT_d.rearrange("(k p) s -> p k s", p=P)),
                                         (wk[:, :, :], w["WkT"].rearrange("(k p) n -> p k n", p=P)),
                                         (bqk[:, 1, :], w["bk"].rearrange("(m p) -> p m", p=P))):
                            with nc.allow_non_contiguous_dma(reason="bias columns"):
                                sp.dma_start(dst, src).then_inc(ld, 16)
                        sp.dma_start(wv[:, :, :], w["WvT"].rearrange("(k p) n -> p k n", p=P)).then_inc(ldv, 16)
                        sp.dma_start(bvb[:, :], w["bv"].rearrange("(a n) -> a n", a=1).to_broadcast([P, D]))\
                          .then_inc(ldv, 16)
                        sp.dma_start(wq[:, :, :], w["WqT"].rearrange("(k p) n -> p k n", p=P)).then_inc(ldx, 16)
                        with nc.allow_non_contiguous_dma(reason="bias columns"):
                            sp.dma_start(bqk[:, 0, :], w["bq"].rearrange("(m p) -> p m", p=P)).then_inc(ldx, 16)
                        for m in range(KD):
                            sp.wait_ge(spl, m + 1)
                            sp.dma_start(Ks[:, m * P:(m + 1) * P, :].rearrange("t p s -> p t s"),
                                         parts[:, :, 0:S]).then_inc(sto, 16)
                        sp.wait_ge(sto, 32)
                        for b, (_, kp) in enumerate(PAIRS):
                            sp.dma_start(Kst[b * DH:(b + 1) * DH, :, 0:S],
                                         Ks[kp].rearrange("(h d) s -> d h s", d=DH)).then_inc(kload, 16)
                        for m in range(KD):
                            sp.wait_ge(spl, KD + m + 1)
                            sp.dma_start(Qs[:, m * P:(m + 1) * P, :].rearrange("t p s -> p t s"),
                                         parts[:, :, :]).then_inc(sto, 16)
                        sp.wait_ge(sto, 64)
                        sp.wait_ge(kload, 16 * len(PAIRS))

                    @block.gpsimd
                    def _(pool):
                        pool.memset(Vaug[:, :, :, :], 1.0).then_inc(vones, 1)
                        pool.wait_ge(vones, 1)
                        pool.memset(Kst[NB:NB + 4, :, :], 1.0).then_inc(vones, 1)
                        pool.wait_ge(vones, 2)
                        pool.memset(Kst[RB:RB + 1, :, :], 0.0).then_inc(vones, 1)

                    @block.scalar
                    def _(act):
                        act.wait_ge(ld, 48)
                        n = 0
                        for m in range(KD):
                            if m:
                                act.wait_ge(chain, 4 * m)
                            for a, c in kcols:
                                act.wait_ge(mm, n + 1)
                                act.activation(kf[:, a:a + c], bank(n % 4)[:, 0:c], ACT.Identity,
                                               bias=bqk[:, 1, m:m + 1]).then_inc(ev, 1)
                                n += 1
                        act.wait_ge(lnv, 1)
                        act.activation(lnw[:, 3, :], lnw[:, 2, :], ACT.Sqrt).then_inc(lns, 1)
                        act.wait_ge(ldx, 32)
                        act.activation(bqk[:, 0, :], bqk[:, 0, :], ACT.Copy, scale=0.25).then_inc(bq4, 1)
                        for i in range(8):
                            act.wait_ge(tr, i + 1)
                            k, g = i % 2, i // 2
                            act.activation(xT[:, k, g * 512:(g + 1) * 512], bank(i % 2)[:, :], ACT.Copy)\
                               .then_inc(tre, 1)
                        act.wait_ge(bq4, 1)
                        for m in range(KD):
                            act.wait_ge(chain, 4 * (KD + m))
                            for c in range(NC):
                                act.wait_ge(mm, n + 1)
                                act.activation(kf[:, c * QC:(c + 1) * QC], bank(n % 4)[:, :], ACT.Identity,
                                               bias=bqk[:, 0, m:m + 1], scale=0.25).then_inc(ev, 1)
                                n += 1

                    @block.tensor
                    def _(pe):
                        pe.wait_ge(ld, 48)
                        n = 0
                        for m in range(KD):
                            for a, c in kcols:
                                if n >= 4:
                                    pe.wait_ge(ev, n - 3)
                                for k in range(KD):
                                    mmi = pe.matmul(bank(n % 4)[:, 0:c], wk[:, k, m * P:(m + 1) * P],
                                                    cT[:, k, a:a + c], start=(k == 0), stop=(k == KD - 1))
                                mmi.then_inc(mm, 1)
                                n += 1
                        pe.wait_ge(ldv, 32)
                        for j, (k0, kw) in enumerate(key_tiles()):
                            if j >= 2:
                                pe.wait_ge(vev, j - 1)
                            for k in range(KD):
                                mmi = pe.matmul(bank(6 + j % 2)[0:kw, 0:D], cT[:, k, k0:k0 + kw], wv[:, k, :],
                                                start=(k == 0), stop=(k == KD - 1))
                            mmi.then_inc(vmm, 1)
                        pe.wait_ge(lns, 1)
                        pe.wait_ge(ev, 2 * NKP)
                        for i in range(8):
                            k, g = i % 2, i // 2
                            if i >= 2:
                                pe.wait_ge(tre, i - 1)
                            pe.wait_ge(lnc, xn_done - NQT + 4 * g + 4)
                            for q in range(4):
                                mmi = pe.transpose(bank(i % 2)[:, q * P:(q + 1) * P],
                                                   xn[:, 4 * g + q, k * P:(k + 1) * P], ident[:, :])
                            mmi.then_inc(tr, 1)
                        pe.wait_ge(tre, 8)
                        pe.wait_ge(ldx, 32)
                        for m in range(KD):
                            for c in range(NC):
                                if n >= 4:
                                    pe.wait_ge(ev, n - 3)
                                for k in range(KD):
                                    mmi = pe.matmul(bank(n % 4)[:, :], wq[:, k, m * P:(m + 1) * P],
                                                    xT[:, k, c * QC:(c + 1) * QC], start=(k == 0), stop=(k == KD - 1))
                                mmi.then_inc(mm, 1)
                                n += 1

                    def split(dve, cols, i, n_ev):
                        dve.wait_ge(ev, n_ev)
                        if i:
                            dve.wait_ge(sto, 16 * i)
                        n = 4 * i
                        dve.tensor_copy(parts[:, 0, cols], kf[:, cols]).then_inc(chain, 1)
                        dve.wait_ge(chain, n + 1)
                        dve.tensor_tensor(rest[:, cols], kf[:, cols], parts[:, 0, cols], ALU.subtract).then_inc(chain, 1)
                        dve.wait_ge(chain, n + 2)
                        dve.tensor_copy(parts[:, 1, cols], rest[:, cols]).then_inc(chain, 1)
                        dve.wait_ge(chain, n + 3)
                        dve.tensor_tensor(parts[:, 2, cols], rest[:, cols], parts[:, 1, cols], ALU.subtract)\
                           .then_inc(chain, 1)
                        dve.wait_ge(chain, n + 4)
                        dve.sem_inc(spl, 1)

                    @block.vector
                    def _(dve):
                        for m in range(KD):
                            split(dve, slice(0, S), m, NKP * (m + 1))
                        dve.wait_ge(ldv, 32)
                        dve.wait_ge(vones, 3)
                        for j, (k0, kw) in enumerate(key_tiles()):
                            dve.wait_ge(vmm, j + 1)
                            dve.tensor_tensor(Vaug[0:kw, j, :, 0:DH],
                                              bank(6 + j % 2)[0:kw, 0:D].rearrange("p (h d) -> p h d", h=H),
                                              bvb[0:kw, :].rearrange("p (h d) -> p h d", h=H), ALU.add)\
                               .then_inc(vev, 1)
                        got = norm_vector(dve, xn, lnc, lns, lnv)
                        assert got == xn_done, got
                        for m in range(KD):
                            split(dve, slice(0, T), KD + m, 2 * NKP + NC * (m + 1))

        def attention(L, causal, first, Kst, Vaug, OT, live, Qs, tag):
            tiles = key_tiles(first)
            nt = len(tiles)
            masked = not causal

            def seen(i):
                return min(i + 1, nt) if causal else nt

            def max_pieces(s):
                out = []
                for q in range(QTC):
                    i = s * QTC + q
                    for n, (j0, m) in enumerate(groups_of(seen(i), 4)):
                        w = sum(t[1] for t in tiles[j0:j0 + m])
                        diag = (i - j0) * P if causal and j0 <= i < j0 + m else None
                        out.append((q, n, tiles[j0][0], w, diag))
                return out

            def first_column(s, j):
                return max(0, j - s * QTC) * P if causal else 0

            PIECES = [max_pieces(s) for s in range(NC)]
            TILES = [seen(s * QTC + QTC - 1) for s in range(NC)]
            piece0 = [H * sum(len(PIECES[z]) for z in range(s)) for s in range(NC + 1)]
            pack0 = [H // 2 * sum(TILES[:s]) for s in range(NC + 1)]
            NG = H // G
            NI = NG // 2

            with ExitStack() as st:
                QB = 2 if masked else 3
                Qst = sb(st, f"Qst{tag}", [P, QB, H * QC], BF16)
                Pt = sb(st, f"Pt{tag}", [P, SLOTS, 2, QC])
                Vg = sb(st, f"Vg{tag}", [P, 2, nt, G, NV])
                mxp = sb(st, f"mxp{tag}", [P, QTC, H, 4])
                mx = sb(st, f"mx{tag}", [P, QTC, H])
                mrest = sb(st, f"mrest{tag}", [P, QTC, H])
                mparts = sb(st, f"mparts{tag}", [P, QTC, 3, H], BF16)
                mT = sb(st, f"mT{tag}", [3 * H, 2, QC], BF16)
                Kf = Kst[:, :, :].rearrange("p h s -> p (h s)")
                if masked:
                    mrow = sb(st, f"mrow{tag}", [P, QTC, S], BF16)
                    mcol = sb(st, f"mcol{tag}", [P, nt, QC], BF16)
                    mi = sb(st, f"mi{tag}", [P, 2, QC], I32)
                    mask_ld = [sem(f"a{tag}_mask_loaded{i}") for i in range(2)]
                    mask_mk = sem(f"a{tag}_mask_made")
                o_zero, q_ones = sem(f"a{tag}_out_zeroed"), sem(f"a{tag}_q_ones")
                q_ld = [sem(f"a{tag}_q_loaded{s}") for s in range(NC)]
                a_done, a_free = sem(f"a{tag}_max_scores"), sem(f"a{tag}_max_taken")
                m_spl, m_tr, m_sb = (sem(f"a{tag}_max_{n}") for n in ("split", "transposed", "on_sbuf"))
                m_ld = [sem(f"a{tag}_max_stacked{s}") for s in range(NC)]
                vg = sem(f"a{tag}_group_values")
                sc, pr, pv = (sem(f"a{tag}_{n}") for n in ("scores", "probs", "values"))
                o_free = sem(f"a{tag}_out_read")
                chain = sem(f"a{tag}_chain")

                row_cuts = groups_of(S, QC)
                NROW, NCOL = QTC * len(row_cuts), nt

                def mask_made(rows, cols):
                    return NROW * rows + NCOL * cols

                with nc.Block() as block:
                    @block.sync
                    def _(sp):
                        def load_q(s):
                            for b, (qp, _) in enumerate(PAIRS):
                                sp.dma_start(
                                    Qst[b * DH:(b + 1) * DH, s % QB, :].rearrange("p (h t) -> p h t", h=H),
                                    Qs[qp].rearrange("(h d) t -> d h t", d=DH)[:, :, s * QC:(s + 1) * QC])\
                                    .then_inc(q_ld[s], 16)
                        sp.wait_ge(q_ones, 1)
                        for s in range(QB):
                            load_q(s)
                        for s in range(NC):
                            sp.wait_ge(m_sb, s + 1)
                            for n in range(3):
                                sp.dma_start(
                                    Qst[RM + n:RM + n + 1, s % QB, :].rearrange("p (h t) -> p h t", h=H),
                                    mT[n * H:(n + 1) * H, s % 2, :]).then_inc(m_ld[s], 16)
                            if s >= QB - 2 and s + 1 < NC and s + 1 >= QB:
                                sp.wait_ge(pv, pack0[s + 2 - QB])
                                load_q(s + 1)

                    @block.gpsimd
                    def _(pool):
                        pool.memset(Qst[NB:NB + 4, :, :], 1.0).then_inc(q_ones, 1)
                        pool.wait_ge(q_ones, 1)

                        def mask_pieces(pieces, made):
                            def load(i):
                                src, _ = pieces[i]
                                pool.dma_start(mi[0:src.shape[0], i % 2, 0:src.shape[1]], src)\
                                    .then_inc(mask_ld[(made + i) % 2], 16)
                            load(0)
                            load(1)
                            for i, (src, dst) in enumerate(pieces):
                                n = made + i
                                pool.wait_ge(mask_ld[n % 2], 16 * (n // 2 + 1))
                                pool.tensor_scalar(dst, mi[0:src.shape[0], i % 2, 0:src.shape[1]], 0, MASKED,
                                                   ALU.is_equal, ALU.mult).then_inc(mask_mk, 1)
                                pool.wait_ge(mask_mk, n + 1)
                                if i + 2 < len(pieces):
                                    load(i + 2)

                        for stage in range(NC + 1):
                            a, s = stage, stage - 1
                            if masked and a < NC:
                                if a:
                                    pool.wait_ge(a_done, piece0[a])
                                mask_pieces([(mask_d[(a * QTC + q) * P:(a * QTC + q + 1) * P, c0:c0 + cw],
                                              mrow[:, q, c0:c0 + cw]) for q in range(QTC) for c0, cw in row_cuts],
                                            mask_made(a, max(a - 1, 0)))
                            if s < 0:
                                continue
                            if masked:
                                if s:
                                    pool.wait_ge(pv, pack0[s])
                                mask_pieces([(maskT_d[k0:k0 + kw, s * QC:(s + 1) * QC], mcol[0:kw, j, :])
                                             for j, (k0, kw) in enumerate(tiles)], mask_made(min(s + 2, NC), s))
                            with pool.Fori(0, NI) as it:
                                for z in range(2):
                                    before = pack0[s] - 2 * TILES[s - 1] * (1 - z) if s else 0
                                    here = pack0[s] + 2 * TILES[s] * (z + 1)
                                    pool.wait_ge(pv, it * (here - before) + before)
                                    pool.tensor_copy(Vg[:, z, :, :, :],
                                                     Vaug[:, first:NKT, bass.ds(it * (2 * G) + z * G, G), :]).then_inc(vg, 1)

                    @block.tensor
                    def _(pe):
                        def max_piece(s, it, u, n):
                            q, pc, k0, w, diag = PIECES[s][n]
                            np_ = len(PIECES[s])
                            g = piece0[s] + u * np_ + n
                            pe.wait_ge(a_free, it * (2 * G * np_) + (g + 1))
                            h = it * (2 * G) + u
                            out = psA[:, g % 2, 0:w]
                            mmi = pe.matmul(out, Qst[0:KA, s % QB, bass.ds(h * QC + q * P, P)],
                                            Kf[0:KA, bass.ds(h * SP_ + k0, w)], start=True,
                                            stop=diag is None and not masked)
                            if diag is not None:
                                dw = min(P, w - diag)
                                mmi = pe.matmul(psA[:, g % 2, diag:diag + dw], identb[:, :], causb[:, 0:dw],
                                                start=False, stop=True)
                            if masked:
                                mmi = pe.matmul(out, identb[:, :], mrow[:, q, k0:k0 + w], start=False, stop=True)
                            mmi.then_inc(a_done, 1)

                        def score_pack(s, it, z, j, b):
                            k0, kw = tiles[j]
                            col = first_column(s, j)
                            n = pack0[s] + (z * TILES[s] + j) * 2 + b
                            pe.wait_ge(pr, it * (4 * TILES[s]) + (n + 1))
                            for y in range(2):
                                h = it * (2 * G) + (z * G + 2 * b + y)
                                mmi = pe.matmul(psC[0:kw, n % 2, y * 512 + col:y * 512 + QC],
                                                Kf[0:KC, bass.ds(h * SP_ + k0, kw)],
                                                Qst[0:KC, s % QB, bass.ds(h * QC + col, QC - col)],
                                                start=True, stop=not (masked or (causal and j >= s * QTC)))
                                if masked:
                                    mmi = pe.matmul(psC[0:kw, n % 2, y * 512:y * 512 + QC], identb[0:kw, 0:kw],
                                                    mcol[0:kw, j, :], start=False, stop=True)
                                elif j >= s * QTC:
                                    mmi = pe.matmul(psC[0:kw, n % 2, y * 512 + col:y * 512 + col + P],
                                                    identb[0:kw, 0:kw], causbT[0:kw, :], start=False, stop=True)
                            mmi.then_inc(sc, 1)

                        def value_pack(s, it, z, j, b):
                            kw = tiles[j][1]
                            col = first_column(s, j)
                            n = pack0[s] + (z * TILES[s] + j) * 2 + b
                            if j == 0 and b == 0:
                                pe.wait_ge(o_free, it * 2 + (s * NG + z + 1))
                                pe.wait_ge(vg, it * 2 + (s * NG + z + 1))
                            pe.wait_ge(pr, it * (4 * TILES[s]) + (n + 3))
                            for y in range(2):
                                u = 2 * b + y
                                mmi = pe.matmul(psO[32 * u:32 * u + NV, z, col:QC], Vg[0:kw, z, j, u, :],
                                                Pt[0:kw, n % SLOTS, y, col:QC],
                                                start=(j == 0), stop=(j == TILES[s] - 1),
                                                skip_group_check=True)
                            mmi.then_inc(pv, 1)

                        for stage in range(NC + 1):
                            a, c = stage, stage - 1
                            if a < NC:
                                pe.wait_ge(q_ld[a], 16 * len(PAIRS))
                                if masked:
                                    pe.wait_ge(mask_mk, mask_made(a + 1, max(a - 1, 0)))
                                if a:
                                    pe.wait_ge(m_sb, a)
                            if c >= 0:
                                pe.wait_ge(m_ld[c], 48)
                                if c == 0:
                                    pe.wait_ge(o_zero, 1)
                                if masked:
                                    pe.wait_ge(mask_mk, mask_made(min(c + 2, NC), c + 1))
                            with pe.Fori(0, NI) as it:
                                na = 2 * G * len(PIECES[a]) if a < NC else 0
                                steps = []
                                if c >= 0:
                                    order = [(z, j, b) for z in range(2) for j in range(TILES[c]) for b in range(2)]
                                    for i in range(len(order) + LAG):
                                        if i < len(order):
                                            steps.append((score_pack, order[i]))
                                        if i >= LAG:
                                            steps.append((value_pack, order[i - LAG]))
                                done = 0
                                for i, (step, where) in enumerate(steps):
                                    step(c, it, *where)
                                    to = na * (i + 1) // len(steps)
                                    for n in range(done, to):
                                        max_piece(a, it, n // len(PIECES[a]), n % len(PIECES[a]))
                                    done = to
                                for n in range(done, na):
                                    max_piece(a, it, n // len(PIECES[a]), n % len(PIECES[a]))
                            if a < NC:
                                pe.wait_ge(m_spl, a + 1)
                                for q in range(QTC):
                                    mmi = pe.transpose(psA[:, 0, :].bitcast(BF16)[0:3 * H, q * P:(q + 1) * P],
                                                       mparts[:, q, :, :].rearrange("p a h -> p (a h)"), identb[:, :])
                                mmi.then_inc(m_tr, 1)

                    @block.scalar
                    def _(act):
                        act.sem_inc(pr, 2)
                        act.sem_inc(o_free, 2)
                        for stage in range(NC + 1):
                            a, c = stage, stage - 1
                            if c >= 0:
                                def read_out(it, z):
                                    act.wait_ge(pv, it * (4 * TILES[c]) + (pack0[c] + 2 * TILES[c] * (z + 1)))
                                    act.activation(OT[:, bass.ds(it * (2 * T) + (z * T + c * QC), QC)],
                                                   psO[:, z, :], ACT.Copy).then_inc(o_free, 1)
                                with act.Fori(0, NI) as it:
                                    for z in range(2):
                                        for j in range(TILES[c]):
                                            kw = tiles[j][1]
                                            col = first_column(c, j)
                                            for b in range(2):
                                                n = pack0[c] + (z * TILES[c] + j) * 2 + b
                                                act.wait_ge(sc, it * (4 * TILES[c]) + (n + 1))
                                                if n >= SLOTS:
                                                    act.wait_ge(pv, it * (4 * TILES[c]) + (n + 1 - SLOTS))
                                                act.activation(
                                                    Pt[0:kw, n % SLOTS, :, col:QC],
                                                    psC[0:kw, n % 2, :].rearrange("p (y t) -> p y t", y=2)[:, :, col:QC],
                                                    ACT.Exp).then_inc(pr, 1)
                                            if z == 1 and j == 1:
                                                read_out(it, 0)
                                    read_out(it, 1)
                            if a < NC:
                                act.wait_ge(m_tr, a + 1)
                                if a >= 2:
                                    act.wait_ge(m_ld[a - 2], 48)
                                act.activation(mT[:, a % 2, :], psA[:, 0, :].bitcast(BF16)[0:3 * H, 0:QC], ACT.Copy)\
                                   .then_inc(m_sb, 1)

                    @block.vector
                    def _(dve):
                        n = [0]

                        def link(ins):
                            n[0] += 1
                            ins.then_inc(chain, 1)
                            dve.wait_ge(chain, n[0])

                        dve.memset(psO[:, :, :], 0.0).then_inc(o_zero, 1)
                        dve.sem_inc(a_free, 2)
                        mxf = mxp[:, :, :, :].rearrange("p q h n -> p (q h n)")
                        for s in range(NC):
                            np_ = len(PIECES[s])
                            with dve.Fori(0, NI) as it:
                                for u in range(2 * G):
                                    for i, (q, pc, k0, w, diag) in enumerate(PIECES[s]):
                                        g = piece0[s] + u * np_ + i
                                        dve.wait_ge(a_done, it * (2 * G * np_) + (g + 1))
                                        dve.tensor_reduce(mxf[:, bass.ds(it * (2 * G * 4) + ((q * H + u) * 4 + pc), 1)],
                                                          psA[:, g % 2, 0:w], AX.X, ALU.max).then_inc(a_free, 1)
                            dve.wait_ge(a_free, 2 + piece0[s + 1])
                            if s:
                                dve.wait_ge(m_tr, s)
                            for q in range(QTC):
                                npc = 1 + max(x[1] for x in PIECES[s] if x[0] == q)
                                link(dve.tensor_reduce(mx[:, q, :], mxp[:, q, :, 0:npc], AX.X, ALU.max))
                            link(dve.tensor_scalar(mparts[:, :, 0, :], mx[:, :, :], -1.0, None, ALU.mult))
                            link(dve.scalar_tensor_tensor(out=mrest[:, :, :], in0=mx[:, :, :], scalar=-1.0,
                                                          in1=mparts[:, :, 0, :], op0=ALU.mult, op1=ALU.subtract))
                            link(dve.tensor_copy(mparts[:, :, 1, :], mrest[:, :, :]))
                            link(dve.tensor_tensor(mparts[:, :, 2, :], mrest[:, :, :], mparts[:, :, 1, :], ALU.subtract))
                            if masked:
                                link(dve.tensor_scalar(live[:, s * QTC:(s + 1) * QTC, :], mx[:, :, :], DEAD, None, ALU.is_ge))
                            dve.sem_inc(m_spl, 1)

        def output_projection(L, OT, live):
            NG = H // G
            with ExitStack() as st:
                w = W[L]
                att = sb(st, f"att{L}", [P, NQT, D])
                rden = sb(st, f"rden{L}", [P, NC * NG, QTC, G])
                wo = sb(st, f"wo{L}", [P, KD, D])
                bob = sb(st, f"bob{L}", [P, D])
                aT = sb(st, f"aT{L}", [P, 2, KD, QC])
                ld, chain, att_s, bias_s = sem(f"o{L}_loaded"), sem(f"o{L}_chain"), sem(f"o{L}_att"), sem(f"o{L}_bias")
                ot, rd = sem(f"o{L}_out_transposed"), sem(f"o{L}_sum_inverse")
                tr, tre, mm, up = (sem(f"o{L}_{n}") for n in ("transposed", "aT", "done", "residual"))
                with nc.Block() as block:
                    @block.sync
                    def _(sp):
                        sp.dma_start(wo[:, :, :], w["WoT"].rearrange("(k p) n -> p k n", p=P)).then_inc(ld, 16)
                        sp.dma_start(bob[:, :], w["bo"].rearrange("(a n) -> a n", a=1).to_broadcast([P, D]))\
                          .then_inc(ld, 16)

                    @block.gpsimd
                    def _(pool):
                        pool.wait_ge(ld, 32)
                        pool.tensor_scalar(bob[:, :], bob[:, :], gates[:, L:L + 1], 0.0, ALU.mult, ALU.add).then_inc(bias_s, 1)
                        pool.wait_ge(bias_s, 1)
                        for g in range(NC):
                            v = xres[:, g * QTC:(g + 1) * QTC, :]
                            pool.tensor_tensor(v, v, bob[:, :].unsqueeze(1).to_broadcast([P, QTC, D]), ALU.add).then_inc(bias_s, 1)

                    @block.vector
                    def _(dve):
                        def residual(g):
                            for i in (2 * g, 2 * g + 1):
                                dve.wait_ge(mm, i + 1)
                                v = xres[:, 2 * i:2 * i + 2, :].rearrange("p q d -> p (q d)")
                                dve.scalar_tensor_tensor(out=v, in0=bank(4 + i % 4), scalar=gates[:, L:L + 1], in1=v,
                                                         op0=ALU.mult, op1=ALU.add).then_inc(up, 1)
                        nrd = 0
                        for c in range(NC):
                            for g in range(NG):
                                i = c * NG + g
                                dve.wait_ge(ot, i + 1)
                                o = bank(i % 2).rearrange("p (q u n) -> p q u n", q=QTC, u=G)
                                r = rden[:, i, :, :]
                                if live is not None:
                                    lv = live[:, c * QTC:(c + 1) * QTC, g * G:(g + 1) * G]
                                    dve.tensor_tensor(r, o[:, :, :, DH], lv, ALU.mult).then_inc(rd, 1)
                                    nrd += 1
                                    dve.wait_ge(rd, nrd)
                                    dve.reciprocal(r, r).then_inc(rd, 1)
                                    nrd += 1
                                    dve.wait_ge(rd, nrd)
                                    dve.tensor_tensor(r, r, lv, ALU.mult).then_inc(rd, 1)
                                else:
                                    dve.reciprocal(r, o[:, :, :, DH]).then_inc(rd, 1)
                                nrd += 1
                                dve.wait_ge(rd, nrd)
                                for q in range(QTC):
                                    last = dve.tensor_tensor(
                                        att[:, c * QTC + q, g * G * DH:(g + 1) * G * DH].rearrange("p (u d) -> p u d", u=G),
                                        o[:, q, :, 0:DH], r[:, q, :].unsqueeze(2).to_broadcast([P, G, DH]), ALU.mult)
                                last.then_inc(att_s, 1)
                            if c == 1:
                                dve.wait_ge(bias_s, 1 + NC)
                            if c:
                                residual(c - 1)
                        residual(NC - 1)

                    @block.scalar
                    def _(act):
                        for g in range(NC):
                            for k in range(KD):
                                act.wait_ge(tr, 2 * g + k + 1)
                                if g >= 2:
                                    act.wait_ge(mm, 2 * (g - 1))
                                act.activation(aT[:, g % 2, k, :], bank(2 + k)[:, :], ACT.Copy).then_inc(tre, 1)

                    @block.tensor
                    def _(pe):
                        def heads_back(c):
                            for g in range(NG):
                                i = c * NG + g
                                if i >= 2:
                                    pe.wait_ge(att_s, i - 1)
                                for q in range(QTC):
                                    at = g * T + (c * QTC + q) * P
                                    mmi = pe.transpose(bank(i % 2)[:, q * P:(q + 1) * P], OT[:, at:at + P], ident[:, :])
                                mmi.then_inc(ot, 1)

                        heads_back(0)
                        for g in range(NC):
                            if g + 1 < NC:
                                heads_back(g + 1)
                            pe.wait_ge(att_s, NG * (g + 1))
                            for k in range(KD):
                                if g:
                                    pe.wait_ge(tre, 2 * (g - 1) + k + 1)
                                for q in range(QTC):
                                    mmi = pe.transpose(bank(2 + k)[:, q * P:(q + 1) * P],
                                                       att[:, g * QTC + q, k * P:(k + 1) * P], ident[:, :])
                                mmi.then_inc(tr, 1)
                            pe.wait_ge(tre, 2 * (g + 1))
                            if g == 0:
                                pe.wait_ge(ld, 32)
                            for half in range(2):
                                i = 2 * g + half
                                if i >= 4:
                                    pe.wait_ge(up, i - 3)
                                for z in range(2):
                                    q = 2 * half + z
                                    for k in range(KD):
                                        mmi = pe.matmul(bank(4 + i % 4)[:, z * D:(z + 1) * D],
                                                        aT[:, g % 2, k, q * P:(q + 1) * P], wo[:, k, :],
                                                        start=(k == 0), stop=(k == KD - 1))
                                mmi.then_inc(mm, 1)

        def attention_layer(L):
            with ExitStack() as st:
                Kst = sb(st, f"Kst{L}", [P, H, SP_], BF16)
                Vaug = sb(st, f"Vaug{L}", [P, NKT, H, NV])
                Qs = scratch(f"q_parts{L}", [3, D, T], BF16)
                Ks = scratch(f"k_parts{L}", [3, D, S], BF16)
                projections(L, Kst, Vaug, Qs, Ks)
                if stop == f"proj{L}":
                    return False
                OT = sb(st, f"OT{L}", [P, H // G * T])
                live = sb(st, f"live{L}", [P, NQT, H]) if L else None
                attention(L, L == 0, 0, Kst, Vaug, OT, live, Qs, str(L))
                if stop == f"att{L}":
                    return False
                output_projection(L, OT, live)
            return True

        def route(L, E, wr_d, rb_d, xn, xT, gate, slot, xs, places):
            with ExitStack() as st:
                wr = sb(st, f"wr{L}", [P, KD, E])
                rb = sb(st, f"rb{L}", [P, E])
                lg = sb(st, f"lg{L}", [P, NQT, E])
                v8 = sb(st, f"v8{L}", [P, NQT, 8])
                i8 = sb(st, f"i8{L}", [P, NQT, 8], U32)
                idx = sb(st, f"idx{L}", [P, 2, NQT])
                small = sb(st, f"small{L}", [P, 6, NQT])
                ex = sb(st, f"ex{L}", [P, NQT, E])
                iota_i = sb(st, f"iota_i{L}", [P, E, NQT], I32)
                iota_e = sb(st, f"iota_e{L}", [P, E, NQT])
                again = sb(st, f"again{L}", [P, E, NQT])
                hot = sb(st, f"hot{L}", [P, 2, E, NQT])
                both = sb(st, f"both{L}", [P, E, NQT])
                upto = sb(st, f"upto{L}", [P, E, NQT])
                below = sb(st, f"below{L}", [P, E, NQT])
                row = sb(st, f"row{L}", [P, E, NQT])
                pick = sb(st, f"pick{L}", [P, E, NQT])
                srow = sb(st, f"srow{L}", [P, 2, NQT])
                lower = sb(st, f"lower{L}", [P, P])
                ones = sb(st, f"ones{L}", [P, P])
                ld = sem(f"r{L}_loaded")
                lnc, lns, lnv = sem(f"r{L}_ln"), sem(f"r{L}_ln_sqrt"), sem(f"r{L}_ln_var")
                tr, tre, lgt, pos = (sem(f"r{L}_{n}") for n in ("transposed", "xT", "logits", "positions"))
                chain, exps, exin, cst, csts = (sem(f"r{L}_{n}") for n in ("chain", "exp", "exp_in", "const", "const_steps"))
                slots_s, scat, sums_in = sem(f"r{L}_slots"), sem(f"r{L}_scattered"), sem(f"r{L}_counted")
                xn_done = 2 * NQT + 7
                with nc.Block() as block:
                    @block.sync
                    def _(sp):
                        sp.dma_start(wr[:, :, :], wr_d.rearrange("(k p) n -> p k n", p=P)).then_inc(ld, 16)
                        if rb_d is not None:
                            sp.dma_start(rb[:, :], rb_d.rearrange("(a n) -> a n", a=1).to_broadcast([P, E])).then_inc(ld, 16)

                    @block.gpsimd
                    def _(pool):
                        pool.iota(iota_i[:, :, :], [[1, E], [0, NQT]], base=0, channel_multiplier=0).then_inc(cst, 1)
                        pool.memset(again[:, :, :], 1.0).then_inc(csts, 1)
                        pool.memset(lower[:, :], 1.0).then_inc(csts, 1)
                        pool.wait_ge(csts, 2)
                        pool.memset(again[:, :, 0:1], 0.0).then_inc(cst, 1)
                        pool.memset(ones[:, :], 1.0).then_inc(cst, 1)
                        pool.affine_select(out=lower[:, :], in_=lower[:, :], compare_op=ALU.is_ge, fill=0.0,
                                           base=-1, pattern=[[1, P]], channel_multiplier=-1).then_inc(cst, 1)
                        if L == 0:
                            places["consts"](pool, cst)
                        pool.wait_ge(slots_s, 1)
                        pool.wait_ge(zeroed, 32)
                        for t in range(NQT):
                            for k in range(2):
                                pool.indirect_dma_start(
                                    xs[:, :], bass.IndirectOffsetOnAxis(ap=slot[:, k, t:t + 1], axis=0),
                                    xn[:, t, :], None, bounds_check=ROWS - 1, oob_is_err=False).then_inc(scat, 16)
                        pool.wait_ge(scat, 16 * 2 * NQT)

                    @block.scalar
                    def _(act):
                        act.wait_ge(lnv, 1)
                        act.activation(lnw[:, 3, :], lnw[:, 2, :], ACT.Sqrt).then_inc(lns, 1)
                        for i in range(8):
                            act.wait_ge(tr, i + 1)
                            k, g = i % 2, i // 2
                            act.activation(xT[:, k, g * 512:(g + 1) * 512], bank(i % 2)[:, :], ACT.Copy)\
                               .then_inc(tre, 1)
                        act.wait_ge(exin, 1)
                        if L == 0:
                            act.activation(small[:, 1, :], small[:, 0, :], ACT.Exp).then_inc(exps, 1)
                        else:
                            act.activation(ex[:, :, :], ex[:, :, :], ACT.Exp).then_inc(exps, 1)
                            act.activation(small[:, 1, :], small[:, 0, :], ACT.Exp).then_inc(exps, 1)

                    @block.tensor
                    def _(pe):
                        for i in range(8):
                            k, g = i % 2, i // 2
                            if i >= 2:
                                pe.wait_ge(tre, i - 1)
                            pe.wait_ge(lnc, xn_done - NQT + 4 * g + 4)
                            for q in range(4):
                                mmi = pe.transpose(bank(i % 2)[:, q * P:(q + 1) * P],
                                                   xn[:, 4 * g + q, k * P:(k + 1) * P], ident[:, :])
                            mmi.then_inc(tr, 1)
                        pe.wait_ge(ld, 16 if rb_d is None else 32)
                        pe.wait_ge(tre, 8)
                        for t in range(NQT):
                            for k in range(KD):
                                mmi = pe.matmul(bank(2)[:, t * E:(t + 1) * E], xT[:, k, t * P:(t + 1) * P], wr[:, k, :],
                                                start=(k == 0), stop=(k == KD - 1))
                        mmi.then_inc(lgt, 1)
                        pe.wait_ge(sums_in, 1)
                        pe.wait_ge(cst, 4)
                        pe.matmul(bank(3)[:, 0:E * NQT], lower[:, :], both[:, :, :].rearrange("p e t -> p (e t)"),
                                  start=True, stop=False)
                        pe.matmul(bank(3)[:, 0:E * NQT], ones[:, :], below[:, :, :].rearrange("p e t -> p (e t)"),
                                  start=False, stop=True)
                        pe.matmul(bank(4)[:, 0:E], ones[:, :], upto[:, :, NQT - 1], start=True, stop=True)\
                          .then_inc(pos, 1)

                    @block.vector
                    def _(dve):
                        got = norm_vector(dve, xn, lnc, lns, lnv)
                        assert got == xn_done, got
                        n = [0]

                        def link(ins):
                            n[0] += 1
                            ins.then_inc(chain, 1)
                            dve.wait_ge(chain, n[0])

                        dve.wait_ge(lgt, 1)
                        logits = bank(2)[:, 0:NQT * E].rearrange("p (t e) -> p t e", e=E)
                        if rb_d is None:
                            link(dve.tensor_copy(lg[:, :, :], logits))
                        else:
                            dve.wait_ge(ld, 32)
                            link(dve.tensor_tensor(lg[:, :, :], logits, rb[:, :].unsqueeze(1).to_broadcast([P, NQT, E]), ALU.add))
                        for t in range(NQT):
                            dve.max(v8[:, t, :], lg[:, t, :]).then_inc(chain, 1)
                        n[0] += NQT
                        dve.wait_ge(chain, n[0])
                        for t in range(NQT):
                            dve.max_index(i8[:, t, :], v8[:, t, :], lg[:, t, :]).then_inc(chain, 1)
                        n[0] += NQT
                        dve.wait_ge(chain, n[0])
                        d, e2, s1, s2, r, w = (small[:, i, :] for i in range(6))
                        if L:
                            link(dve.tensor_tensor(ex[:, :, :], lg[:, :, :], v8[:, :, 0:1].to_broadcast([P, NQT, E]), ALU.subtract))
                        link(dve.tensor_tensor(d, v8[:, :, 1], v8[:, :, 0], ALU.subtract))
                        dve.sem_inc(exin, 1)
                        for k in range(2):
                            link(dve.tensor_copy(idx[:, k, :], i8[:, :, k]))
                        dve.wait_ge(cst, 2)
                        link(dve.tensor_copy(iota_e[:, :, :], iota_i[:, :, :]))
                        for k in range(2):
                            link(dve.tensor_tensor(hot[:, k, :, :], iota_e[:, :, :],
                                                   idx[:, k, :].unsqueeze(1).to_broadcast([P, E, NQT]), ALU.is_equal))
                        link(dve.tensor_tensor(both[:, :, :], hot[:, 0, :, :], hot[:, 1, :, :], ALU.add))
                        flat = lambda x: x[:, :, :].rearrange("p e t -> p (e t)")
                        link(dve.tensor_tensor_scan(flat(upto), flat(again), flat(both), 0.0, ALU.mult, ALU.add))
                        link(dve.tensor_tensor(below[:, :, :], upto[:, :, :], both[:, :, :], ALU.subtract))
                        dve.sem_inc(sums_in, 1)
                        if L == 0:
                            dve.wait_ge(exps, 1)
                            link(dve.tensor_scalar(s1, e2, 1.0, None, ALU.add))
                            link(dve.reciprocal(gate[:, 0, :], s1))
                            link(dve.tensor_tensor(gate[:, 1, :], gate[:, 0, :], e2, ALU.mult))
                        else:
                            dve.wait_ge(exps, 2)
                            link(dve.tensor_reduce(s1, ex[:, :, :], AX.X, ALU.add))
                            link(dve.reciprocal(s2, s1))
                            link(dve.tensor_tensor(r, s2, e2, ALU.mult))
                            link(dve.tensor_tensor(w, s2, r, ALU.add))
                            link(dve.tensor_scalar(w, w, 1e-9, None, ALU.add))
                            link(dve.reciprocal(w, w))
                            link(dve.tensor_tensor(gate[:, 0, :], s2, w, ALU.mult))
                            link(dve.tensor_tensor(gate[:, 1, :], r, w, ALU.mult))
                        dve.wait_ge(pos, 1)
                        place = bank(3)[:, 0:E * NQT].rearrange("p (e t) -> p e t", e=E)
                        places["rows"](dve, link, place, bank(4)[:, 0:E], row, iota_e, pick, cst)
                        for k in range(2):
                            link(dve.tensor_tensor(pick[:, :, :], row[:, :, :], hot[:, k, :, :], ALU.mult))
                            link(dve.tensor_reduce(srow[:, k, :], pick[:, :, :].rearrange("p e t -> p t e"), AX.X, ALU.add))
                        if L:
                            for k in range(2):
                                link(dve.tensor_scalar(w, srow[:, k, :], float(ROWS), None, ALU.is_lt))
                                link(dve.tensor_tensor(gate[:, k, :], gate[:, k, :], w, ALU.mult))
                        link(dve.tensor_scalar(gate[:, :, :], gate[:, :, :], gates[:, 2 + L:3 + L], None, ALU.mult))
                        link(dve.tensor_copy(slot[:, :, :], srow[:, :, :]))
                        dve.sem_inc(slots_s, 1)

        def experts0(xs, ys, tile_e, ends):
            with ExitStack() as st:
                FH = 2 * F0
                w1 = sb(st, "w1", [P, 2 * KD * FH])
                w2 = sb(st, "w2", [P, 2 * (F0 // P) * D])
                b1 = sb(st, "b1", [P, 2 * FH])
                b2 = sb(st, "b2", [P, 2 * D])
                xt = sb(st, "xt", [P, 2, D])
                xTt = sb(st, "xTt", [P, 2, KD, P])
                av = sb(st, "av", [P, F0])
                bv = sb(st, "bv", [P, F0])
                hv = sb(st, "hv", [P, 2, F0])
                hT = sb(st, "hT", [P, 2, F0])
                yv = sb(st, "yv", [P, 2, D])
                NF = F0 // P
                w_ld = sem("e0_weights")
                x_ld = [sem(f"e0_rows{i}") for i in range(2)]
                y_st = [sem(f"e0_stored{i}") for i in range(2)]
                xtr, xte, u, ue, si, hd, htr, hte, y, ye = (
                    sem(f"e0_{n}") for n in ("x_transposed", "xT", "up", "up_read", "silu", "hidden",
                                             "hidden_transposed", "hT", "down", "down_read"))
                ch = sem("e0_chain")
                NT2 = NT0 // 2
                with nc.Block() as block:
                    @block.gpsimd
                    def _(pool):
                        for e in range(E0):
                            if e >= 2:
                                last = pool.value_load(ends[0:1, e - 2:e - 1], min_val=0, max_val=NT0)
                                pool.wait_ge(w_ld, 64 * e)
                                pool.wait_ge(ye, last)
                            z = e % 2
                            if e == 1:
                                pool.wait_ge(w_ld, 64)
                            pool.dma_start(w1[:, z * KD * FH:(z + 1) * KD * FH].rearrange("p (k n) -> p k n", k=KD),
                                           F["w1"][e].rearrange("(k p) n -> p k n", p=P)).then_inc(w_ld, 16)
                            pool.dma_start(w2[:, z * NF * D:(z + 1) * NF * D].rearrange("p (k n) -> p k n", k=NF),
                                           F["w2"][e].rearrange("(k p) n -> p k n", p=P)).then_inc(w_ld, 16)
                            pool.dma_start(b1[:, z * FH:(z + 1) * FH],
                                           F["b1"][e:e + 1, :].to_broadcast([P, FH])).then_inc(w_ld, 16)
                            pool.dma_start(b2[:, z * D:(z + 1) * D],
                                           F["b2"][e:e + 1, :].to_broadcast([P, D])).then_inc(w_ld, 16)
                        pool.wait_ge(w_ld, 64 * E0)

                    @block.sync
                    def _(sp):
                        with sp.Fori(0, NT2) as it:
                            for z in range(2):
                                sp.wait_ge(xtr, it * 2 + z)
                                sp.dma_start(xt[:, z, :], xs[bass.ds(it * (2 * P) + z * P, P), :]).then_inc(x_ld[z], 16)
                            for z in range(2):
                                sp.wait_ge(ye, it * 2 + (z + 1))
                                sp.dma_start(ys[bass.ds(it * (2 * P) + z * P, P), :], yv[:, z, :]).then_inc(y_st[z], 16)
                        for z in range(2):
                            sp.wait_ge(y_st[z], 16 * NT2)

                    @block.tensor
                    def _(pe):
                        pe.sem_inc(xtr, 2)

                        def turn_x(it, z):
                            pe.wait_ge(x_ld[z], it * 16 + 16)
                            if True:
                                pe.wait_ge(xte, it * 2 + z)
                            for k in range(KD):
                                mmi = pe.transpose(bank(7)[:, k * P:(k + 1) * P], xt[:, z, k * P:(k + 1) * P], ident[:, :])
                            mmi.then_inc(xtr, 1)

                        def up(it, z):
                            e = pe.value_load(tile_e[0:1, 0, bass.ds(it * 2 + z, 1)], min_val=0, max_val=E0 - 1)
                            odd = pe.value_load(tile_e[0:1, 1, bass.ds(it * 2 + z, 1)], min_val=0, max_val=1)
                            pe.wait_ge(w_ld, e * 64 + 64)
                            pe.wait_ge(xte, it * 2 + (z + 1))
                            for n in range(4):
                                pe.wait_ge(ue, it * 8 + (4 * z + n + 1))
                                for k in range(KD):
                                    mmi = pe.matmul(bank(n), xTt[:, z, k, :],
                                                    w1[:, bass.ds(odd * (KD * FH) + (k * FH + n * 512), 512)],
                                                    start=(k == 0), stop=(k == KD - 1))
                                mmi.then_inc(u, 1)
                            return odd

                        def down(it, z, odd):
                            pe.wait_ge(hd, it * 2 + (z + 1))
                            for c in range(2):
                                pe.wait_ge(hte, it * 4 + (2 * z + c))
                                for f in range(4):
                                    mmi = pe.transpose(bank(4 + c)[:, f * P:(f + 1) * P],
                                                       hv[:, z, (4 * c + f) * P:(4 * c + f + 1) * P], ident[:, :])
                                mmi.then_inc(htr, 1)
                            pe.wait_ge(ye, it * 2 + z)
                            for f in range(NF):
                                if f % 4 == 0:
                                    pe.wait_ge(hte, it * 4 + (2 * z + f // 4 + 3))
                                mmi = pe.matmul(bank(6)[:, 0:D], hT[:, z, f * P:(f + 1) * P],
                                                w2[:, bass.ds(odd * (NF * D) + f * D, D)],
                                                start=(f == 0), stop=(f == NF - 1))
                            mmi.then_inc(y, 1)

                        def pair(it):
                            turn_x(it, 0)
                            o0 = up(it, 0)
                            turn_x(it, 1)
                            o1 = up(it, 1)
                            down(it, 0, o0)
                            down(it, 1, o1)

                        with pe.Fori(0, NT2) as it:
                            pair(it)

                    @block.scalar
                    def _(act):
                        act.sem_inc(hte, 2)
                        with act.Fori(0, NT2) as it:
                            def x_out(z):
                                act.wait_ge(xtr, it * 2 + (z + 3))
                                act.activation(xTt[:, z, :, :].rearrange("p k t -> p (k t)"), bank(7)[:, 0:D], ACT.Copy)\
                                   .then_inc(xte, 1)

                            def silu(z):
                                act.wait_ge(ch, it * 6 + (3 * z + 1))
                                act.activation(av[:, :], av[:, :], ACT.Silu).then_inc(si, 1)

                            def h_out(z):
                                for c in range(2):
                                    act.wait_ge(htr, it * 4 + (2 * z + c + 1))
                                    act.activation(hT[:, z, c * 512:(c + 1) * 512], bank(4 + c), ACT.Copy).then_inc(hte, 1)
                            x_out(0)
                            x_out(1)
                            silu(0)
                            silu(1)
                            h_out(0)
                            h_out(1)

                    @block.vector
                    def _(dve):
                        dve.sem_inc(ue, 4)
                        with dve.Fori(0, NT2) as it:
                            odds = []

                            def hidden(z):
                                e = dve.value_load(tile_e[0:1, 0, bass.ds(it * 2 + z, 1)], min_val=0, max_val=E0 - 1)
                                odd = dve.value_load(tile_e[0:1, 1, bass.ds(it * 2 + z, 1)], min_val=0, max_val=1)
                                odds.append(odd)
                                dve.wait_ge(w_ld, e * 64 + 64)
                                dve.wait_ge(hd, it * 2 + z)
                                for n in range(4):
                                    dve.wait_ge(u, it * 8 + (4 * z + n + 1))
                                    dst = av if n < 2 else bv
                                    last = dve.tensor_tensor(dst[:, (n % 2) * 512:(n % 2) * 512 + 512], bank(n),
                                                             b1[:, bass.ds(odd * FH + n * 512, 512)], ALU.add)
                                    last.then_inc(ue, 1)
                                    if n == 1:
                                        dve.wait_ge(ue, it * 8 + (4 * z + n + 5))
                                        dve.sem_inc(ch, 3)
                                dve.wait_ge(ue, it * 8 + (4 * z + 8))
                                dve.wait_ge(si, it * 2 + (z + 1))
                                dve.wait_ge(htr, it * 4 + 2 * z)
                                dve.tensor_tensor(hv[:, z, :], av[:, :], bv[:, :], ALU.mult).then_inc(hd, 1)

                            def outputs(z):
                                dve.wait_ge(y, it * 2 + (z + 1))
                                dve.wait_ge(y_st[z], it * 16)
                                dve.tensor_tensor(yv[:, z, :], bank(6)[:, 0:D], b2[:, bass.ds(odds[z] * D, D)], ALU.add)\
                                   .then_inc(ye, 1)
                            hidden(0)
                            hidden(1)
                            outputs(0)
                            outputs(1)

        def experts1(xs, ys, xn, xT):
            xn_in = sem("s1_normed_added")
            MF = [(m * P, min(P, F1 - m * P)) for m in range(-(-F1 // P))]
            NM = len(MF)
            CT = [(i * P, min(P, CAP - i * P)) for i in range(-(-CAP // P))]
            with ExitStack() as st:
                wg = sb(st, "wg", [P, 3, KD, F1])
                wu = sb(st, "wu", [P, 3, KD, F1])
                wd = sb(st, "wd", [P, 3, NM, D])
                xe = sb(st, "xe", [P, 2, len(CT), D])
                xTe = sb(st, "xTe", [P, 2, KD, CAP])
                sil = sb(st, "sil", [P, 2, 512])
                hT1 = sb(st, "hT1", [P, 2, NM, 512])
                ye1 = sb(st, "ye1", [P, 2, len(CT), D])
                w_ld = [sem(f"e1_weights{i}") for i in range(3)]
                x_ld = [sem(f"e1_rows{i}") for i in range(2)]
                y_st = [sem(f"e1_stored{i}") for i in range(2)]
                xtr, xte, gu, si, h, y, ye = (sem(f"e1_{n}") for n in ("x_transposed", "xT", "gate_up", "silu", "hidden", "down", "down_read"))
                s_gu, s_si, s_h, s_y, s_ye = (sem(f"s1_{n}") for n in ("gate_up", "silu", "hidden", "down", "down_read"))
                NI1 = E1 // 2

                def load_weights(q, z, g, u_, d, s_):
                    q.dma_start(wg[:, z, :, :], g.rearrange("(k p) n -> p k n", p=P)).then_inc(s_, 16)
                    q.dma_start(wu[:, z, :, :], u_.rearrange("(k p) n -> p k n", p=P)).then_inc(s_, 16)
                    full = F1 // P * P
                    q.dma_start(wd[:, z, 0:F1 // P, :], d[0:full, :].rearrange("(m p) n -> p m n", p=P)).then_inc(s_, 16)
                    q.dma_start(wd[0:F1 - full, z, F1 // P, :], d[full:F1, :]).then_inc(s_, 16)

                with nc.Block() as block:
                    @block.sync
                    def _(sp):
                        load_weights(sp, 2, F["sw_gate"], F["sw_up"], F["sw_down"], w_ld[2])
                        full = CAP // P * P
                        with sp.Fori(0, NI1) as it:
                            for z in range(2):
                                sp.wait_ge(xtr, it * 2 + z)
                                r = it * (2 * CAP) + z * CAP
                                sp.dma_start(xe[:, z, 0:CAP // P, :],
                                             xs[bass.ds(r, full), :].rearrange("(m p) n -> p m n", p=P)).then_inc(x_ld[z], 16)
                                sp.dma_start(xe[0:CAP - full, z, CAP // P, :],
                                             xs[bass.ds(r + full, CAP - full), :]).then_inc(x_ld[z], 16)
                            for z in range(2):
                                sp.wait_ge(ye, it * 2 + (z + 1))
                                r = it * (2 * CAP) + z * CAP
                                sp.dma_start(ys[bass.ds(r, full), :].rearrange("(m p) n -> p m n", p=P),
                                             ye1[:, z, 0:CAP // P, :]).then_inc(y_st[z], 16)
                                sp.dma_start(ys[bass.ds(r + full, CAP - full), :],
                                             ye1[0:CAP - full, z, CAP // P, :]).then_inc(y_st[z], 16)
                        for z in range(2):
                            sp.wait_ge(y_st[z], 32 * NI1)

                    @block.gpsimd
                    def _(pool):
                        for e in range(E1):
                            if e >= 2:
                                pool.wait_ge(y, e - 1)
                            load_weights(pool, e % 2, F["w_gate"][e], F["w_up"][e], F["w_down"][e], w_ld[e % 2])

                    @block.tensor
                    def _(pe):
                        pe.wait_ge(w_ld[2], 64)
                        for c in range(NC):
                            for m, (f0, fw) in enumerate(MF):
                                n = c * NM + m
                                if n >= 2:
                                    pe.wait_ge(s_h, n - 1)
                                for i, w in enumerate((wg, wu)):
                                    for k in range(KD):
                                        mmi = pe.matmul(bank(2 * (n % 2) + i)[0:fw, :], w[:, 2, k, f0:f0 + fw],
                                                        xT[:, k, c * QC:(c + 1) * QC], start=(k == 0), stop=(k == KD - 1))
                                mmi.then_inc(s_gu, 1)
                            pe.wait_ge(s_h, (c + 1) * NM)
                            for q in range(QTC):
                                j = c * QTC + q
                                if j >= 2:
                                    pe.wait_ge(s_ye, j - 1)
                                for m, (f0, fw) in enumerate(MF):
                                    mmi = pe.matmul(bank(4 + j % 2)[:, 0:D], hT1[0:fw, c % 2, m, q * P:(q + 1) * P],
                                                    wd[0:fw, 2, m, :], start=(m == 0), stop=(m == NM - 1))
                                mmi.then_inc(s_y, 1)
                        pe.wait_ge(s_ye, NQT)
                        pe.sem_inc(xtr, 2)
                        with pe.Fori(0, NI1) as it:
                            for z in range(2):
                                pe.wait_ge(x_ld[z], it * 32 + 32)
                                pe.wait_ge(xte, it * 4 + 2 * z)
                                for k in range(KD):
                                    for i, (c0, cw) in enumerate(CT):
                                        mmi = pe.transpose(bank(6 + k)[:, c0:c0 + cw], xe[0:cw, z, i, k * P:(k + 1) * P],
                                                           ident[0:cw, 0:cw])
                                mmi.then_inc(xtr, 1)
                                pe.wait_ge(w_ld[z], it * 64 + 64)
                                pe.wait_ge(xte, it * 4 + (2 * z + 2))
                                for m, (f0, fw) in enumerate(MF):
                                    pe.wait_ge(h, it * 6 + (NM * z + m + 1))
                                    b = (NM * z + m) % 2
                                    for i, w in enumerate((wg, wu)):
                                        for k in range(KD):
                                            mmi = pe.matmul(bank(2 * b + i)[0:fw, 0:CAP], w[:, z, k, f0:f0 + fw],
                                                            xTe[:, z, k, :], start=(k == 0), stop=(k == KD - 1))
                                    mmi.then_inc(gu, 1)
                                pe.wait_ge(h, it * 6 + (NM * z + NM + 2))
                                pe.wait_ge(ye, it * 2 + z)
                                for i, (c0, cw) in enumerate(CT):
                                    for m, (f0, fw) in enumerate(MF):
                                        mmi = pe.matmul(bank(4 + i // 2)[0:cw, (i % 2) * D:(i % 2 + 1) * D],
                                                        hT1[0:fw, z, m, c0:c0 + cw], wd[0:fw, z, m, :],
                                                        start=(m == 0), stop=(m == NM - 1))
                                mmi.then_inc(y, 1)

                    @block.scalar
                    def _(act):
                        for n in range(NC * NM):
                            fw = MF[n % NM][1]
                            act.wait_ge(s_gu, n + 1)
                            if n >= 2:
                                act.wait_ge(s_h, n - 1)
                            act.activation(sil[0:fw, n % 2, :], bank(2 * (n % 2))[0:fw, :], ACT.Silu).then_inc(s_si, 1)
                        act.wait_ge(s_h, NC * NM)
                        with act.Fori(0, NI1) as it:
                            for z in range(2):
                                act.wait_ge(xtr, it * 2 + (z + 3))
                                act.wait_ge(y, it * 2 + z)
                                for k in range(KD):
                                    act.activation(xTe[:, z, k, :], bank(6 + k)[:, 0:CAP], ACT.Copy).then_inc(xte, 1)
                                for m, (f0, fw) in enumerate(MF):
                                    b = (NM * z + m) % 2
                                    act.wait_ge(gu, it * 6 + (NM * z + m + 1))
                                    act.wait_ge(h, it * 6 + (NM * z + m + 1))
                                    act.activation(sil[0:fw, b, 0:CAP], bank(2 * b)[0:fw, 0:CAP], ACT.Silu).then_inc(si, 1)
                                act.wait_ge(y, it * 2 + (z + 1))
                                act.wait_ge(y_st[z], it * 32)
                                act.activation(ye1[:, z, 0:2, :].rearrange("p a d -> p (a d)"), bank(4), ACT.Copy)
                                act.activation(ye1[0:CT[2][1], z, 2, :], bank(5)[0:CT[2][1], 0:D], ACT.Copy).then_inc(ye, 1)

                    @block.vector
                    def _(dve):
                        for j in range(NQT):
                            dve.scalar_tensor_tensor(out=xres[:, j, :], in0=xn[:, j, :], scalar=gates[:, 3:4],
                                                     in1=xres[:, j, :], op0=ALU.mult, op1=ALU.add).then_inc(xn_in, 1)

                        def shared_out(c):
                            for q in range(QTC):
                                j = c * QTC + q
                                dve.wait_ge(s_y, j + 1)
                                dve.wait_ge(xn_in, j + 1)
                                dve.scalar_tensor_tensor(out=xres[:, j, :], in0=bank(4 + j % 2)[:, 0:D], scalar=gates[:, 3:4],
                                                         in1=xres[:, j, :], op0=ALU.mult, op1=ALU.add).then_inc(s_ye, 1)
                        for c in range(NC):
                            for m, (f0, fw) in enumerate(MF):
                                n = c * NM + m
                                dve.wait_ge(s_si, n + 1)
                                dve.tensor_tensor(hT1[0:fw, c % 2, m, :], sil[0:fw, n % 2, :],
                                                  bank(2 * (n % 2) + 1)[0:fw, :], ALU.mult).then_inc(s_h, 1)
                            shared_out(c)
                        dve.sem_inc(h, 2)
                        with dve.Fori(0, NI1) as it:
                            for z in range(2):
                                dve.wait_ge(y, it * 2 + z)
                                for m, (f0, fw) in enumerate(MF):
                                    b = (NM * z + m) % 2
                                    dve.wait_ge(si, it * 6 + (NM * z + m + 1))
                                    dve.tensor_tensor(hT1[0:fw, z, m, 0:CAP], sil[0:fw, b, 0:CAP],
                                                      bank(2 * b + 1)[0:fw, 0:CAP], ALU.mult).then_inc(h, 1)

        def combine(L, ys, gate, slot):
            with ExitStack() as st:
                NR = 8
                yg = sb(st, f"yg{L}", [P, NR, D])
                zs = sem(f"c{L}_zeroed")
                got = [sem(f"c{L}_gathered{i}") for i in range(NR)]
                used = sem(f"c{L}_used")
                with nc.Block() as block:
                    @block.gpsimd
                    def _(pool):
                        pool.memset(yg[:, :, :], 0.0).then_inc(zs, 1)
                        pool.wait_ge(zs, 1)
                        for n in range(2 * NQT):
                            t, k = n // 2, n % 2
                            if n >= NR:
                                pool.wait_ge(used, n - NR + 1)
                            pool.indirect_dma_start(
                                yg[:, n % NR, :], None, ys[:, :],
                                bass.IndirectOffsetOnAxis(ap=slot[:, k, t:t + 1], axis=0),
                                bounds_check=ROWS - 1, oob_is_err=False).then_inc(got[n % NR], 16)

                    @block.vector
                    def _(dve):
                        for n in range(2 * NQT):
                            t, k = n // 2, n % 2
                            dve.wait_ge(got[n % NR], 16 * (n // NR + 1))
                            if k:
                                dve.wait_ge(used, n)
                            dve.scalar_tensor_tensor(out=xres[:, t, :], in0=yg[:, n % NR, :], scalar=gate[:, k, t:t + 1],
                                                     in1=xres[:, t, :], op0=ALU.mult, op1=ALU.add).then_inc(used, 1)

        def ffn_layer(L):
            with ExitStack() as st:
                E = (E0, E1)[L]
                gate = sb(st, f"gate{L}", [P, 2, NQT])
                slot = sb(st, f"slot{L}", [P, 2, NQT], U32)
                xn = sb(st, f"fxn{L}", [P, NQT, D])
                xT = sb(st, f"fxT{L}", [P, KD, T])
                places = {}
                if L == 0:
                    tile_e = sb(st, "tile_e", [P, 2, NT0], I32)
                    ends = sb(st, "ends", [P, E0], I32)
                    tile_f = sb(st, "tile_f", [P, 2, NT0])
                    cnt = sb(st, "cnt", [P, 4, E0])
                    thr_i = sb(st, "thr_i", [P, E0, NQT], I32)
                    thr = sb(st, "thr", [P, E0, NQT])
                    tno_i = sb(st, "tno_i", [P, NT0, E0 - 1], I32)
                    tno = sb(st, "tno", [P, NT0, E0 - 1])
                    sign = sb(st, "sign", [P, E0])
                    one8 = sb(st, "one8", [P, E0])

                    def consts(pool, cst):
                        pool.iota(thr_i[:, :, :], [[0, E0], [P, NQT]], base=0, channel_multiplier=0).then_inc(cst, 1)
                        pool.iota(tno_i[:, :, :], [[1, NT0], [0, E0 - 1]], base=0, channel_multiplier=0).then_inc(cst, 1)
                        pool.memset(one8[:, :], 1.0).then_inc(cst, 1)
                        pool.memset(sign[:, :].rearrange("p (a b) -> p a b", b=2)[:, :, 0], 1.0).then_inc(cst, 1)
                        pool.memset(sign[:, :].rearrange("p (a b) -> p a b", b=2)[:, :, 1], -1.0).then_inc(cst, 1)

                    def rows(dve, link, place, counts, row, iota_e, pick, cst):
                        dve.wait_ge(cst, 9)
                        link(dve.tensor_copy(thr[:, :, :], thr_i[:, :, :]))
                        link(dve.tensor_copy(tno[:, :, :], tno_i[:, :, :]))
                        n, nt, end, start = (cnt[:, i, :] for i in range(4))
                        link(dve.tensor_copy(n, counts))
                        link(dve.tensor_tensor(pick[:, :, :], thr[:, :, :], n.unsqueeze(2).to_broadcast([P, E0, NQT]), ALU.is_lt))
                        link(dve.tensor_reduce(nt, pick[:, :, :], AX.X, ALU.add))
                        link(dve.tensor_tensor_scan(end, one8[:, :], nt, 0.0, ALU.mult, ALU.add))
                        link(dve.tensor_tensor(start, end, nt, ALU.subtract))
                        link(dve.tensor_scalar(start, start, float(P), None, ALU.mult))
                        link(dve.tensor_tensor(row[:, :, :], place, start.unsqueeze(2).to_broadcast([P, E0, NQT]), ALU.add))
                        link(dve.tensor_copy(ends[:, :], end))
                        link(dve.tensor_tensor(tno[:, :, :], tno[:, :, :],
                                               end[:, 0:E0 - 1].unsqueeze(1).to_broadcast([P, NT0, E0 - 1]), ALU.is_ge))
                        link(dve.tensor_reduce(tile_f[:, 0, :], tno[:, :, :], AX.X, ALU.add))
                        link(dve.tensor_tensor(tno[:, :, :], tno[:, :, :],
                                               sign[:, 0:E0 - 1].unsqueeze(1).to_broadcast([P, NT0, E0 - 1]), ALU.mult))
                        link(dve.tensor_reduce(tile_f[:, 1, :], tno[:, :, :], AX.X, ALU.add))
                        link(dve.tensor_copy(tile_e[:, :, :], tile_f[:, :, :]))
                    places["consts"], places["rows"] = consts, rows
                    route(0, E, F["wrT"], None, xn, xT, gate, slot, xs0, places)
                    experts0(xs0, ys0, tile_e, ends)
                    combine(0, ys0, gate, slot)
                else:
                    def rows1(dve, link, place, counts, row, iota_e, pick, cst):
                        link(dve.tensor_scalar(pick[:, :, :], place, float(CAP), float(FAR), ALU.is_ge, ALU.mult))
                        link(dve.scalar_tensor_tensor(out=row[:, :, :], in0=iota_e[:, :, :], scalar=float(CAP), in1=pick[:, :, :],
                                                      op0=ALU.mult, op1=ALU.add))
                        link(dve.tensor_tensor(row[:, :, :], row[:, :, :], place, ALU.add))
                    places["rows"] = rows1
                    route(1, E, F["router_w"], F["router_b"], xn, xT, gate, slot, xs1, places)
                    experts1(xs1, ys1, xn, xT)
                    combine(1, ys1, gate, slot)

        def store_out():
            done = sem("out_stored")
            with nc.Block() as block:
                @block.sync
                def _(sp):
                    sp.dma_start(out_d.rearrange("(t p) d -> p t d", p=P), xres[:, :, :]).then_inc(done, 16)
                    sp.wait_ge(done, 16)

        xs0, xs1 = scratch("rows0", [ROWS, D], F32), scratch("rows1", [ROWS, D], F32)
        ys0, ys1 = scratch("outs0", [ROWS, D], F32), scratch("outs1", [ROWS, D], F32)
        zero = sb(ctx, "zero", [P, D])
        zeroed, zms = ctx.enter_context(nc.semaphore("rows_zeroed")), sem("zero_made")
        with nc.Block() as block:
            @block.gpsimd
            def _(pool):
                pool.memset(zero[:, :], 0.0).then_inc(zms, 1)

            @block.sync
            def _(sp):
                sp.wait_ge(zms, 1)
                for r in (xs0, xs1):
                    sp.dma_start(r.rearrange("(t p) d -> p t d", p=P),
                                 zero[:, :].unsqueeze(1).to_broadcast([P, ROWS // P, D])).then_inc(zeroed, 16)
                sp.wait_ge(zeroed, 32)

        stages = (("x1", attention_layer, 0), ("x2", ffn_layer, 0), ("x3", attention_layer, 1), ("x4", ffn_layer, 1))
        for name, layer, L in stages:
            layer(L)
            free_semaphores()
            if stop == name:
                break
        store_out()


STOP = None
_NAMES = ["Wq", "bq", "Wk", "bk", "Wv", "bv", "Wo", "bo"]


def kernel(**inputs):
    import concourse.bacc as _bacc
    from concourse.bass_utils import run_bass_kernel_spmd as _run

    nc = _bacc.Bacc("TRN2", target_bir_lowering=False, num_devices=1)
    arrays = {}

    def give(name, a):
        a = np.ascontiguousarray(a)
        arrays[name] = a
        return nc.dram_tensor(name, a.shape, mybir.dt.from_np(a.dtype), kind="ExternalInput").ap()

    x = give("x", inputs["x"].reshape(T, D))
    ctxT = give("ctxT", inputs["ctx_1024"].reshape(S, D).T)
    mask = give("mask", inputs["mask_SxS2_ik0"])
    maskT = give("maskT", inputs["mask_SxS2_ik0"].T)
    gx, gf = give("g_xattn", inputs["g_xattn"]), give("g_ffn", inputs["g_ffn"])
    W = []
    for L in range(2):
        w = {}
        for n in _NAMES:
            a = inputs[f"L{L}_xattn_{n}"]
            if n[0] == "W":
                w[n + "T"] = give(f"L{L}_{n}T", a.T)
            else:
                w[n] = give(f"L{L}_{n}", a)
        W.append(w)
    out = nc.dram_tensor("out", (T, D), F32, kind="ExternalOutput").ap()
    F = {n: give(f"L0_{n}", inputs[f"L0_ffn_{n}"]) for n in ("w1", "b1", "w2", "b2")}
    F["wrT"] = give("L0_wrT", inputs["L0_ffn_wr"].T)
    for n in ("router_w", "router_b", "w_gate", "w_up", "w_down", "sw_gate", "sw_up", "sw_down"):
        F[n] = give(f"L1_{n}", inputs[f"L1_ffn_{n}"])
    build(nc, x, ctxT, mask, maskT, gx, gf, W, F, out, STOP)
    r = _run(nc, [arrays], core_ids=[0])
    return r.results[0]["out"].reshape(1, T, D)
```

```python
from contextlib import ExitStack, contextmanager

import numpy as np

import concourse.bass as bass
from concourse import mybir

F32 = mybir.dt.float32
BF16 = mybir.dt.bfloat16
I32 = mybir.dt.int32
U32 = mybir.dt.uint32
ALU = mybir.AluOpType
ACT = mybir.ActivationFunctionType
AX = mybir.AxisListType

P = 128
T = 2048
D = 256
KD = D // P
S = 1601
NQT = T // P
H = 16
DH = D // H
NKT = -(-S // P)
QC = 512
NC = T // QC
QTC = QC // P
SP_ = S + 1
TAIL = 9
EPS = 1e-5
MASKED = -1e30
DEAD = -1e29
PAIRS = ((0, 0), (0, 1), (1, 0), (0, 2), (1, 1), (2, 0))
NB = len(PAIRS) * DH
RB = NB
RM = NB + 1
KA = NB + 1
KC = NB + 4
G = 4
NV = DH + 1
SLOTS = 4
LAG = 2

E0, F0 = 8, 1024
E1, F1 = 16, 352
CAP = -(-5 * 2 * T // (4 * E1))
ROWS = E1 * CAP
NT0 = ROWS // P
FAR = 1 << 20
assert NT0 >= 2 * T // P + E0 - 1


def key_tiles(first=0):
    return [(j * P, min(P, S - j * P)) for j in range(first, NKT)]


def groups_of(n, most):
    k = -(-n // most)
    out, at = [], 0
    for i in range(k):
        m = n // k + (i < n % k)
        out.append((at, m))
        at += m
    return out


def build(nc, x_d, ctxT_d, mask_d, maskT_d, gx_d, gf_d, W, F, out_d, stop=None):
    ctx = ExitStack()

    def sb(stack, name, shape, dt=F32):
        return stack.enter_context(nc.sbuf_tensor(name, shape, dt))

    layer_sems = []

    def sem(name):
        layer_sems.append(nc.alloc_semaphore(name=name))
        return layer_sems[-1]

    def free_semaphores():
        nc.clear_and_free_semaphores(layer_sems)
        nc.all_engine_barrier()
        layer_sems.clear()

    def scratch(name, shape, dt):
        return nc.dram_tensor(name, shape, dt, kind="Internal").ap()

    with ctx:
        psA = ctx.enter_context(nc.psum_tensor("psA", [P, 2, 512], F32))
        psC = ctx.enter_context(nc.psum_tensor("psC", [P, 2, 1024], F32))
        psO = ctx.enter_context(nc.psum_tensor("psO", [P, 2, 512], F32))

        def bank(i):
            if i < 2:
                return psA[:, i, :]
            if i < 6:
                return psC[:, (i - 2) // 2, (i % 2) * 512:(i % 2) * 512 + 512]
            return psO[:, i - 6, :]

        xres = sb(ctx, "xres", [P, NQT, D])
        ident = sb(ctx, "ident", [P, P])
        identb = sb(ctx, "identb", [P, P], BF16)
        causb = sb(ctx, "causb", [P, P], BF16)
        gates = sb(ctx, "gates", [P, 4])
        causbT = sb(ctx, "causbT", [P, P], BF16)
        ignored = sb(ctx, "ignored", [P, S], BF16)
        stats = sb(ctx, "stats", [P, NQT, 6])
        lnw = sb(ctx, "lnw", [P, 6, NQT])

        c_ld, c_ms, c_id, c_tanh = sem("const_loaded"), sem("const_memset"), sem("const_made"), sem("tanh_done")
        with nc.Block() as block:
            @block.sync
            def _(sp):
                sp.dma_start(xres[:, :, :], x_d.rearrange("(t p) d -> p t d", p=P)).then_inc(c_ld, 16)
                sp.dma_start(gates[:, 0:2], gx_d.rearrange("(a n) -> a n", a=1).to_broadcast([P, 2])).then_inc(c_ld, 16)
                sp.dma_start(gates[:, 2:4], gf_d.rearrange("(a n) -> a n", a=1).to_broadcast([P, 2])).then_inc(c_ld, 16)
                sp.wait_ge(c_ld, 48)

            @block.scalar
            def _(act):
                act.wait_ge(c_ld, 48)
                act.activation(gates[:, :], gates[:, :], ACT.Tanh).then_inc(c_tanh, 1)

            @block.gpsimd
            def _(pool):
                pool.memset(ident[:, :], 0.0).then_inc(c_ms, 1)
                pool.memset(identb[:, :], 0.0).then_inc(c_ms, 1)
                pool.memset(causb[:, :], 0.0).then_inc(c_ms, 1)
                pool.memset(causbT[:, :], 0.0).then_inc(c_ms, 1)
                pool.wait_ge(c_ms, 4)
                pool.affine_select(out=causbT[:, :], in_=causbT[:, :], compare_op=ALU.is_ge, fill=MASKED,
                                   base=0, pattern=[[1, P]], channel_multiplier=-1).then_inc(c_id, 1)
                for m in (ident, identb):
                    pool.affine_select(out=m[:, :], in_=m[:, :], compare_op=ALU.not_equal, fill=1.0,
                                       base=0, pattern=[[-1, P]], channel_multiplier=1).then_inc(c_id, 1)
                pool.affine_select(out=causb[:, :], in_=causb[:, :], compare_op=ALU.is_ge, fill=MASKED,
                                   base=0, pattern=[[-1, P]], channel_multiplier=1).then_inc(c_id, 1)

        def norm_vector(dve, xn, chain, tag_sqrt, tag_var):
            n = [0]

            def link(ins):
                n[0] += 1
                ins.then_inc(chain, 1)
                dve.wait_ge(chain, n[0])

            with dve.Fori(0, NQT) as t:
                dve.bn_stats(stats[:, bass.ds(t, 1), :].rearrange("p a b -> p (a b)"),
                             xres[:, bass.ds(t, 1), :].rearrange("p a b -> p (a b)")).then_inc(chain, 1)
            n[0] = NQT
            dve.wait_ge(chain, NQT)
            me, ve, mo, vo = (stats[:, :, i] for i in (1, 2, 4, 5))
            mean, diff, var, std, rstd, tmp = (lnw[:, i, :] for i in range(6))
            link(dve.tensor_tensor(mean, me, mo, ALU.add))
            link(dve.tensor_scalar(mean, mean, 0.5, None, ALU.mult))
            link(dve.tensor_tensor(diff, me, mo, ALU.subtract))
            link(dve.tensor_tensor(diff, diff, diff, ALU.mult))
            link(dve.tensor_tensor(var, ve, vo, ALU.add))
            link(dve.tensor_scalar(var, var, 1.0 / D, EPS, ALU.mult, ALU.add))
            dve.scalar_tensor_tensor(out=var, in0=diff, scalar=0.25, in1=var, op0=ALU.mult, op1=ALU.add)\
               .then_inc(tag_var, 1)
            dve.wait_ge(tag_sqrt, 1)
            link(dve.reciprocal(rstd, std))
            with dve.Fori(0, NQT) as t:
                dve.tensor_scalar(xn[:, bass.ds(t, 1), :].rearrange("p a b -> p (a b)"),
                                  xres[:, bass.ds(t, 1), :].rearrange("p a b -> p (a b)"),
                                  lnw[:, 0, bass.ds(t, 1)], lnw[:, 4, bass.ds(t, 1)],
                                  ALU.subtract, ALU.mult).then_inc(chain, 1)
            return n[0] + NQT

        def projections(L, Kst, Vaug, Qs, Ks):
            with ExitStack() as st:
                w = W[L]
                xn = sb(st, f"xn{L}", [P, NQT, D])
                xT = sb(st, f"xT{L}", [P, KD, T])
                cT = sb(st, f"cT{L}", [P, KD, S])
                wq, wk, wv = (sb(st, f"w{n}{L}", [P, KD, D]) for n in "qkv")
                bqk = sb(st, f"bqk{L}", [P, 2, KD])
                bvb = sb(st, f"bvb{L}", [P, D])
                kf = sb(st, f"kf{L}", [P, T])
                rest = sb(st, f"rest{L}", [P, T])
                parts = sb(st, f"parts{L}", [P, 3, T], BF16)
                ld, ldv, ldx = sem(f"p{L}_k_loaded"), sem(f"p{L}_v_loaded"), sem(f"p{L}_q_loaded")
                vones = sem(f"p{L}_v_ones")
                mm, ev = sem(f"p{L}_kq_done"), sem(f"p{L}_kq_evacuated")
                vmm, vev = sem(f"p{L}_v_done"), sem(f"p{L}_v_evacuated")
                spl, sto = sem(f"p{L}_split"), sem(f"p{L}_stored")
                lnc, lns, lnv = sem(f"p{L}_ln"), sem(f"p{L}_ln_sqrt"), sem(f"p{L}_ln_var")
                bq4, tr, tre = sem(f"p{L}_bq_scaled"), sem(f"p{L}_transposed"), sem(f"p{L}_xT")
                chain = sem(f"p{L}_chain")
                kload = sem(f"p{L}_kstack")
                kcols = [(a, n) for a, n in groups_of(S, 512)]
                NKP = len(kcols)
                xn_done = 2 * NQT + 7

                with nc.Block() as block:
                    @block.sync
                    def _(sp):
                        for dst, src in ((cT[:, :, :], ctxT_d.rearrange("(k p) s -> p k s", p=P)),
                                         (wk[:, :, :], w["WkT"].rearrange("(k p) n -> p k n", p=P)),
                                         (bqk[:, 1, :], w["bk"].rearrange("(m p) -> p m", p=P))):
                            with nc.allow_non_contiguous_dma(reason="bias columns"):
                                sp.dma_start(dst, src).then_inc(ld, 16)
                        sp.dma_start(wv[:, :, :], w["WvT"].rearrange("(k p) n -> p k n", p=P)).then_inc(ldv, 16)
                        sp.dma_start(bvb[:, :], w["bv"].rearrange("(a n) -> a n", a=1).to_broadcast([P, D]))\
                          .then_inc(ldv, 16)
                        sp.dma_start(wq[:, :, :], w["WqT"].rearrange("(k p) n -> p k n", p=P)).then_inc(ldx, 16)
                        with nc.allow_non_contiguous_dma(reason="bias columns"):
                            sp.dma_start(bqk[:, 0, :], w["bq"].rearrange("(m p) -> p m", p=P)).then_inc(ldx, 16)
                        for m in range(KD):
                            sp.wait_ge(spl, m + 1)
                            sp.dma_start(Ks[:, m * P:(m + 1) * P, :].rearrange("t p s -> p t s"),
                                         parts[:, :, 0:S]).then_inc(sto, 16)
                        sp.wait_ge(sto, 32)
                        for b, (_, kp) in enumerate(PAIRS):
                            sp.dma_start(Kst[b * DH:(b + 1) * DH, :, 0:S],
                                         Ks[kp].rearrange("(h d) s -> d h s", d=DH)).then_inc(kload, 16)
                        for m in range(KD):
                            sp.wait_ge(spl, KD + m + 1)
                            sp.dma_start(Qs[:, m * P:(m + 1) * P, :].rearrange("t p s -> p t s"),
                                         parts[:, :, :]).then_inc(sto, 16)
                        sp.wait_ge(sto, 64)
                        sp.wait_ge(kload, 16 * len(PAIRS))

                    @block.gpsimd
                    def _(pool):
                        pool.memset(Vaug[:, :, :, :], 1.0).then_inc(vones, 1)
                        pool.wait_ge(vones, 1)
                        pool.memset(Kst[NB:NB + 4, :, :], 1.0).then_inc(vones, 1)
                        pool.wait_ge(vones, 2)
                        pool.memset(Kst[RB:RB + 1, :, :], 0.0).then_inc(vones, 1)

                    @block.scalar
                    def _(act):
                        act.wait_ge(ld, 48)
                        n = 0
                        for m in range(KD):
                            if m:
                                act.wait_ge(chain, 4 * m)
                            for a, c in kcols:
                                act.wait_ge(mm, n + 1)
                                act.activation(kf[:, a:a + c], bank(n % 4)[:, 0:c], ACT.Identity,
                                               bias=bqk[:, 1, m:m + 1]).then_inc(ev, 1)
                                n += 1
                        act.wait_ge(lnv, 1)
                        act.activation(lnw[:, 3, :], lnw[:, 2, :], ACT.Sqrt).then_inc(lns, 1)
                        act.wait_ge(ldx, 32)
                        act.activation(bqk[:, 0, :], bqk[:, 0, :], ACT.Copy, scale=0.25).then_inc(bq4, 1)
                        for i in range(8):
                            act.wait_ge(tr, i + 1)
                            k, g = i % 2, i // 2
                            act.activation(xT[:, k, g * 512:(g + 1) * 512], bank(i % 2)[:, :], ACT.Copy)\
                               .then_inc(tre, 1)
                        act.wait_ge(bq4, 1)
                        for m in range(KD):
                            act.wait_ge(chain, 4 * (KD + m))
                            for c in range(NC):
                                act.wait_ge(mm, n + 1)
                                act.activation(kf[:, c * QC:(c + 1) * QC], bank(n % 4)[:, :], ACT.Identity,
                                               bias=bqk[:, 0, m:m + 1], scale=0.25).then_inc(ev, 1)
                                n += 1

                    @block.tensor
                    def _(pe):
                        pe.wait_ge(ld, 48)
                        n = 0
                        for m in range(KD):
                            for a, c in kcols:
                                if n >= 4:
                                    pe.wait_ge(ev, n - 3)
                                for k in range(KD):
                                    mmi = pe.matmul(bank(n % 4)[:, 0:c], wk[:, k, m * P:(m + 1) * P],
                                                    cT[:, k, a:a + c], start=(k == 0), stop=(k == KD - 1))
                                mmi.then_inc(mm, 1)
                                n += 1
                        pe.wait_ge(ldv, 32)
                        for j, (k0, kw) in enumerate(key_tiles()):
                            if j >= 2:
                                pe.wait_ge(vev, j - 1)
                            for k in range(KD):
                                mmi = pe.matmul(bank(6 + j % 2)[0:kw, 0:D], cT[:, k, k0:k0 + kw], wv[:, k, :],
                                                start=(k == 0), stop=(k == KD - 1))
                            mmi.then_inc(vmm, 1)
                        pe.wait_ge(lns, 1)
                        pe.wait_ge(ev, 2 * NKP)
                        for i in range(8):
                            k, g = i % 2, i // 2
                            if i >= 2:
                                pe.wait_ge(tre, i - 1)
                            pe.wait_ge(lnc, xn_done - NQT + 4 * g + 4)
                            for q in range(4):
                                mmi = pe.transpose(bank(i % 2)[:, q * P:(q + 1) * P],
                                                   xn[:, 4 * g + q, k * P:(k + 1) * P], ident[:, :])
                            mmi.then_inc(tr, 1)
                        pe.wait_ge(tre, 8)
                        pe.wait_ge(ldx, 32)
                        for m in range(KD):
                            for c in range(NC):
                                if n >= 4:
                                    pe.wait_ge(ev, n - 3)
                                for k in range(KD):
                                    mmi = pe.matmul(bank(n % 4)[:, :], wq[:, k, m * P:(m + 1) * P],
                                                    xT[:, k, c * QC:(c + 1) * QC], start=(k == 0), stop=(k == KD - 1))
                                mmi.then_inc(mm, 1)
                                n += 1

                    def split(dve, cols, i, n_ev):
                        dve.wait_ge(ev, n_ev)
                        if i:
                            dve.wait_ge(sto, 16 * i)
                        n = 4 * i
                        dve.tensor_copy(parts[:, 0, cols], kf[:, cols]).then_inc(chain, 1)
                        dve.wait_ge(chain, n + 1)
                        dve.tensor_tensor(rest[:, cols], kf[:, cols], parts[:, 0, cols], ALU.subtract).then_inc(chain, 1)
                        dve.wait_ge(chain, n + 2)
                        dve.tensor_copy(parts[:, 1, cols], rest[:, cols]).then_inc(chain, 1)
                        dve.wait_ge(chain, n + 3)
                        dve.tensor_tensor(parts[:, 2, cols], rest[:, cols], parts[:, 1, cols], ALU.subtract)\
                           .then_inc(chain, 1)
                        dve.wait_ge(chain, n + 4)
                        dve.sem_inc(spl, 1)

                    @block.vector
                    def _(dve):
                        for m in range(KD):
                            split(dve, slice(0, S), m, NKP * (m + 1))
                        dve.wait_ge(ldv, 32)
                        dve.wait_ge(vones, 3)
                        for j, (k0, kw) in enumerate(key_tiles()):
                            dve.wait_ge(vmm, j + 1)
                            dve.tensor_tensor(Vaug[0:kw, j, :, 0:DH],
                                              bank(6 + j % 2)[0:kw, 0:D].rearrange("p (h d) -> p h d", h=H),
                                              bvb[0:kw, :].rearrange("p (h d) -> p h d", h=H), ALU.add)\
                               .then_inc(vev, 1)
                        got = norm_vector(dve, xn, lnc, lns, lnv)
                        assert got == xn_done, got
                        for m in range(KD):
                            split(dve, slice(0, T), KD + m, 2 * NKP + NC * (m + 1))

        def attention(st, causal, masked, first, Kst, Vaug, OT, live, Qs, tag):
            tiles = key_tiles(first)
            nt = len(tiles)

            def seen(i):
                return min(i + 1, nt) if causal else nt

            def max_pieces(s):
                out = []
                for q in range(QTC):
                    i = s * QTC + q
                    for n, (j0, m) in enumerate(groups_of(seen(i), 4)):
                        w = sum(t[1] for t in tiles[j0:j0 + m])
                        diag = (i - j0) * P if causal and j0 <= i < j0 + m else None
                        out.append((q, n, tiles[j0][0], w, diag))
                return out

            def first_column(s, j):
                return max(0, j - s * QTC) * P if causal else 0

            PIECES = [max_pieces(s) for s in range(NC)]
            TILES = [seen(s * QTC + QTC - 1) for s in range(NC)]
            piece0 = [H * sum(len(PIECES[z]) for z in range(s)) for s in range(NC + 1)]
            pack0 = [H // 2 * sum(TILES[:s]) for s in range(NC + 1)]
            NG = H // G
            NI = NG // 2

            QB = 2 if masked else 3
            Qst = sb(st, f"Qst{tag}", [P, QB, H * QC], BF16)
            Pt = sb(st, f"Pt{tag}", [P, SLOTS, 2, QC])
            Vg = sb(st, f"Vg{tag}", [P, 2, nt, G, NV])
            mxp = sb(st, f"mxp{tag}", [P, QTC, H, 4])
            mx = sb(st, f"mx{tag}", [P, QTC, H])
            mrest = sb(st, f"mrest{tag}", [P, QTC, H])
            mparts = sb(st, f"mparts{tag}", [P, QTC, 3, H], BF16)
            mT = sb(st, f"mT{tag}", [3 * H, 2, QC], BF16)
            Kf = Kst[:, :, :].rearrange("p h s -> p (h s)")
            if masked:
                mrow = sb(st, f"mrow{tag}", [P, QTC, S], BF16)
                mcol = sb(st, f"mcol{tag}", [P, nt, QC], BF16)
                mi = sb(st, f"mi{tag}", [P, 2, QC], I32)
                mask_ld = [sem(f"a{tag}_mask_loaded{i}") for i in range(2)]
                mask_mk = sem(f"a{tag}_mask_made")
            o_zero, q_ones = sem(f"a{tag}_out_zeroed"), sem(f"a{tag}_q_ones")
            q_ld = [sem(f"a{tag}_q_loaded{s}") for s in range(NC)]
            a_done, a_free = sem(f"a{tag}_max_scores"), sem(f"a{tag}_max_taken")
            m_spl, m_tr, m_sb = (sem(f"a{tag}_max_{n}") for n in ("split", "transposed", "on_sbuf"))
            m_ld = [sem(f"a{tag}_max_stacked{s}") for s in range(NC)]
            vg = sem(f"a{tag}_group_values")
            sc, pr, pv = (sem(f"a{tag}_{n}") for n in ("scores", "probs", "values"))
            o_free = sem(f"a{tag}_out_read")
            chain = sem(f"a{tag}_chain")

            row_cuts = groups_of(S, QC)
            NROW, NCOL = QTC * len(row_cuts), nt

            def mask_made(rows, cols):
                return NROW * rows + NCOL * cols

            def sync(sp):
                def load_q(s):
                    for b, (qp, _) in enumerate(PAIRS):
                        sp.dma_start(
                            Qst[b * DH:(b + 1) * DH, s % QB, :].rearrange("p (h t) -> p h t", h=H),
                            Qs[qp].rearrange("(h d) t -> d h t", d=DH)[:, :, s * QC:(s + 1) * QC])\
                            .then_inc(q_ld[s], 16)
                sp.wait_ge(q_ones, 1)
                for s in range(QB):
                    load_q(s)
                for s in range(NC):
                    sp.wait_ge(m_sb, s + 1)
                    for n in range(3):
                        sp.dma_start(
                            Qst[RM + n:RM + n + 1, s % QB, :].rearrange("p (h t) -> p h t", h=H),
                            mT[n * H:(n + 1) * H, s % 2, :]).then_inc(m_ld[s], 16)
                    if s >= QB - 2 and s + 1 < NC and s + 1 >= QB:
                        sp.wait_ge(pv, 1 + pack0[s + 2 - QB])
                        load_q(s + 1)

            def gpsimd(pool):
                pool.memset(Qst[NB:NB + 4, :, :], 1.0).then_inc(q_ones, 1)
                pool.wait_ge(q_ones, 1)

                def mask_pieces(pieces, made):
                    def load(i):
                        src, _ = pieces[i]
                        pool.dma_start(mi[0:src.shape[0], i % 2, 0:src.shape[1]], src)\
                            .then_inc(mask_ld[(made + i) % 2], 16)
                    load(0)
                    load(1)
                    for i, (src, dst) in enumerate(pieces):
                        n = made + i
                        pool.wait_ge(mask_ld[n % 2], 16 * (n // 2 + 1))
                        pool.tensor_scalar(dst, mi[0:src.shape[0], i % 2, 0:src.shape[1]], 0, MASKED,
                                           ALU.is_equal, ALU.mult).then_inc(mask_mk, 1)
                        pool.wait_ge(mask_mk, n + 1)
                        if i + 2 < len(pieces):
                            load(i + 2)

                for stage in range(NC + 1):
                    a, s = stage, stage - 1
                    if masked and a < NC:
                        if a:
                            pool.wait_ge(a_done, piece0[a])
                        mask_pieces([(mask_d[(a * QTC + q) * P:(a * QTC + q + 1) * P, c0:c0 + cw],
                                      mrow[:, q, c0:c0 + cw]) for q in range(QTC) for c0, cw in row_cuts],
                                    mask_made(a, max(a - 1, 0)))
                    if s < 0:
                        continue
                    if masked:
                        if s:
                            pool.wait_ge(pv, 1 + pack0[s])
                        mask_pieces([(maskT_d[k0:k0 + kw, s * QC:(s + 1) * QC], mcol[0:kw, j, :])
                                     for j, (k0, kw) in enumerate(tiles)], mask_made(min(s + 2, NC), s))
                    with pool.Fori(0, NI) as it:
                        for z in range(2):
                            before = pack0[s] - 2 * TILES[s - 1] * (1 - z) if s else 0
                            here = pack0[s] + 2 * TILES[s] * (z + 1)
                            pool.wait_ge(pv, it * (here - before) + (before + 1))
                            pool.tensor_copy(Vg[:, z, :, :, :],
                                             Vaug[:, first:NKT, bass.ds(it * (2 * G) + z * G, G), :]).then_inc(vg, 1)

            def tensor(pe):
                pe.sem_inc(pv, 1)
                def max_piece(s, it, u, n):
                    q, pc, k0, w, diag = PIECES[s][n]
                    np_ = len(PIECES[s])
                    g = piece0[s] + u * np_ + n
                    pe.wait_ge(a_free, it * (2 * G * np_) + (g + 1))
                    h = it * (2 * G) + u
                    out = psA[:, g % 2, 0:w]
                    mmi = pe.matmul(out, Qst[0:KA, s % QB, bass.ds(h * QC + q * P, P)],
                                    Kf[0:KA, bass.ds(h * SP_ + k0, w)], start=True,
                                    stop=diag is None and not masked)
                    if diag is not None:
                        dw = min(P, w - diag)
                        mmi = pe.matmul(psA[:, g % 2, diag:diag + dw], identb[:, :], causb[:, 0:dw],
                                        start=False, stop=True)
                    if masked:
                        mmi = pe.matmul(out, identb[:, :], mrow[:, q, k0:k0 + w], start=False, stop=True)
                    mmi.then_inc(a_done, 1)

                def score_pack(s, it, z, j, b):
                    k0, kw = tiles[j]
                    col = first_column(s, j)
                    n = pack0[s] + (z * TILES[s] + j) * 2 + b
                    pe.wait_ge(pr, it * (4 * TILES[s]) + (n + 1))
                    for y in range(2):
                        h = it * (2 * G) + (z * G + 2 * b + y)
                        mmi = pe.matmul(psC[0:kw, n % 2, y * 512 + col:y * 512 + QC],
                                        Kf[0:KC, bass.ds(h * SP_ + k0, kw)],
                                        Qst[0:KC, s % QB, bass.ds(h * QC + col, QC - col)],
                                        start=True, stop=not (masked or (causal and j >= s * QTC)))
                        if masked:
                            mmi = pe.matmul(psC[0:kw, n % 2, y * 512:y * 512 + QC], identb[0:kw, 0:kw],
                                            mcol[0:kw, j, :], start=False, stop=True)
                        elif causal and j >= s * QTC:
                            mmi = pe.matmul(psC[0:kw, n % 2, y * 512 + col:y * 512 + col + P],
                                            identb[0:kw, 0:kw], causbT[0:kw, :], start=False, stop=True)
                    mmi.then_inc(sc, 1)

                def value_pack(s, it, z, j, b):
                    kw = tiles[j][1]
                    col = first_column(s, j)
                    n = pack0[s] + (z * TILES[s] + j) * 2 + b
                    if j == 0 and b == 0:
                        pe.wait_ge(o_free, it * 2 + (s * NG + z + 1))
                        pe.wait_ge(vg, it * 2 + (s * NG + z + 1))
                    pe.wait_ge(pr, it * (4 * TILES[s]) + (n + 3))
                    for y in range(2):
                        u = 2 * b + y
                        mmi = pe.matmul(psO[32 * u:32 * u + NV, z, col:QC], Vg[0:kw, z, j, u, :],
                                        Pt[0:kw, n % SLOTS, y, col:QC],
                                        start=(j == 0), stop=(j == TILES[s] - 1),
                                        skip_group_check=True)
                    mmi.then_inc(pv, 1)

                for stage in range(NC + 1):
                    a, c = stage, stage - 1
                    if a < NC:
                        pe.wait_ge(q_ld[a], 16 * len(PAIRS))
                        if masked:
                            pe.wait_ge(mask_mk, mask_made(a + 1, max(a - 1, 0)))
                        if a:
                            pe.wait_ge(m_sb, a)
                    if c >= 0:
                        pe.wait_ge(m_ld[c], 48)
                        if c == 0:
                            pe.wait_ge(o_zero, 1)
                        if masked:
                            pe.wait_ge(mask_mk, mask_made(min(c + 2, NC), c + 1))
                    with pe.Fori(0, NI) as it:
                        na = 2 * G * len(PIECES[a]) if a < NC else 0
                        steps = []
                        if c >= 0:
                            order = [(z, j, b) for z in range(2) for j in range(TILES[c]) for b in range(2)]
                            for i in range(len(order) + LAG):
                                if i < len(order):
                                    steps.append((score_pack, order[i]))
                                if i >= LAG:
                                    steps.append((value_pack, order[i - LAG]))
                        done = 0
                        for i, (step, where) in enumerate(steps):
                            step(c, it, *where)
                            to = na * (i + 1) // len(steps)
                            for n in range(done, to):
                                max_piece(a, it, n // len(PIECES[a]), n % len(PIECES[a]))
                            done = to
                        for n in range(done, na):
                            max_piece(a, it, n // len(PIECES[a]), n % len(PIECES[a]))
                    if a < NC:
                        pe.wait_ge(m_spl, a + 1)
                        for q in range(QTC):
                            mmi = pe.transpose(psA[:, 0, :].bitcast(BF16)[0:3 * H, q * P:(q + 1) * P],
                                               mparts[:, q, :, :].rearrange("p a h -> p (a h)"), identb[:, :])
                        mmi.then_inc(m_tr, 1)

            def scalar(act):
                act.sem_inc(pr, 2)
                act.sem_inc(o_free, 2)
                for stage in range(NC + 1):
                    a, c = stage, stage - 1
                    if c >= 0:
                        def read_out(it, z):
                            act.wait_ge(pv, it * (4 * TILES[c]) + (pack0[c] + 2 * TILES[c] * (z + 1) + 1))
                            act.activation(OT[:, bass.ds(it * (2 * T) + (z * T + c * QC), QC)],
                                           psO[:, z, :], ACT.Copy).then_inc(o_free, 1)
                        with act.Fori(0, NI) as it:
                            for z in range(2):
                                for j in range(TILES[c]):
                                    kw = tiles[j][1]
                                    col = first_column(c, j)
                                    for b in range(2):
                                        n = pack0[c] + (z * TILES[c] + j) * 2 + b
                                        act.wait_ge(sc, it * (4 * TILES[c]) + (n + 1))
                                        if n >= SLOTS:
                                            act.wait_ge(pv, it * (4 * TILES[c]) + (n + 2 - SLOTS))
                                        act.activation(
                                            Pt[0:kw, n % SLOTS, :, col:QC],
                                            psC[0:kw, n % 2, :].rearrange("p (y t) -> p y t", y=2)[:, :, col:QC],
                                            ACT.Exp).then_inc(pr, 1)
                                    if z == 1 and j == 1:
                                        read_out(it, 0)
                            read_out(it, 1)
                    if a < NC:
                        act.wait_ge(m_tr, a + 1)
                        if a >= 2:
                            act.wait_ge(m_ld[a - 2], 48)
                        act.activation(mT[:, a % 2, :], psA[:, 0, :].bitcast(BF16)[0:3 * H, 0:QC], ACT.Copy)\
                           .then_inc(m_sb, 1)

            def vector(dve):
                n = [0]

                def link(ins):
                    n[0] += 1
                    ins.then_inc(chain, 1)
                    dve.wait_ge(chain, n[0])

                dve.memset(psO[:, :, :], 0.0).then_inc(o_zero, 1)
                dve.sem_inc(a_free, 2)
                mxf = mxp[:, :, :, :].rearrange("p q h n -> p (q h n)")
                for s in range(NC):
                    np_ = len(PIECES[s])
                    with dve.Fori(0, NI) as it:
                        for u in range(2 * G):
                            for i, (q, pc, k0, w, diag) in enumerate(PIECES[s]):
                                g = piece0[s] + u * np_ + i
                                dve.wait_ge(a_done, it * (2 * G * np_) + (g + 1))
                                dve.tensor_reduce(mxf[:, bass.ds(it * (2 * G * 4) + ((q * H + u) * 4 + pc), 1)],
                                                  psA[:, g % 2, 0:w], AX.X, ALU.max).then_inc(a_free, 1)
                    dve.wait_ge(a_free, 2 + piece0[s + 1])
                    if s:
                        dve.wait_ge(m_tr, s)
                    for q in range(QTC):
                        npc = 1 + max(x[1] for x in PIECES[s] if x[0] == q)
                        link(dve.tensor_reduce(mx[:, q, :], mxp[:, q, :, 0:npc], AX.X, ALU.max))
                    link(dve.tensor_scalar(mparts[:, :, 0, :], mx[:, :, :], -1.0, None, ALU.mult))
                    link(dve.scalar_tensor_tensor(out=mrest[:, :, :], in0=mx[:, :, :], scalar=-1.0,
                                                  in1=mparts[:, :, 0, :], op0=ALU.mult, op1=ALU.subtract))
                    link(dve.tensor_copy(mparts[:, :, 1, :], mrest[:, :, :]))
                    link(dve.tensor_tensor(mparts[:, :, 2, :], mrest[:, :, :], mparts[:, :, 1, :], ALU.subtract))
                    if live is not None:
                        link(dve.tensor_scalar(live[:, s * QTC:(s + 1) * QTC, :], mx[:, :, :], DEAD, None, ALU.is_ge))
                    dve.sem_inc(m_spl, 1)

            return sync, gpsimd, tensor, scalar, vector

        def output_projection(L, OT, live):
            NG = H // G
            with ExitStack() as st:
                w = W[L]
                att = sb(st, f"att{L}", [P, NQT, D])
                rden = sb(st, f"rden{L}", [P, NC * NG, QTC, G])
                wo = sb(st, f"wo{L}", [P, KD, D])
                bob = sb(st, f"bob{L}", [P, D])
                aT = sb(st, f"aT{L}", [P, 2, KD, QC])
                ld, chain, att_s, bias_s = sem(f"o{L}_loaded"), sem(f"o{L}_chain"), sem(f"o{L}_att"), sem(f"o{L}_bias")
                ot, rd = sem(f"o{L}_out_transposed"), sem(f"o{L}_sum_inverse")
                tr, tre, mm, up = (sem(f"o{L}_{n}") for n in ("transposed", "aT", "done", "residual"))
                with nc.Block() as block:
                    @block.sync
                    def _(sp):
                        sp.dma_start(wo[:, :, :], w["WoT"].rearrange("(k p) n -> p k n", p=P)).then_inc(ld, 16)
                        sp.dma_start(bob[:, :], w["bo"].rearrange("(a n) -> a n", a=1).to_broadcast([P, D]))\
                          .then_inc(ld, 16)

                    @block.gpsimd
                    def _(pool):
                        pool.wait_ge(ld, 32)
                        pool.tensor_scalar(bob[:, :], bob[:, :], gates[:, L:L + 1], 0.0, ALU.mult, ALU.add).then_inc(bias_s, 1)
                        pool.wait_ge(bias_s, 1)
                        for g in range(NC):
                            v = xres[:, g * QTC:(g + 1) * QTC, :]
                            pool.tensor_tensor(v, v, bob[:, :].unsqueeze(1).to_broadcast([P, QTC, D]), ALU.add).then_inc(bias_s, 1)

                    @block.vector
                    def _(dve):
                        def residual(g):
                            for i in (2 * g, 2 * g + 1):
                                dve.wait_ge(mm, i + 1)
                                v = xres[:, 2 * i:2 * i + 2, :].rearrange("p q d -> p (q d)")
                                dve.scalar_tensor_tensor(out=v, in0=bank(4 + i % 4), scalar=gates[:, L:L + 1], in1=v,
                                                         op0=ALU.mult, op1=ALU.add).then_inc(up, 1)
                        nrd = 0
                        for c in range(NC):
                            for g in range(NG):
                                i = c * NG + g
                                dve.wait_ge(ot, i + 1)
                                o = bank(i % 2).rearrange("p (q u n) -> p q u n", q=QTC, u=G)
                                r = rden[:, i, :, :]
                                if live is not None:
                                    lv = live[:, c * QTC:(c + 1) * QTC, g * G:(g + 1) * G]
                                    dve.tensor_tensor(r, o[:, :, :, DH], lv, ALU.mult).then_inc(rd, 1)
                                    nrd += 1
                                    dve.wait_ge(rd, nrd)
                                    dve.reciprocal(r, r).then_inc(rd, 1)
                                    nrd += 1
                                    dve.wait_ge(rd, nrd)
                                    dve.tensor_tensor(r, r, lv, ALU.mult).then_inc(rd, 1)
                                else:
                                    dve.reciprocal(r, o[:, :, :, DH]).then_inc(rd, 1)
                                nrd += 1
                                dve.wait_ge(rd, nrd)
                                for q in range(QTC):
                                    last = dve.tensor_tensor(
                                        att[:, c * QTC + q, g * G * DH:(g + 1) * G * DH].rearrange("p (u d) -> p u d", u=G),
                                        o[:, q, :, 0:DH], r[:, q, :].unsqueeze(2).to_broadcast([P, G, DH]), ALU.mult)
                                last.then_inc(att_s, 1)
                            if c == 1:
                                dve.wait_ge(bias_s, 1 + NC)
                            if c:
                                residual(c - 1)
                        residual(NC - 1)

                    @block.scalar
                    def _(act):
                        for g in range(NC):
                            for k in range(KD):
                                act.wait_ge(tr, 2 * g + k + 1)
                                if g >= 2:
                                    act.wait_ge(mm, 2 * (g - 1))
                                act.activation(aT[:, g % 2, k, :], bank(2 + k)[:, :], ACT.Copy).then_inc(tre, 1)

                    @block.tensor
                    def _(pe):
                        def heads_back(c):
                            for g in range(NG):
                                i = c * NG + g
                                if i >= 2:
                                    pe.wait_ge(att_s, i - 1)
                                for q in range(QTC):
                                    at = g * T + (c * QTC + q) * P
                                    mmi = pe.transpose(bank(i % 2)[:, q * P:(q + 1) * P], OT[:, at:at + P], ident[:, :])
                                mmi.then_inc(ot, 1)

                        heads_back(0)
                        for g in range(NC):
                            if g + 1 < NC:
                                heads_back(g + 1)
                            pe.wait_ge(att_s, NG * (g + 1))
                            for k in range(KD):
                                if g:
                                    pe.wait_ge(tre, 2 * (g - 1) + k + 1)
                                for q in range(QTC):
                                    mmi = pe.transpose(bank(2 + k)[:, q * P:(q + 1) * P],
                                                       att[:, g * QTC + q, k * P:(k + 1) * P], ident[:, :])
                                mmi.then_inc(tr, 1)
                            pe.wait_ge(tre, 2 * (g + 1))
                            if g == 0:
                                pe.wait_ge(ld, 32)
                            for half in range(2):
                                i = 2 * g + half
                                if i >= 4:
                                    pe.wait_ge(up, i - 3)
                                for z in range(2):
                                    q = 2 * half + z
                                    for k in range(KD):
                                        mmi = pe.matmul(bank(4 + i % 4)[:, z * D:(z + 1) * D],
                                                        aT[:, g % 2, k, q * P:(q + 1) * P], wo[:, k, :],
                                                        start=(k == 0), stop=(k == KD - 1))
                                mmi.then_inc(mm, 1)

        def summarise_mask(Kst, tail_only):
            k0 = TAIL * P
            cuts = [(c, min(512, k0 - c)) for c in range(0, k0, 512)] + [(k0, S - k0)]
            tail = len(cuts) - 1
            assert tail < 6 and S - k0 <= 512
            with ExitStack() as st:
                onesb = sb(st, "onesb", [P, P], BF16)
                some = sb(st, "some", [P, tail + 1])
                part = sb(st, "part", [P, 2, S - k0])
                bias = sb(st, "bias", [P, S - k0], BF16)
                made, summed, chain = sem("m_ones"), sem("m_summed"), sem("m_chain")
                with nc.Block() as block:
                    @block.gpsimd
                    def _(pool):
                        pool.memset(onesb[:, :], 1.0).then_inc(made, 1)

                    @block.tensor
                    def _(pe):
                        pe.wait_ge(made, 1)
                        for i, (c0, cw) in enumerate(cuts):
                            pe.matmul(bank(i)[:, 0:cw], onesb[:, :], ignored[:, c0:c0 + cw], start=True, stop=True)\
                              .then_inc(summed, 1)

                    @block.vector
                    def _(dve):
                        n = [0]

                        def link(ins):
                            n[0] += 1
                            ins.then_inc(chain, 1)
                            dve.wait_ge(chain, n[0])

                        dve.wait_ge(summed, tail + 1)
                        for i, (c0, cw) in enumerate(cuts[:tail]):
                            link(dve.tensor_reduce(some[:, i:i + 1], bank(i)[:, 0:cw], AX.X, ALU.min))
                        link(dve.tensor_scalar(some[:, 0:tail], some[:, 0:tail], -1.0, float(T), ALU.mult, ALU.add))
                        last = bank(tail)[:, 0:S - k0]
                        link(dve.tensor_scalar(part[:, 0, :], last, -1.0, float(T), ALU.mult, ALU.add))
                        link(dve.tensor_tensor(part[:, 1, :], part[:, 0, :], last, ALU.mult))
                        link(dve.tensor_reduce(some[:, tail:tail + 1], part[:, 1, :], AX.X, ALU.max))
                        link(dve.tensor_reduce(part[:, 0, 0:1], some[:, :], AX.X, ALU.max))
                        link(dve.tensor_scalar(tail_only[:, :], part[:, 0, 0:1], 0.0, None, ALU.is_equal))
                        link(dve.tensor_scalar(bias[:, :], last, float(T), MASKED, ALU.is_equal, ALU.mult))
                        link(dve.tensor_copy(Kst[RB:RB + 1, :, k0:S],
                                             bias[RB:RB + 1, :].unsqueeze(1).to_broadcast([1, H, S - k0])))

        def attention_layer(L):
            with ExitStack() as st:
                Kst = sb(st, f"Kst{L}", [P, H, SP_], BF16)
                Vaug = sb(st, f"Vaug{L}", [P, NKT, H, NV])
                Qs = scratch(f"q_parts{L}", [3, D, T], BF16)
                Ks = scratch(f"k_parts{L}", [3, D, S], BF16)
                projections(L, Kst, Vaug, Qs, Ks)
                if stop == f"proj{L}":
                    return False
                OT = sb(st, f"OT{L}", [P, H // G * T])
                live = sb(st, f"live{L}", [P, NQT, H]) if L else None
                if L == 0:
                    with ExitStack() as at:
                        sync, gpsimd, tensor, scalar, vector = attention(at, True, False, 0, Kst, Vaug, OT, None, Qs, "0")
                        with nc.Block() as block:
                            block.sync(sync)
                            block.gpsimd(gpsimd)
                            block.tensor(tensor)
                            block.scalar(scalar)
                            block.vector(vector)
                else:
                    tail_only = sb(st, "tail_only", [P, 1], I32)
                    summarise_mask(Kst, tail_only)
                    with ExitStack() as at:
                        tail = attention(at, False, False, TAIL, Kst, Vaug, OT, live, Qs, "t")
                    with ExitStack() as at:
                        every = attention(at, False, True, 0, Kst, Vaug, OT, live, Qs, "g")

                        def either(i):
                            def program(eng):
                                flag = eng.value_load(tail_only[0:1, 0:1], min_val=0, max_val=1)
                                with eng.If(flag > 0):
                                    tail[i](eng)
                                with eng.Else():
                                    every[i](eng)
                            return program
                        with nc.Block() as block:
                            block.sync(either(0))
                            block.gpsimd(either(1))
                            block.tensor(either(2))
                            block.scalar(either(3))
                            block.vector(either(4))
                if stop == f"att{L}":
                    return False
                output_projection(L, OT, live)
            return True

        def load_expert(queue, e, w1, w2, w_ld):
            z = e % 2
            queue.dma_start(w1[:, z, :, :], F["w1"][e].rearrange("(k p) n -> p k n", p=P)).then_inc(w_ld, 16)
            nf = F0 // P
            queue.dma_start(w2[:, z * nf * D:(z + 1) * nf * D].rearrange("p (k n) -> p k n", k=nf),
                            F["w2"][e].rearrange("(k p) n -> p k n", p=P)).then_inc(w_ld, 16)

        def route(L, E, wr_d, rb_d, xn, xT, gate, slot, xs, places):
            with ExitStack() as st:
                wr = sb(st, f"wr{L}", [P, KD, E])
                rb = sb(st, f"rb{L}", [P, E])
                lg = sb(st, f"lg{L}", [P, NQT, E])
                v8 = sb(st, f"v8{L}", [P, NQT, 8])
                i8 = sb(st, f"i8{L}", [P, NQT, 8], U32)
                idx = sb(st, f"idx{L}", [P, 2, NQT])
                small = sb(st, f"small{L}", [P, 6, NQT])
                ex = sb(st, f"ex{L}", [P, NQT, E])
                iota_i = sb(st, f"iota_i{L}", [P, E, NQT], I32)
                iota_e = sb(st, f"iota_e{L}", [P, E, NQT])
                again = sb(st, f"again{L}", [P, E, NQT])
                hot = sb(st, f"hot{L}", [P, 2, E, NQT])
                both = sb(st, f"both{L}", [P, E, NQT])
                upto = sb(st, f"upto{L}", [P, E, NQT])
                below = sb(st, f"below{L}", [P, E, NQT])
                row = sb(st, f"row{L}", [P, E, NQT])
                pick = sb(st, f"pick{L}", [P, E, NQT])
                srow = sb(st, f"srow{L}", [P, 2, NQT])
                lower = sb(st, f"lower{L}", [P, P])
                ones = sb(st, f"ones{L}", [P, P])
                ld = sem(f"r{L}_loaded")
                lnc, lns, lnv = sem(f"r{L}_ln"), sem(f"r{L}_ln_sqrt"), sem(f"r{L}_ln_var")
                tr, tre, lgt, pos = (sem(f"r{L}_{n}") for n in ("transposed", "xT", "logits", "positions"))
                chain, exps, exin, cst, csts = (sem(f"r{L}_{n}") for n in ("chain", "exp", "exp_in", "const", "const_steps"))
                slots_s, scat, sums_in = sem(f"r{L}_slots"), sem(f"r{L}_scattered"), sem(f"r{L}_counted")

                def scatter(pool):
                    for t in range(NQT):
                        for k in range(2):
                            pool.indirect_dma_start(
                                xs[:, :], bass.IndirectOffsetOnAxis(ap=slot[:, k, t:t + 1], axis=0),
                                xn[:, t, :], None, bounds_check=ROWS - 1, oob_is_err=False).then_inc(scat, 16)

                xn_done = 2 * NQT + 7
                with nc.Block() as block:
                    @block.sync
                    def _(sp):
                        sp.dma_start(wr[:, :, :], wr_d.rearrange("(k p) n -> p k n", p=P)).then_inc(ld, 16)
                        if rb_d is not None:
                            sp.dma_start(rb[:, :], rb_d.rearrange("(a n) -> a n", a=1).to_broadcast([P, E])).then_inc(ld, 16)
                        places["loads"](sp)

                    @block.gpsimd
                    def _(pool):
                        places["weights"](pool, 0)
                        pool.iota(iota_i[:, :, :], [[1, E], [0, NQT]], base=0, channel_multiplier=0).then_inc(cst, 1)
                        pool.memset(again[:, :, :], 1.0).then_inc(csts, 1)
                        pool.memset(lower[:, :], 1.0).then_inc(csts, 1)
                        pool.wait_ge(csts, 2)
                        pool.memset(again[:, :, 0:1], 0.0).then_inc(cst, 1)
                        pool.memset(ones[:, :], 1.0).then_inc(cst, 1)
                        pool.affine_select(out=lower[:, :], in_=lower[:, :], compare_op=ALU.is_ge, fill=0.0,
                                           base=-1, pattern=[[1, P]], channel_multiplier=-1).then_inc(cst, 1)
                        if L == 0:
                            places["consts"](pool, cst)
                        pool.wait_ge(slots_s, 1)
                        pool.wait_ge(zeroed, 48)
                        if L == 0:
                            scatter(pool)
                            places["weights"](pool, 1)
                            pool.wait_ge(scat, 16 * 2 * NQT)

                    @block.scalar
                    def _(act):
                        act.wait_ge(lnv, 1)
                        act.activation(lnw[:, 3, :], lnw[:, 2, :], ACT.Sqrt).then_inc(lns, 1)
                        for i in range(8):
                            act.wait_ge(tr, i + 1)
                            k, g = i % 2, i // 2
                            act.activation(xT[:, k, g * 512:(g + 1) * 512], bank(i % 2)[:, :], ACT.Copy)\
                               .then_inc(tre, 1)
                        act.wait_ge(exin, 1)
                        if L == 0:
                            act.activation(small[:, 1, :], small[:, 0, :], ACT.Exp).then_inc(exps, 1)
                        else:
                            act.activation(ex[:, :, :], ex[:, :, :], ACT.Exp).then_inc(exps, 1)
                            act.activation(small[:, 1, :], small[:, 0, :], ACT.Exp).then_inc(exps, 1)

                    @block.tensor
                    def _(pe):
                        for i in range(8):
                            k, g = i % 2, i // 2
                            if i >= 2:
                                pe.wait_ge(tre, i - 1)
                            pe.wait_ge(lnc, xn_done - NQT + 4 * g + 4)
                            for q in range(4):
                                mmi = pe.transpose(bank(i % 2)[:, q * P:(q + 1) * P],
                                                   xn[:, 4 * g + q, k * P:(k + 1) * P], ident[:, :])
                            mmi.then_inc(tr, 1)
                        pe.wait_ge(ld, 16 if rb_d is None else 32)
                        pe.wait_ge(tre, 8)
                        for t in range(NQT):
                            for k in range(KD):
                                mmi = pe.matmul(bank(2)[:, t * E:(t + 1) * E], xT[:, k, t * P:(t + 1) * P], wr[:, k, :],
                                                start=(k == 0), stop=(k == KD - 1))
                        mmi.then_inc(lgt, 1)
                        pe.wait_ge(sums_in, 1)
                        pe.wait_ge(cst, 4)
                        pe.matmul(bank(3)[:, 0:E * NQT], lower[:, :], both[:, :, :].rearrange("p e t -> p (e t)"),
                                  start=True, stop=False)
                        pe.matmul(bank(3)[:, 0:E * NQT], ones[:, :], below[:, :, :].rearrange("p e t -> p (e t)"),
                                  start=False, stop=True)
                        pe.matmul(bank(4)[:, 0:E], ones[:, :], upto[:, :, NQT - 1], start=True, stop=True)\
                          .then_inc(pos, 1)

                    @block.vector
                    def _(dve):
                        got = norm_vector(dve, xn, lnc, lns, lnv)
                        assert got == xn_done, got
                        n = [0]

                        def link(ins):
                            n[0] += 1
                            ins.then_inc(chain, 1)
                            dve.wait_ge(chain, n[0])

                        dve.wait_ge(lgt, 1)
                        logits = bank(2)[:, 0:NQT * E].rearrange("p (t e) -> p t e", e=E)
                        if rb_d is None:
                            link(dve.tensor_copy(lg[:, :, :], logits))
                        else:
                            dve.wait_ge(ld, 32)
                            link(dve.tensor_tensor(lg[:, :, :], logits, rb[:, :].unsqueeze(1).to_broadcast([P, NQT, E]), ALU.add))
                        for t in range(NQT):
                            dve.max(v8[:, t, :], lg[:, t, :]).then_inc(chain, 1)
                        n[0] += NQT
                        dve.wait_ge(chain, n[0])
                        for t in range(NQT):
                            dve.max_index(i8[:, t, :], v8[:, t, :], lg[:, t, :]).then_inc(chain, 1)
                        n[0] += NQT
                        dve.wait_ge(chain, n[0])
                        d, e2, s1, s2, r, w = (small[:, i, :] for i in range(6))
                        if L:
                            link(dve.tensor_tensor(ex[:, :, :], lg[:, :, :], v8[:, :, 0:1].to_broadcast([P, NQT, E]), ALU.subtract))
                        link(dve.tensor_tensor(d, v8[:, :, 1], v8[:, :, 0], ALU.subtract))
                        dve.sem_inc(exin, 1)
                        for k in range(2):
                            link(dve.tensor_copy(idx[:, k, :], i8[:, :, k]))
                        dve.wait_ge(cst, 2)
                        link(dve.tensor_copy(iota_e[:, :, :], iota_i[:, :, :]))
                        for k in range(2):
                            link(dve.tensor_tensor(hot[:, k, :, :], iota_e[:, :, :],
                                                   idx[:, k, :].unsqueeze(1).to_broadcast([P, E, NQT]), ALU.is_equal))
                        link(dve.tensor_tensor(both[:, :, :], hot[:, 0, :, :], hot[:, 1, :, :], ALU.add))
                        flat = lambda x: x[:, :, :].rearrange("p e t -> p (e t)")
                        link(dve.tensor_tensor_scan(flat(upto), flat(again), flat(both), 0.0, ALU.mult, ALU.add))
                        link(dve.tensor_tensor(below[:, :, :], upto[:, :, :], both[:, :, :], ALU.subtract))
                        dve.sem_inc(sums_in, 1)
                        if L == 0:
                            dve.wait_ge(exps, 1)
                            link(dve.tensor_scalar(s1, e2, 1.0, None, ALU.add))
                            link(dve.reciprocal(gate[:, 0, :], s1))
                            link(dve.tensor_tensor(gate[:, 1, :], gate[:, 0, :], e2, ALU.mult))
                        else:
                            dve.wait_ge(exps, 2)
                            link(dve.tensor_reduce(s1, ex[:, :, :], AX.X, ALU.add))
                            link(dve.reciprocal(s2, s1))
                            link(dve.tensor_tensor(r, s2, e2, ALU.mult))
                            link(dve.tensor_tensor(w, s2, r, ALU.add))
                            link(dve.tensor_scalar(w, w, 1e-9, None, ALU.add))
                            link(dve.reciprocal(w, w))
                            link(dve.tensor_tensor(gate[:, 0, :], s2, w, ALU.mult))
                            link(dve.tensor_tensor(gate[:, 1, :], r, w, ALU.mult))
                        dve.wait_ge(pos, 1)
                        place = bank(3)[:, 0:E * NQT].rearrange("p (e t) -> p e t", e=E)
                        places["rows"](dve, link, place, bank(4)[:, 0:E], row, iota_e, pick, cst)
                        for k in range(2):
                            link(dve.tensor_tensor(pick[:, :, :], row[:, :, :], hot[:, k, :, :], ALU.mult))
                            link(dve.tensor_reduce(srow[:, k, :], pick[:, :, :].rearrange("p e t -> p t e"), AX.X, ALU.add))
                        if L:
                            for k in range(2):
                                link(dve.tensor_scalar(w, srow[:, k, :], float(ROWS), None, ALU.is_lt))
                                link(dve.tensor_tensor(gate[:, k, :], gate[:, k, :], w, ALU.mult))
                        link(dve.tensor_scalar(gate[:, :, :], gate[:, :, :], gates[:, 2 + L:3 + L], None, ALU.mult))
                        link(dve.tensor_copy(slot[:, :, :], srow[:, :, :]))
                        dve.sem_inc(slots_s, 1)
                return scatter, scat

        def experts0(xs, ys, tile_e, ends, pairs, ws, w_ld, b_ld):
            w1, w2, b1r, b2 = ws
            NF = F0 // P
            NJ = NF // 2
            NW = 32
            with ExitStack() as st:
                b1 = sb(st, "b1", [P, P])
                xt = sb(st, "xt", [P, 2, D])
                xTt = sb(st, "xTt", [P, 2, KD, P])
                sil = sb(st, "sil", [P, NJ, 2, P])
                hT = sb(st, "hT", [P, 2, F0])
                yv = sb(st, "yv", [P, 2, D])
                mi = sb(st, "mi", [P, 2, S], I32)
                off = sb(st, "mask_off", [P, S], BF16)
                mask_ld = [sem(f"e0_mask_loaded{i}") for i in range(2)]
                seen, counted = sem("e0_mask_seen"), sem("e0_mask_counted")
                x_ld = [sem(f"e0_rows{i}") for i in range(2)]
                y_st = [sem(f"e0_stored{i}") for i in range(2)]
                xtr, xte, u, si, hd, y, ye = (
                    sem(f"e0_{n}") for n in ("x_transposed", "xT", "up", "silu", "hidden", "down", "down_read"))
                btr, bt = sem("e0_bias_transposed"), sem("e0_bias")

                def pair_count(eng):
                    return eng.value_load(pairs[0:1, 0:1], min_val=1, max_val=NT0 // 2)

                with nc.Block() as block:
                    @block.gpsimd
                    def _(pool):
                        def load_mask(t):
                            pool.dma_start(mi[:, t % 2, :], mask_d[t * P:(t + 1) * P, :]).then_inc(mask_ld[t % 2], 16)

                        def count_mask(t):
                            pool.wait_ge(mask_ld[t % 2], 16 * (t // 2 + 1))
                            pool.tensor_scalar(off[:, :], mi[:, t % 2, :], 0, None, ALU.is_equal).then_inc(seen, 1)
                            pool.wait_ge(seen, t + 1)
                            pool.tensor_tensor(ignored[:, :], ignored[:, :], off[:, :], ALU.add).then_inc(counted, 1)
                            pool.wait_ge(counted, t + 2)
                            if t + 2 < NQT:
                                load_mask(t + 2)

                        pool.memset(ignored[:, :], 0.0).then_inc(counted, 1)
                        pool.wait_ge(counted, 1)
                        load_mask(0)
                        load_mask(1)
                        for e in range(2, E0):
                            for t in range(NQT * (e - 2) // (E0 - 2), NQT * (e - 1) // (E0 - 2)):
                                count_mask(t)
                            last = pool.value_load(ends[0:1, e - 2:e - 1], min_val=2, max_val=NT0 + 2)
                            pool.wait_ge(w_ld, NW * e)
                            pool.wait_ge(ye, last)
                            load_expert(pool, e, w1, w2, w_ld)
                        pool.wait_ge(w_ld, NW * E0)
                        count = pair_count(pool)
                        for z in range(2):
                            pool.wait_ge(y_st[z], count * 16 + 16)
                            pool.wait_ge(x_ld[z], count * 16 + 16)

                    @block.sync
                    def _(sp):
                        def load_rows(first, z):
                            sp.dma_start(xt[:, z, :], xs[bass.ds(first, P), :]).then_inc(x_ld[z], 16)

                        for z in range(2):
                            sp.sem_inc(y_st[z], 16)
                            load_rows(z * P, z)
                        with sp.Fori(0, pair_count(sp)) as it:
                            for z in range(2):
                                sp.wait_ge(xtr, it * 2 + (z + 1))
                                load_rows(it * (2 * P) + (2 + z) * P, z)
                            for z in range(2):
                                sp.wait_ge(ye, it * 2 + (z + 3))
                                sp.dma_start(ys[bass.ds(it * (2 * P) + z * P, P), :], yv[:, z, :]).then_inc(y_st[z], 16)

                    @block.tensor
                    def _(pe):
                        pe.sem_inc(y, 2)
                        pe.wait_ge(b_ld, 32)
                        pe.transpose(bank(4)[:, 0:P], b1r[:, :], ident[:, :]).then_inc(btr, 1)

                        def turn_x(z):
                            for k in range(KD):
                                mmi = pe.transpose(bank(6 + z)[:, k * P:(k + 1) * P], xt[:, z, k * P:(k + 1) * P], ident[:, :])
                            mmi.then_inc(xtr, 1)

                        def up(it, z, side):
                            for j in range(NJ):
                                pe.wait_ge(hd, it * (2 * NJ) + (z * NJ + j + 1))
                                for i, f in enumerate((2 * j, 2 * j + 1, NF + 2 * j, NF + 2 * j + 1)):
                                    for k in range(KD):
                                        mmi = pe.matmul(bank(j)[:, i * P:(i + 1) * P], w1[:, side, k, f * P:(f + 1) * P],
                                                        xTt[:, z, k, :], start=(k == 0), stop=(k == KD - 1))
                                mmi.then_inc(u, 1)

                        def down(it, z, odd):
                            pe.wait_ge(ye, it * 2 + (z + 1))
                            for f in range(NF):
                                if f % 2 == 0:
                                    pe.wait_ge(hd, it * (2 * NJ) + (z * NJ + f // 2 + 5))
                                mmi = pe.matmul(bank(4 + z)[:, 0:D], hT[:, z, f * P:(f + 1) * P],
                                                w2[:, bass.ds(odd * (NF * D) + f * D, D)],
                                                start=(f == 0), stop=(f == NF - 1))
                            mmi.then_inc(y, 1)

                        for z in range(2):
                            pe.wait_ge(x_ld[z], 16)
                            turn_x(z)
                        pe.wait_ge(bt, 1)
                        with pe.Fori(0, pair_count(pe)) as it:
                            expert = [pe.value_load(tile_e[0:1, 0, bass.ds(it * 2 + z, 1)], min_val=0, max_val=E0 - 1)
                                      for z in range(2)]
                            odd = [pe.value_load(tile_e[0:1, 1, bass.ds(it * 2 + z, 1)], min_val=0, max_val=1)
                                   for z in range(2)]
                            for z in range(2):
                                pe.wait_ge(w_ld, expert[z] * NW + NW)
                                pe.wait_ge(xte, it * 2 + (z + 1))
                                with pe.If(odd[z] > 0):
                                    up(it, z, 1)
                                with pe.Else():
                                    up(it, z, 0)
                            for z in range(2):
                                pe.wait_ge(x_ld[z], it * 16 + 32)
                                turn_x(z)
                            for z in range(2):
                                down(it, z, odd[z])

                    @block.scalar
                    def _(act):
                        act.wait_ge(btr, 1)
                        act.activation(b1[:, :], bank(4)[:, 0:P], ACT.Copy).then_inc(bt, 1)

                        def x_out(n, z):
                            act.wait_ge(xtr, n + 1)
                            act.activation(xTt[:, z, :, :].rearrange("p k t -> p (k t)"), bank(6 + z)[:, 0:D], ACT.Copy)\
                               .then_inc(xte, 1)
                        x_out(0, 0)
                        x_out(1, 1)
                        act.wait_ge(bt, 1)
                        with act.Fori(0, pair_count(act)) as it:
                            for z in range(2):
                                e = act.value_load(tile_e[0:1, 0, bass.ds(it * 2 + z, 1)], min_val=0, max_val=E0 - 1)
                                for j in range(NJ):
                                    act.wait_ge(u, it * (2 * NJ) + (z * NJ + j + 1))
                                    for i in range(2):
                                        last = act.activation(sil[:, j, i, :], bank(j)[:, i * P:(i + 1) * P], ACT.Silu,
                                                              bias=b1[:, bass.ds(e * (2 * NF) + (2 * j + i), 1)])
                                    last.then_inc(si, 1)
                            for z in range(2):
                                x_out(it * 2 + (z + 2), z)

                    @block.vector
                    def _(dve):
                        dve.sem_inc(hd, NJ)
                        dve.sem_inc(ye, 2)
                        dve.wait_ge(bt, 1)
                        with dve.Fori(0, pair_count(dve)) as it:
                            experts = []
                            for z in range(2):
                                e = dve.value_load(tile_e[0:1, 0, bass.ds(it * 2 + z, 1)], min_val=0, max_val=E0 - 1)
                                experts.append(e)
                                dve.wait_ge(y, it * 2 + (z + 1))
                                for j in range(NJ):
                                    dve.wait_ge(si, it * (2 * NJ) + (z * NJ + j + 1))
                                    for i in range(2):
                                        f = 2 * j + i
                                        last = dve.scalar_tensor_tensor(
                                            out=hT[:, z, f * P:(f + 1) * P], in0=bank(j)[:, (2 + i) * P:(3 + i) * P],
                                            scalar=b1[:, bass.ds(e * (2 * NF) + (NF + f), 1)], in1=sil[:, j, i, :],
                                            op0=ALU.add, op1=ALU.mult)
                                    last.then_inc(hd, 1)
                            for z in range(2):
                                dve.wait_ge(y, it * 2 + (z + 3))
                                dve.wait_ge(y_st[z], it * 16 + 16)
                                dve.tensor_tensor(yv[:, z, :], bank(4 + z)[:, 0:D],
                                                  b2[:, bass.ds(experts[z] * D, D)], ALU.add).then_inc(ye, 1)

        MF = [(m * P, min(P, F1 - m * P)) for m in range(-(-F1 // P))]
        NM = len(MF)
        WB = 4
        SHARED = WB

        def load_mlp(queue, at, gate_d, up_d, down_d, wts, done):
            wg, wu, wd = wts
            full = F1 // P * P
            queue.dma_start(wg[:, at, :, :], gate_d.rearrange("(k p) n -> p k n", p=P)).then_inc(done, 16)
            queue.dma_start(wu[:, at, :, :], up_d.rearrange("(k p) n -> p k n", p=P)).then_inc(done, 16)
            queue.dma_start(wd[:, at, 0:F1 // P, :], down_d[0:full, :].rearrange("(m p) n -> p m n", p=P)).then_inc(done, 16)
            queue.dma_start(wd[0:F1 - full, at, F1 // P, :], down_d[full:F1, :]).then_inc(done, 16)

        def experts1(xs, ys, xn, xT, wts, w_ld, scatter, scat):
            wg, wu, wd = wts
            CT = [(i * P, min(P, CAP - i * P)) for i in range(-(-CAP // P))]
            full = CAP // P * P
            with ExitStack() as st:
                xe = sb(st, "xe", [P, 2, len(CT), D])
                xTe = sb(st, "xTe", [P, 2, KD, CAP])
                sil = sb(st, "sil1", [P, 2, 512])
                hT1 = sb(st, "hT1", [P, 2, NM, 512])
                ye1 = sb(st, "ye1", [P, 2, len(CT), D])
                xn_in = sem("s1_normed_added")
                x_ld = [sem(f"e1_rows{i}") for i in range(2)]
                y_st = [sem(f"e1_stored{i}") for i in range(2)]
                xtr, xte, gu, si, h, y, ye = (
                    sem(f"e1_{n}") for n in ("x_transposed", "xT", "gate_up", "silu", "hidden", "down", "down_read"))
                s_gu, s_si, s_h, s_y, s_ye = (sem(f"s1_{n}") for n in ("gate_up", "silu", "hidden", "down", "down_read"))
                NI1 = E1 // WB

                with nc.Block() as block:
                    @block.sync
                    def _(sp):
                        def load_rows(r, z):
                            sp.dma_start(xe[:, z, 0:CAP // P, :],
                                         xs[bass.ds(r, full), :].rearrange("(m p) n -> p m n", p=P)).then_inc(x_ld[z], 16)
                            sp.dma_start(xe[0:CAP - full, z, CAP // P, :],
                                         xs[bass.ds(r + full, CAP - full), :]).then_inc(x_ld[z], 16)

                        sp.wait_ge(scat, 16 * 2 * NQT)
                        for z in range(2):
                            sp.sem_inc(y_st[z], 32)
                            load_rows(z * CAP, z)
                        with sp.Fori(0, NI1) as it:
                            for q0 in range(0, WB, 2):
                                for z in range(2):
                                    sp.wait_ge(xtr, it * WB + (q0 + z + 1))
                                    load_rows(it * (WB * CAP) + (q0 + z + 2) * CAP, z)
                                for z in range(2):
                                    sp.wait_ge(ye, it * WB + (q0 + z + 2))
                                    r = it * (WB * CAP) + (q0 + z) * CAP
                                    sp.dma_start(ys[bass.ds(r, full), :].rearrange("(m p) n -> p m n", p=P),
                                                 ye1[:, z, 0:CAP // P, :]).then_inc(y_st[z], 16)
                                    sp.dma_start(ys[bass.ds(r + full, CAP - full), :],
                                                 ye1[0:CAP - full, z, CAP // P, :]).then_inc(y_st[z], 16)
                        for z in range(2):
                            sp.wait_ge(y_st[z], 32 + 32 * (E1 // 2))
                            sp.wait_ge(x_ld[z], 32 + 32 * (E1 // 2))

                    @block.gpsimd
                    def _(pool):
                        scatter(pool)
                        for e in range(WB, E1):
                            pool.wait_ge(y, 2 + e - WB + 1)
                            load_mlp(pool, e % WB, F["w_gate"][e], F["w_up"][e], F["w_down"][e], wts, w_ld[e % WB])

                    @block.tensor
                    def _(pe):
                        pe.wait_ge(w_ld[SHARED], 64)

                        def shared_down(c):
                            pe.wait_ge(s_h, (c + 1) * NM)
                            for q in range(QTC):
                                j = c * QTC + q
                                if j >= 2:
                                    pe.wait_ge(s_ye, j - 1)
                                for m, (f0, fw) in enumerate(MF):
                                    mmi = pe.matmul(bank(4 + j % 2)[:, 0:D], hT1[0:fw, c % 2, m, q * P:(q + 1) * P],
                                                    wd[0:fw, SHARED, m, :], start=(m == 0), stop=(m == NM - 1))
                                mmi.then_inc(s_y, 1)

                        for c in range(NC):
                            for m, (f0, fw) in enumerate(MF):
                                n = c * NM + m
                                if n >= 2:
                                    pe.wait_ge(s_h, n - 1)
                                for i, w in enumerate((wg, wu)):
                                    for k in range(KD):
                                        mmi = pe.matmul(bank(2 * (n % 2) + i)[0:fw, :], w[:, SHARED, k, f0:f0 + fw],
                                                        xT[:, k, c * QC:(c + 1) * QC], start=(k == 0), stop=(k == KD - 1))
                                mmi.then_inc(s_gu, 1)
                            if c:
                                shared_down(c - 1)
                        shared_down(NC - 1)

                        def turn_x(z):
                            for k in range(KD):
                                for i, (c0, cw) in enumerate(CT):
                                    mmi = pe.transpose(bank(6 + k)[:, c0:c0 + cw], xe[0:cw, z, i, k * P:(k + 1) * P],
                                                       ident[0:cw, 0:cw])
                            mmi.then_inc(xtr, 1)

                        def up(it, q):
                            z = q % 2
                            pe.wait_ge(w_ld[q], it * 64 + 64)
                            pe.wait_ge(xte, it * (2 * WB) + 2 * (q + 1))
                            for m, (f0, fw) in enumerate(MF):
                                pe.wait_ge(h, it * (WB * NM) + (NM * q + m + 1))
                                b = (NM * q + m) % 2
                                for i, w in enumerate((wg, wu)):
                                    for k in range(KD):
                                        mmi = pe.matmul(bank(2 * b + i)[0:fw, 0:CAP], w[:, q, k, f0:f0 + fw],
                                                        xTe[:, z, k, :], start=(k == 0), stop=(k == KD - 1))
                                mmi.then_inc(gu, 1)

                        def down(it, q):
                            z = q % 2
                            pe.wait_ge(h, it * (WB * NM) + (NM * q + NM + 2))
                            pe.wait_ge(ye, it * WB + (q + 1))
                            for i, (c0, cw) in enumerate(CT):
                                for m, (f0, fw) in enumerate(MF):
                                    mmi = pe.matmul(bank(4 + i // 2)[0:cw, (i % 2) * D:(i % 2 + 1) * D],
                                                    hT1[0:fw, z, m, c0:c0 + cw], wd[0:fw, q, m, :],
                                                    start=(m == 0), stop=(m == NM - 1))
                            mmi.then_inc(y, 1)

                        for z in range(2):
                            pe.wait_ge(x_ld[z], 32)
                            if z:
                                pe.wait_ge(xte, 2)
                            turn_x(z)
                        pe.wait_ge(s_ye, NQT)
                        pe.sem_inc(y, 2)
                        with pe.Fori(0, NI1) as it:
                            for q0 in range(0, WB, 2):
                                up(it, q0)
                                up(it, q0 + 1)
                                for q in (q0, q0 + 1):
                                    down(it, q)
                                    pe.wait_ge(x_ld[q % 2], it * (32 * WB // 2) + 32 * (q // 2 + 2))
                                    pe.wait_ge(xte, it * (2 * WB) + (2 * q + 4))
                                    turn_x(q % 2)

                    @block.scalar
                    def _(act):
                        act.sem_inc(ye, 1)
                        for n in range(NC * NM):
                            fw = MF[n % NM][1]
                            act.wait_ge(s_gu, n + 1)
                            if n >= 2:
                                act.wait_ge(s_h, n - 1)
                            act.activation(sil[0:fw, n % 2, :], bank(2 * (n % 2))[0:fw, :], ACT.Silu).then_inc(s_si, 1)
                        act.wait_ge(s_h, NC * NM)

                        def x_out(n, z):
                            act.wait_ge(xtr, n + 1)
                            for k in range(KD):
                                act.activation(xTe[:, z, k, :], bank(6 + k)[:, 0:CAP], ACT.Copy).then_inc(xte, 1)

                        for z in range(2):
                            x_out(z, z)
                        with act.Fori(0, NI1) as it:
                            for q0 in range(0, WB, 2):
                                for q in (q0, q0 + 1):
                                    for m, (f0, fw) in enumerate(MF):
                                        b = (NM * q + m) % 2
                                        act.wait_ge(gu, it * (WB * NM) + (NM * q + m + 1))
                                        act.wait_ge(h, it * (WB * NM) + (NM * q + m + 1))
                                        act.activation(sil[0:fw, b, 0:CAP], bank(2 * b)[0:fw, 0:CAP], ACT.Silu)\
                                           .then_inc(si, 1)
                                for q in (q0, q0 + 1):
                                    z = q % 2
                                    act.wait_ge(y, it * WB + (q + 3))
                                    act.wait_ge(y_st[z], it * (32 * WB // 2) + 32 * (q // 2 + 1))
                                    act.activation(ye1[:, z, 0:2, :].rearrange("p a d -> p (a d)"), bank(4), ACT.Copy)
                                    act.activation(ye1[0:CT[2][1], z, 2, :], bank(5)[0:CT[2][1], 0:D], ACT.Copy).then_inc(ye, 1)
                                    x_out(it * WB + (q + 2), z)

                    @block.vector
                    def _(dve):
                        dve.sem_inc(h, 2)
                        for j in range(NQT):
                            dve.scalar_tensor_tensor(out=xres[:, j, :], in0=xn[:, j, :], scalar=gates[:, 3:4],
                                                     in1=xres[:, j, :], op0=ALU.mult, op1=ALU.add).then_inc(xn_in, 1)

                        def shared_out(c):
                            for q in range(QTC):
                                j = c * QTC + q
                                dve.wait_ge(s_y, j + 1)
                                dve.wait_ge(xn_in, j + 1)
                                dve.scalar_tensor_tensor(out=xres[:, j, :], in0=bank(4 + j % 2)[:, 0:D], scalar=gates[:, 3:4],
                                                         in1=xres[:, j, :], op0=ALU.mult, op1=ALU.add).then_inc(s_ye, 1)
                        for c in range(NC):
                            for m, (f0, fw) in enumerate(MF):
                                n = c * NM + m
                                dve.wait_ge(s_si, n + 1)
                                dve.tensor_tensor(hT1[0:fw, c % 2, m, :], sil[0:fw, n % 2, :],
                                                  bank(2 * (n % 2) + 1)[0:fw, :], ALU.mult).then_inc(s_h, 1)
                            if c:
                                shared_out(c - 1)
                        shared_out(NC - 1)
                        with dve.Fori(0, NI1) as it:
                            for q in range(WB):
                                dve.wait_ge(y, it * WB + (q + 1))
                                for m, (f0, fw) in enumerate(MF):
                                    b = (NM * q + m) % 2
                                    dve.wait_ge(si, it * (WB * NM) + (NM * q + m + 1))
                                    dve.tensor_tensor(hT1[0:fw, q % 2, m, 0:CAP], sil[0:fw, b, 0:CAP],
                                                      bank(2 * b + 1)[0:fw, 0:CAP], ALU.mult).then_inc(h, 1)

        def combine(L, ys, gate, slot):
            with ExitStack() as st:
                NR = 8
                yg = sb(st, f"yg{L}", [P, NR, D])
                zs = sem(f"c{L}_zeroed")
                got = [sem(f"c{L}_gathered{i}") for i in range(NR)]
                used = sem(f"c{L}_used")
                with nc.Block() as block:
                    @block.gpsimd
                    def _(pool):
                        pool.memset(yg[:, :, :], 0.0).then_inc(zs, 1)
                        pool.wait_ge(zs, 1)
                        for n in range(2 * NQT):
                            t, k = n // 2, n % 2
                            if n >= NR:
                                pool.wait_ge(used, n - NR + 1)
                            pool.indirect_dma_start(
                                yg[:, n % NR, :], None, ys[:, :],
                                bass.IndirectOffsetOnAxis(ap=slot[:, k, t:t + 1], axis=0),
                                bounds_check=ROWS - 1, oob_is_err=False).then_inc(got[n % NR], 16)

                    @block.vector
                    def _(dve):
                        for n in range(2 * NQT):
                            t, k = n // 2, n % 2
                            dve.wait_ge(got[n % NR], 16 * (n // NR + 1))
                            if k:
                                dve.wait_ge(used, n)
                            dve.scalar_tensor_tensor(out=xres[:, t, :], in0=yg[:, n % NR, :], scalar=gate[:, k, t:t + 1],
                                                     in1=xres[:, t, :], op0=ALU.mult, op1=ALU.add).then_inc(used, 1)

        def ffn_layer(L):
            with ExitStack() as st:
                E = (E0, E1)[L]
                gate = sb(st, f"gate{L}", [P, 2, NQT])
                slot = sb(st, f"slot{L}", [P, 2, NQT], U32)
                xn = sb(st, f"fxn{L}", [P, NQT, D])
                xT = sb(st, f"fxT{L}", [P, KD, T])
                places = {}
                if L == 0:
                    pairs = sb(st, "pairs", [P, 1], I32)
                    pairs_f = sb(st, "pairs_f", [P, 1])
                    w1 = sb(st, "w1", [P, 2, KD, 2 * F0])
                    w2 = sb(st, "w2", [P, 2 * (F0 // P) * D])
                    b1r = sb(st, "b1r", [P, P])
                    b2 = sb(st, "b2", [P, E0 * D])
                    w_ld, b_ld = sem("e0_weights"), sem("e0_biases_loaded")

                    def loads(sp):
                        sp.dma_start(b1r[:, :], F["b1"].rearrange("e (f p) -> (e f) p", p=P)).then_inc(b_ld, 16)
                        sp.dma_start(b2[:, :], F["b2"].rearrange("(a e) d -> a (e d)", a=1).to_broadcast([P, E0 * D]))\
                          .then_inc(b_ld, 16)

                    def first_weights(pool, e):
                        if e:
                            pool.wait_ge(w_ld, 32)
                        load_expert(pool, e, w1, w2, w_ld)
                    tile_e = sb(st, "tile_e", [P, 2, NT0], I32)
                    ends = sb(st, "ends", [P, E0], I32)
                    tile_f = sb(st, "tile_f", [P, 2, NT0])
                    cnt = sb(st, "cnt", [P, 4, E0])
                    thr_i = sb(st, "thr_i", [P, E0, NQT], I32)
                    thr = sb(st, "thr", [P, E0, NQT])
                    tno_i = sb(st, "tno_i", [P, NT0, E0 - 1], I32)
                    tno = sb(st, "tno", [P, NT0, E0 - 1])
                    sign = sb(st, "sign", [P, E0])
                    one8 = sb(st, "one8", [P, E0])

                    def consts(pool, cst):
                        pool.iota(thr_i[:, :, :], [[0, E0], [P, NQT]], base=0, channel_multiplier=0).then_inc(cst, 1)
                        pool.iota(tno_i[:, :, :], [[1, NT0], [0, E0 - 1]], base=0, channel_multiplier=0).then_inc(cst, 1)
                        pool.memset(one8[:, :], 1.0).then_inc(cst, 1)
                        pool.memset(sign[:, :].rearrange("p (a b) -> p a b", b=2)[:, :, 0], 1.0).then_inc(cst, 1)
                        pool.memset(sign[:, :].rearrange("p (a b) -> p a b", b=2)[:, :, 1], -1.0).then_inc(cst, 1)

                    def rows(dve, link, place, counts, row, iota_e, pick, cst):
                        dve.wait_ge(cst, 9)
                        link(dve.tensor_copy(thr[:, :, :], thr_i[:, :, :]))
                        link(dve.tensor_copy(tno[:, :, :], tno_i[:, :, :]))
                        n, nt, end, start = (cnt[:, i, :] for i in range(4))
                        link(dve.tensor_copy(n, counts))
                        link(dve.tensor_tensor(pick[:, :, :], thr[:, :, :], n.unsqueeze(2).to_broadcast([P, E0, NQT]), ALU.is_lt))
                        link(dve.tensor_reduce(nt, pick[:, :, :], AX.X, ALU.add))
                        link(dve.tensor_tensor_scan(end, one8[:, :], nt, 0.0, ALU.mult, ALU.add))
                        link(dve.tensor_tensor(start, end, nt, ALU.subtract))
                        link(dve.tensor_scalar(start, start, float(P), None, ALU.mult))
                        link(dve.tensor_tensor(row[:, :, :], place, start.unsqueeze(2).to_broadcast([P, E0, NQT]), ALU.add))
                        link(dve.tensor_scalar(ends[:, :], end, 2.0, None, ALU.add))
                        even = tno[:, :, 0].rearrange("p (a b) -> p a b", b=2)[:, :, 0]
                        tests = tile_f[:, 0, 0:NT0 // 2]
                        link(dve.tensor_tensor(tests, even, end[:, E0 - 1:E0].to_broadcast([P, NT0 // 2]), ALU.is_lt))
                        link(dve.tensor_reduce(pairs_f[:, :], tests, AX.X, ALU.add))
                        link(dve.tensor_copy(pairs[:, :], pairs_f[:, :]))
                        link(dve.tensor_tensor(tno[:, :, :], tno[:, :, :],
                                               end[:, 0:E0 - 1].unsqueeze(1).to_broadcast([P, NT0, E0 - 1]), ALU.is_ge))
                        link(dve.tensor_reduce(tile_f[:, 0, :], tno[:, :, :], AX.X, ALU.add))
                        link(dve.tensor_tensor(tno[:, :, :], tno[:, :, :],
                                               sign[:, 0:E0 - 1].unsqueeze(1).to_broadcast([P, NT0, E0 - 1]), ALU.mult))
                        link(dve.tensor_reduce(tile_f[:, 1, :], tno[:, :, :], AX.X, ALU.add))
                        link(dve.tensor_copy(tile_e[:, :, :], tile_f[:, :, :]))
                    places["consts"], places["rows"], places["loads"] = consts, rows, loads
                    places["weights"] = first_weights
                    route(0, E, F["wrT"], None, xn, xT, gate, slot, xs0, places)
                    experts0(xs0, ys0, tile_e, ends, pairs, (w1, w2, b1r, b2), w_ld, b_ld)
                    combine(0, ys0, gate, slot)
                else:
                    def rows1(dve, link, place, counts, row, iota_e, pick, cst):
                        link(dve.tensor_scalar(pick[:, :, :], place, float(CAP), float(FAR), ALU.is_ge, ALU.mult))
                        link(dve.scalar_tensor_tensor(out=row[:, :, :], in0=iota_e[:, :, :], scalar=float(CAP), in1=pick[:, :, :],
                                                      op0=ALU.mult, op1=ALU.add))
                        link(dve.tensor_tensor(row[:, :, :], row[:, :, :], place, ALU.add))
                    wts = (sb(st, "wg", [P, WB + 1, KD, F1]), sb(st, "wu", [P, WB + 1, KD, F1]), sb(st, "wd", [P, WB + 1, NM, D]))
                    w_ld = [sem(f"e1_weights{i}") for i in range(WB + 1)]

                    def first_weights1(pool, e):
                        load_mlp(pool, SHARED, F["sw_gate"], F["sw_up"], F["sw_down"], wts, w_ld[SHARED])
                        for e in range(WB):
                            load_mlp(pool, e, F["w_gate"][e], F["w_up"][e], F["w_down"][e], wts, w_ld[e])
                    places["rows"], places["loads"] = rows1, lambda sp: None
                    places["weights"] = first_weights1
                    scatter, scat = route(1, E, F["router_w"], F["router_b"], xn, xT, gate, slot, xs1, places)
                    experts1(xs1, ys1, xn, xT, wts, w_ld, scatter, scat)
                    combine(1, ys1, gate, slot)

        def store_out():
            done = sem("out_stored")
            with nc.Block() as block:
                @block.sync
                def _(sp):
                    sp.dma_start(out_d.rearrange("(t p) d -> p t d", p=P), xres[:, :, :]).then_inc(done, 16)
                    sp.wait_ge(done, 16)

        xs0, xs1 = scratch("rows0", [ROWS + 2 * P, D], F32), scratch("rows1", [ROWS + 2 * CAP, D], F32)
        ys0, ys1 = scratch("outs0", [ROWS, D], F32), scratch("outs1", [ROWS, D], F32)
        zero = sb(ctx, "zero", [P, D])
        zeroed, zms = ctx.enter_context(nc.semaphore("rows_zeroed")), sem("zero_made")
        with nc.Block() as block:
            @block.gpsimd
            def _(pool):
                pool.memset(zero[:, :], 0.0).then_inc(zms, 1)

            @block.sync
            def _(sp):
                sp.wait_ge(zms, 1)
                for r in (xs0, xs1, ys0[2 * T:ROWS, :]):
                    sp.dma_start(r.rearrange("(t p) d -> p t d", p=P),
                                 zero[:, :].unsqueeze(1).to_broadcast([P, r.shape[0] // P, D])).then_inc(zeroed, 16)
                sp.wait_ge(zeroed, 48)

        stages = (("x1", attention_layer, 0), ("x2", ffn_layer, 0), ("x3", attention_layer, 1), ("x4", ffn_layer, 1))
        for name, layer, L in stages:
            layer(L)
            free_semaphores()
            if stop == name:
                break
        store_out()


STOP = None
_NAMES = ["Wq", "bq", "Wk", "bk", "Wv", "bv", "Wo", "bo"]


def kernel(**inputs):
    import concourse.bacc as _bacc
    from concourse.bass_utils import run_bass_kernel_spmd as _run

    nc = _bacc.Bacc("TRN2", target_bir_lowering=False, num_devices=1)
    arrays = {}

    def give(name, a):
        a = np.ascontiguousarray(a)
        arrays[name] = a
        return nc.dram_tensor(name, a.shape, mybir.dt.from_np(a.dtype), kind="ExternalInput").ap()

    x = give("x", inputs["x"].reshape(T, D))
    ctxT = give("ctxT", inputs["ctx_1024"].reshape(S, D).T)
    mask = give("mask", inputs["mask_SxS2_ik0"])
    maskT = give("maskT", inputs["mask_SxS2_ik0"].T)
    gx, gf = give("g_xattn", inputs["g_xattn"]), give("g_ffn", inputs["g_ffn"])
    W = []
    for L in range(2):
        w = {}
        for n in _NAMES:
            a = inputs[f"L{L}_xattn_{n}"]
            if n[0] == "W":
                w[n + "T"] = give(f"L{L}_{n}T", a.T)
            else:
                w[n] = give(f"L{L}_{n}", a)
        W.append(w)
    out = nc.dram_tensor("out", (T, D), F32, kind="ExternalOutput").ap()
    F = {n: give(f"L0_{n}", inputs[f"L0_ffn_{n}"]) for n in ("w1", "b1", "w2", "b2")}
    F["wrT"] = give("L0_wrT", inputs["L0_ffn_wr"].T)
    for n in ("router_w", "router_b", "w_gate", "w_up", "w_down", "sw_gate", "sw_up", "sw_down"):
        F[n] = give(f"L1_{n}", inputs[f"L1_ffn_{n}"])
    build(nc, x, ctxT, mask, maskT, gx, gf, W, F, out, STOP)
    r = _run(nc, [arrays], core_ids=[0])
    return r.results[0]["out"].reshape(1, T, D)
```

```python
from contextlib import ExitStack

import numpy as np

import concourse.bass as bass
from concourse import mybir

F32 = mybir.dt.float32
BF16 = mybir.dt.bfloat16
I32 = mybir.dt.int32
U32 = mybir.dt.uint32
ALU = mybir.AluOpType
ACT = mybir.ActivationFunctionType
AX = mybir.AxisListType

P = 128
T = 2048
D = 256
KD = D // P
S = 1601
NQT = T // P
H = 16
DH = D // H
NKT = -(-S // P)
QC = 512
NC = T // QC
QTC = QC // P
SP_ = S + 1
TAIL = 9
EPS = 1e-5
MASKED = -1e30
DEAD = -1e29
PAIRS = ((0, 0), (0, 1), (1, 0), (0, 2), (1, 1), (2, 0))
NB = len(PAIRS) * DH
RB = NB
RM = NB + 1
KA = NB + 1
KC = NB + 4
G = 4
NV = DH + 1
SLOTS = 4
LAG = 2
AB = 3

E0, F0 = 8, 1024
E1, F1 = 16, 352
CAP = -(-5 * 2 * T // (4 * E1))
ROWS = E1 * CAP
NT0 = ROWS // P
FAR = 1 << 20
assert NT0 >= 2 * T // P + E0 - 1


def key_tiles(first=0):
    return [(j * P, min(P, S - j * P)) for j in range(first, NKT)]


def groups_of(n, most):
    k = -(-n // most)
    out, at = [], 0
    for i in range(k):
        m = n // k + (i < n % k)
        out.append((at, m))
        at += m
    return out


def build(nc, x_d, ctxT_d, mask_d, maskT_d, gx_d, gf_d, W, F, out_d):
    ctx = ExitStack()

    def sb(stack, name, shape, dt=F32):
        return stack.enter_context(nc.sbuf_tensor(name, shape, dt))

    layer_sems = []

    def sem(name):
        layer_sems.append(nc.alloc_semaphore(name=name))
        return layer_sems[-1]

    def free_semaphores():
        nc.clear_and_free_semaphores(layer_sems)
        nc.all_engine_barrier()
        layer_sems.clear()

    def scratch(name, shape, dt):
        return nc.dram_tensor(name, shape, dt, kind="Internal").ap()

    with ctx:
        psA = ctx.enter_context(nc.psum_tensor("psA", [P, AB, 512], F32))
        psO = ctx.enter_context(nc.psum_tensor("psO", [P, 512], F32))
        psC = ctx.enter_context(nc.psum_tensor("psC", [P, 2, 1024], F32))

        def bank(i):
            if i < AB:
                return psA[:, i, :]
            if i == AB:
                return psO[:, :]
            return psC[:, (i - 4) // 2, (i % 2) * 512:(i % 2) * 512 + 512]

        xres = sb(ctx, "xres", [P, NQT, D])
        Kst = sb(ctx, "Kst", [P, H, SP_], BF16)
        ident = sb(ctx, "ident", [P, P])
        identb = sb(ctx, "identb", [P, P], BF16)
        causb = sb(ctx, "causb", [P, P], BF16)
        gates = sb(ctx, "gates", [P, 4])
        causbT = sb(ctx, "causbT", [P, P], BF16)
        ignored = sb(ctx, "ignored", [P, S], BF16)
        stats = sb(ctx, "stats", [P, NQT, 6])
        zero = sb(ctx, "zero", [P, D])
        lnw = sb(ctx, "lnw", [P, 6, NQT])
        tail_only = sb(ctx, "tail_only", [P, 1], I32)

        c_ld, c_ms, c_id, c_tanh = sem("const_loaded"), sem("const_memset"), sem("const_made"), sem("tanh_done")
        with nc.Block() as block:
            @block.sync
            def _(sp):
                sp.dma_start(gates[:, 0:2], gx_d.rearrange("(a n) -> a n", a=1).to_broadcast([P, 2])).then_inc(c_ld, 16)
                sp.dma_start(gates[:, 2:4], gf_d.rearrange("(a n) -> a n", a=1).to_broadcast([P, 2])).then_inc(c_ld, 16)

            @block.scalar
            def _(act):
                act.wait_ge(c_ld, 32)
                act.activation(gates[:, :], gates[:, :], ACT.Tanh).then_inc(c_tanh, 1)

            @block.gpsimd
            def _(pool):
                pool.memset(ident[:, :], 0.0).then_inc(c_ms, 1)
                pool.memset(identb[:, :], 0.0).then_inc(c_ms, 1)
                pool.memset(causb[:, :], 0.0).then_inc(c_ms, 1)
                pool.memset(causbT[:, :], 0.0).then_inc(c_ms, 1)
                pool.memset(zero[:, :], 0.0).then_inc(c_ms, 1)
                pool.wait_ge(c_ms, 5)
                pool.affine_select(out=causbT[:, :], in_=causbT[:, :], compare_op=ALU.is_ge, fill=MASKED,
                                   base=0, pattern=[[1, P]], channel_multiplier=-1).then_inc(c_id, 1)
                for m in (ident, identb):
                    pool.affine_select(out=m[:, :], in_=m[:, :], compare_op=ALU.not_equal, fill=1.0,
                                       base=0, pattern=[[-1, P]], channel_multiplier=1).then_inc(c_id, 1)
                pool.affine_select(out=causb[:, :], in_=causb[:, :], compare_op=ALU.is_ge, fill=MASKED,
                                   base=0, pattern=[[-1, P]], channel_multiplier=1).then_inc(c_id, 1)

        def norm_vector(dve, xn, chain, tag_sqrt, tag_var, have_stats=False):
            n = [0]

            def link(ins):
                n[0] += 1
                ins.then_inc(chain, 1)
                dve.wait_ge(chain, n[0])

            if not have_stats:
                with dve.Fori(0, NQT // 4) as t4:
                    for i in range(4):
                        t = t4 * 4 + i
                        dve.bn_stats(stats[:, bass.ds(t, 1), :].rearrange("p a b -> p (a b)"),
                                     xres[:, bass.ds(t, 1), :].rearrange("p a b -> p (a b)")).then_inc(chain, 1)
                n[0] = NQT
                dve.wait_ge(chain, NQT)
            me, ve, mo, vo = (stats[:, :, i] for i in (1, 2, 4, 5))
            mean, diff, var, std, rstd, tmp = (lnw[:, i, :] for i in range(6))
            link(dve.tensor_tensor(mean, me, mo, ALU.add))
            link(dve.tensor_scalar(mean, mean, 0.5, None, ALU.mult))
            link(dve.tensor_tensor(diff, me, mo, ALU.subtract))
            link(dve.tensor_tensor(diff, diff, diff, ALU.mult))
            link(dve.tensor_tensor(var, ve, vo, ALU.add))
            link(dve.tensor_scalar(var, var, 1.0 / D, EPS, ALU.mult, ALU.add))
            dve.scalar_tensor_tensor(out=var, in0=diff, scalar=0.25, in1=var, op0=ALU.mult, op1=ALU.add)\
               .then_inc(tag_var, 1)
            dve.wait_ge(tag_sqrt, 1)
            link(dve.reciprocal(rstd, std))
            with dve.Fori(0, NQT // 4) as t4:
                for i in range(4):
                    t = t4 * 4 + i
                    dve.tensor_scalar(xn[:, bass.ds(t, 1), :].rearrange("p a b -> p (a b)"),
                                      xres[:, bass.ds(t, 1), :].rearrange("p a b -> p (a b)"),
                                      lnw[:, 0, bass.ds(t, 1)], lnw[:, 4, bass.ds(t, 1)],
                                      ALU.subtract, ALU.mult).then_inc(chain, 1)
            return n[0] + NQT

        def load_key_stack(queue, l, Ks, done):
            for b, (_, kp) in enumerate(PAIRS):
                queue.dma_start(Kst[b * DH:(b + 1) * DH, :, 0:S],
                                Ks[l][kp].rearrange("(h d) s -> d h s", d=DH)).then_inc(done, 16)

        def projections(L, ql, kl, Vaug=None, Qs=None, beside=None):
            with ExitStack() as st:
                NB = 2
                width_most = S if ql is None else T
                if ql is not None:
                    w = W[ql]
                    xn = sb(st, f"xn{L}", [P, NQT, D])
                    xT = sb(st, f"xT{L}", [P, KD, T])
                    wq = sb(st, f"wq{L}", [P, KD, D])
                    bq = sb(st, f"bq{L}", [P, KD])
                full = sb(st, f"full{L}", [P, NB, width_most])
                parts = sb(st, f"parts{L}", [P, NB, 3, width_most], BF16)
                mm, ev, spl = sem(f"p{L}_kq_done"), sem(f"p{L}_kq_evacuated"), sem(f"p{L}_split")
                sto = [sem(f"p{L}_stored{i}") for i in range(NB)]
                lnc, lns, lnv = sem(f"p{L}_ln"), sem(f"p{L}_ln_sqrt"), sem(f"p{L}_ln_var")
                ldq, bq4, tr, tre = (sem(f"p{L}_{n}") for n in ("q_loaded", "bq_scaled", "transposed", "xT"))
                chain, vones = sem(f"p{L}_chain"), sem(f"p{L}_v_ones")
                have_stats = ql != 0
                xn_done = (1 if have_stats else 2) * NQT + 7
                kcols, qcols = groups_of(S, 512), groups_of(T, 512)
                jobs = []
                if kl is not None:
                    jobs += [("k", m, kcols) for m in range(KD)]
                    cT = sb(st, f"cT{L}", [P, KD, S])
                    wk, wv = sb(st, f"wk{L}", [P, KD, D]), sb(st, f"wv{L}", [P, KD, D])
                    bk, bvb = sb(st, f"bk{L}", [P, KD]), sb(st, f"bvb{L}", [P, D])
                    ld, ldv = sem(f"p{L}_k_loaded"), sem(f"p{L}_v_loaded")
                    vmm, vev = sem(f"p{L}_v_done"), sem(f"p{L}_v_evacuated")
                if kl == 0:
                    ones_row, zero_row = sb(st, "ones_row", [3, SP_], BF16), sb(st, "zero_row", [1, SP_], BF16)
                    kload, rload, rows_made = sem("p_kstack"), sem("p_kstack_rows"), sem("p_rows_made")
                    x_loaded = sem("x_loaded")
                if kl == 1:
                    VB = 4
                    vout = sb(st, "vout", [P, VB, H, NV])
                    v_sto = [sem(f"p_v_stored{i}") for i in range(VB)]
                if ql is not None:
                    jobs += [("q", m, qcols) for m in range(KD)]
                if ql == 1:
                    vload = sem("p_v_reloaded")
                pieces = [sum(len(x[2]) for x in jobs[:i]) for i in range(len(jobs) + 1)]

                with nc.Block() as block:
                    @block.sync
                    def _(sp):
                        if ql == 0:
                            sp.dma_start(xres[:, :, :], x_d.rearrange("(t p) d -> p t d", p=P)).then_inc(x_loaded, 16)
                        if kl is not None:
                            sp.dma_start(cT[:, :, :], ctxT_d.rearrange("(k p) s -> p k s", p=P)).then_inc(ld, 16)
                            sp.dma_start(wk[:, :, :], W[kl]["WkT"].rearrange("(k p) n -> p k n", p=P)).then_inc(ld, 16)
                            with nc.allow_non_contiguous_dma(reason="bias columns"):
                                sp.dma_start(bk[:, :], W[kl]["bk"].rearrange("(m p) -> p m", p=P)).then_inc(ld, 16)
                            sp.dma_start(wv[:, :, :], W[kl]["WvT"].rearrange("(k p) n -> p k n", p=P)).then_inc(ldv, 16)
                            sp.dma_start(bvb[:, :], W[kl]["bv"].rearrange("(a n) -> a n", a=1).to_broadcast([P, D]))\
                              .then_inc(ldv, 16)
                        if ql == 1:
                            sp.dma_start(Vaug[:, 0:S // P, :, :].rearrange("p j h n -> p j (h n)"),
                                         Vs[0:S // P].rearrange("j p n -> p j n")).then_inc(vload, 16)
                            sp.wait_ge(vones, 1)
                            sp.dma_start(Vaug[0:S % P, S // P, :, :].rearrange("p h n -> p (h n)"),
                                         Vs[S // P, 0:S % P, :]).then_inc(vload, 16)
                        if ql is not None:
                            sp.dma_start(wq[:, :, :], w["WqT"].rearrange("(k p) n -> p k n", p=P)).then_inc(ldq, 16)
                            with nc.allow_non_contiguous_dma(reason="bias columns"):
                                sp.dma_start(bq[:, :], w["bq"].rearrange("(m p) -> p m", p=P)).then_inc(ldq, 16)
                        if kl == 0:
                            sp.wait_ge(rows_made, 2)
                            sp.dma_start(Kst[RB:RB + 1, :, :], zero_row[:, :].unsqueeze(1).to_broadcast([1, H, SP_]))\
                              .then_inc(rload, 16)
                            sp.dma_start(Kst[RM:RM + 3, :, :], ones_row[:, :].unsqueeze(1).to_broadcast([3, H, SP_]))\
                              .then_inc(rload, 16)
                        if kl == 1:
                            for j, (k0, kw) in enumerate(key_tiles()):
                                sp.wait_ge(vev, j + 1)
                                sp.dma_start(Vs[j, 0:kw, :], vout[0:kw, j % VB, :, :].rearrange("p h n -> p (h n)"))\
                                  .then_inc(v_sto[j % VB], 16)
                        for i, (kind, m, _) in enumerate(jobs):
                            dst, n = (Qs, T) if kind == "q" else (Ks[kl], S)
                            sp.wait_ge(spl, i + 1)
                            sp.dma_start(dst[:, m * P:(m + 1) * P, :].rearrange("t p s -> p t s"),
                                         parts[:, i % NB, :, 0:n]).then_inc(sto[i % NB], 16)
                            if kl == 0 and i == 1:
                                for b in range(NB):
                                    sp.wait_ge(sto[b], 16)
                                load_key_stack(sp, 0, Ks, kload)
                        if kl == 1:
                            for b in range(VB):
                                sp.wait_ge(v_sto[b], 16 * len(range(b, NKT, VB)))
                        if kl == 0:
                            sp.wait_ge(kload, 16 * len(PAIRS))
                            sp.wait_ge(rload, 32)
                        if ql == 1:
                            sp.wait_ge(vload, 32)
                        for b in range(NB):
                            sp.wait_ge(sto[b], 16 * (len(jobs) // NB))

                    @block.gpsimd
                    def _(pool):
                        if Vaug is not None:
                            pool.memset(Vaug[:, NKT - 1, :, :], 1.0).then_inc(vones, 1)
                        if kl == 0:
                            pool.memset(Vaug[:, 0:NKT - 1, :, DH:NV], 1.0).then_inc(vones, 1)
                        if kl == 1:
                            pool.memset(vout[:, :, :, DH:NV], 1.0).then_inc(vones, 1)
                        if beside is not None:
                            beside(pool)

                    @block.scalar
                    def _(act):
                        if ql is not None:
                            act.wait_ge(ldq, 32)
                            act.activation(bq[:, :], bq[:, :], ACT.Copy, scale=0.25).then_inc(bq4, 1)
                            act.wait_ge(bq4, 1)
                        if kl is not None:
                            act.wait_ge(ld, 48)
                        for i, (kind, m, cols) in enumerate(jobs):
                            if kind == "q" and m == 0:
                                act.wait_ge(lnv, 1)
                                act.activation(lnw[:, 3, :], lnw[:, 2, :], ACT.Sqrt).then_inc(lns, 1)
                                for b in range(8):
                                    act.wait_ge(tr, b + 1)
                                    k, g = b % 2, b // 2
                                    act.activation(xT[:, k, g * 512:(g + 1) * 512], bank(4 + b % 2)[:, :], ACT.Copy)\
                                       .then_inc(tre, 1)
                            if i >= NB:
                                act.wait_ge(chain, 3 * (i - NB + 1))
                                act.wait_ge(sto[i % NB], 16 * (i // NB))
                            bias, scale = (bq[:, m:m + 1], 0.25) if kind == "q" else (bk[:, m:m + 1], 1.0)
                            for c, (a, n) in enumerate(cols):
                                src = bank((pieces[i] + c) % 4)[:, 0:n]
                                act.wait_ge(mm, pieces[i] + c + 1)
                                act.activation(full[:, i % NB, a:a + n], src, ACT.Identity, bias=bias, scale=scale)
                                act.activation(parts[:, i % NB, 0, a:a + n], src, ACT.Identity, bias=bias, scale=scale)\
                                   .then_inc(ev, 1)

                    @block.tensor
                    def _(pe):
                        def half(i, wgt, src):
                            _, m, cols = jobs[i]
                            for c, (a, cw) in enumerate(cols):
                                n = pieces[i] + c
                                if n >= 4:
                                    pe.wait_ge(ev, n - 3)
                                for k in range(KD):
                                    mmi = pe.matmul(bank(n % 4)[:, 0:cw], wgt[:, k, m * P:(m + 1) * P],
                                                    src[:, k, a:a + cw], start=(k == 0), stop=(k == KD - 1))
                                mmi.then_inc(mm, 1)

                        def values():
                            pe.wait_ge(ldv, 32)
                            for j, (k0, kw) in enumerate(key_tiles()):
                                if j >= 2:
                                    pe.wait_ge(vev, j - 1)
                                for k in range(KD):
                                    mmi = pe.matmul(bank(6 + j % 2)[0:kw, 0:D], cT[:, k, k0:k0 + kw], wv[:, k, :],
                                                    start=(k == 0), stop=(k == KD - 1))
                                mmi.then_inc(vmm, 1)

                        i = 0
                        if kl == 1:
                            pe.wait_ge(ld, 48)
                            values()
                        if kl is not None:
                            pe.wait_ge(ld, 48)
                            for m in range(KD):
                                half(i, wk, cT)
                                i += 1
                        if ql is not None:
                            for b in range(8):
                                k, g = b % 2, b // 2
                                if b >= 2:
                                    pe.wait_ge(tre, b - 1)
                                pe.wait_ge(lnc, xn_done - NQT + 4 * g + 4)
                                for q in range(4):
                                    mmi = pe.transpose(bank(4 + b % 2)[:, q * P:(q + 1) * P],
                                                       xn[:, 4 * g + q, k * P:(k + 1) * P], ident[:, :])
                                mmi.then_inc(tr, 1)
                            pe.wait_ge(tre, 8)
                            pe.wait_ge(ldq, 32)
                            for m in range(KD):
                                half(i, wq, xT)
                                i += 1
                        if kl == 0:
                            values()

                    @block.vector
                    def _(dve):
                        if kl == 0:
                            dve.memset(ones_row[:, :], 1.0).then_inc(rows_made, 1)
                            dve.memset(zero_row[:, :], 0.0).then_inc(rows_made, 1)
                        if ql == 0:
                            dve.wait_ge(x_loaded, 16)
                        if ql is not None:
                            got = norm_vector(dve, xn, lnc, lns, lnv, have_stats)
                            assert got == xn_done, got

                        def split(i):
                            n = 3 * i
                            f, (p0, p1, p2) = full[:, i % NB, 0:width(i)], (parts[:, i % NB, t, 0:width(i)] for t in range(3))
                            dve.wait_ge(ev, pieces[i + 1])
                            dve.tensor_tensor(f, f, p0, ALU.subtract).then_inc(chain, 1)
                            dve.wait_ge(chain, n + 1)
                            dve.tensor_copy(p1, f).then_inc(chain, 1)
                            dve.wait_ge(chain, n + 2)
                            dve.tensor_tensor(p2, f, p1, ALU.subtract).then_inc(chain, 1)
                            dve.wait_ge(chain, n + 3)
                            dve.sem_inc(spl, 1)

                        def width(i):
                            return T if jobs[i][0] == "q" else S

                        def values():
                            dve.wait_ge(ldv, 32)
                            dve.wait_ge(vones, 2 if kl == 0 else 1)
                            for j, (k0, kw) in enumerate(key_tiles()):
                                dve.wait_ge(vmm, j + 1)
                                if kl and j >= VB:
                                    dve.wait_ge(v_sto[j % VB], 16 * (j // VB))
                                dst = vout[0:kw, j % VB, :, 0:DH] if kl else Vaug[0:kw, j, :, 0:DH]
                                dve.tensor_tensor(dst, bank(6 + j % 2)[0:kw, 0:D].rearrange("p (h d) -> p h d", h=H),
                                                  bvb[0:kw, :].rearrange("p (h d) -> p h d", h=H), ALU.add)\
                                   .then_inc(vev, 1)

                        if kl == 1:
                            values()
                        for i in range(len(jobs)):
                            split(i)
                        if kl == 0:
                            values()

        def attention(st, causal, masked, first, Vaug, OT, live, Qs, tag, more=None):
            tiles = key_tiles(first)
            nt = len(tiles)

            def seen(i):
                return min(i + 1, nt) if causal else nt

            def max_pieces(s):
                out = []
                for q in range(QTC):
                    i = s * QTC + q
                    for n, (j0, m) in enumerate(groups_of(seen(i), 4)):
                        w = sum(t[1] for t in tiles[j0:j0 + m])
                        diag = (i - j0) * P if causal and j0 <= i < j0 + m else None
                        out.append((q, n, tiles[j0][0], w, diag))
                return out

            def first_column(s, j):
                return max(0, j - s * QTC) * P if causal else 0

            PIECES = [max_pieces(s) for s in range(NC)]
            assert all(len(x) % QTC == 0 and max(y[1] for y in x) == len(x) // QTC - 1 for x in PIECES)
            TILES = [seen(s * QTC + QTC - 1) for s in range(NC)]
            piece0 = [H * sum(len(PIECES[z]) for z in range(s)) for s in range(NC + 1)]
            pack0 = [H // 2 * sum(TILES[:s]) for s in range(NC + 1)]
            NG = H // G
            NI = NG // 2

            QB = 2 if masked else 3
            Qst = sb(st, f"Qst{tag}", [P, QB, H * QC], BF16)
            Pt = sb(st, f"Pt{tag}", [P, SLOTS, 2, QC])
            Vg = sb(st, f"Vg{tag}", [P, 2, nt, G, NV])
            mxp = sb(st, f"mxp{tag}", [P, QTC, H, 4])
            mx = sb(st, f"mx{tag}", [P, QTC, H])
            HH = 2 * G
            mparts = sb(st, f"mparts{tag}", [P, QTC, 3, HH], BF16)
            mT = sb(st, f"mT{tag}", [3 * HH, 2 * QC], BF16)
            Kf = Kst[:, :, :].rearrange("p h s -> p (h s)")
            if masked:
                mrow = sb(st, f"mrow{tag}", [P, QTC, S], BF16)
                mcol = sb(st, f"mcol{tag}", [P, nt, QC], BF16)
                mi = sb(st, f"mi{tag}", [P, 2, QC], I32)
                mask_ld = [sem(f"a{tag}_mask_loaded{i}") for i in range(2)]
                mask_mk = sem(f"a{tag}_mask_made")
            ones_q = sb(st, f"ones_q{tag}", [1, P // 2], BF16)
            o_zero, q_ones, ones_made = sem(f"a{tag}_out_zeroed"), sem(f"a{tag}_q_ones"), sem(f"a{tag}_ones_made")
            q_ld = [sem(f"a{tag}_q_loaded{s}") for s in range(NC)]
            a_done, a_free = sem(f"a{tag}_max_scores"), sem(f"a{tag}_max_taken")
            m_spl, m_tr, m_sb = (sem(f"a{tag}_max_{n}") for n in ("split", "transposed", "on_sbuf"))
            m_ld = [sem(f"a{tag}_max_stacked{s}") for s in range(NC)]
            vg = sem(f"a{tag}_group_values")
            sc, pr, pv = (sem(f"a{tag}_{n}") for n in ("scores", "probs", "values"))
            o_free = sem(f"a{tag}_out_read")
            chain = sem(f"a{tag}_chain")

            row_cuts = groups_of(S, QC)
            NROW, NCOL = QTC * len(row_cuts), nt

            def mask_made(rows, cols):
                return NROW * rows + NCOL * cols

            def sync(sp):
                def load_q(s):
                    for b, (qp, _) in enumerate(PAIRS):
                        sp.dma_start(
                            Qst[b * DH:(b + 1) * DH, s % QB, :].rearrange("p (h t) -> p h t", h=H),
                            Qs[qp].rearrange("(h d) t -> d h t", d=DH)[:, :, s * QC:(s + 1) * QC])\
                            .then_inc(q_ld[s], 16)
                sp.wait_ge(ones_made, 1)
                sp.dma_start(Qst[RB:RB + 1, :, :].rearrange("p q (h t) -> p (q h) t", t=P // 2),
                             ones_q[:, :].unsqueeze(1).to_broadcast([1, QB * H * QTC * 2, P // 2])).then_inc(q_ones, 16)
                for s in range(QB):
                    load_q(s)
                for s in range(NC):
                    for half in range(NI):
                        sp.wait_ge(m_sb, NI * s + half + 2)
                        if half:
                            sp.wait_ge(m_ld[s], 48)
                        for n in range(3):
                            sp.dma_start(
                                Qst[RM + n:RM + n + 1, s % QB, half * HH * QC:(half + 1) * HH * QC]
                                .rearrange("p (h t) -> p h t", h=HH),
                                mT[n * HH:(n + 1) * HH, (1 - half) * QC:(2 - half) * QC]).then_inc(m_ld[s], 16)
                        if half == 0 and QB <= s + 1 < NC:
                            sp.wait_ge(pv, 1 + pack0[s + 2 - QB])
                            load_q(s + 1)
                        if half and more is not None:
                            more(sp, s)

            def gpsimd(pool):
                pool.memset(ones_q[:, :], 1.0).then_inc(ones_made, 1)

                def mask_pieces(pieces, made):
                    def load(i):
                        src, _ = pieces[i]
                        pool.dma_start(mi[0:src.shape[0], i % 2, 0:src.shape[1]], src)\
                            .then_inc(mask_ld[(made + i) % 2], 16)
                    load(0)
                    load(1)
                    for i, (src, dst) in enumerate(pieces):
                        n = made + i
                        pool.wait_ge(mask_ld[n % 2], 16 * (n // 2 + 1))
                        pool.tensor_scalar(dst, mi[0:src.shape[0], i % 2, 0:src.shape[1]], 0, MASKED,
                                           ALU.is_equal, ALU.mult).then_inc(mask_mk, 1)
                        pool.wait_ge(mask_mk, n + 1)
                        if i + 2 < len(pieces):
                            load(i + 2)

                for stage in range(NC + 1):
                    a, s = stage, stage - 1
                    if masked and a < NC:
                        if a:
                            pool.wait_ge(a_done, piece0[a])
                        mask_pieces([(mask_d[(a * QTC + q) * P:(a * QTC + q + 1) * P, c0:c0 + cw],
                                      mrow[:, q, c0:c0 + cw]) for q in range(QTC) for c0, cw in row_cuts],
                                    mask_made(a, max(a - 1, 0)))
                    if s < 0:
                        continue
                    if masked:
                        if s:
                            pool.wait_ge(pv, 1 + pack0[s])
                        mask_pieces([(maskT_d[k0:k0 + kw, s * QC:(s + 1) * QC], mcol[0:kw, j, :])
                                     for j, (k0, kw) in enumerate(tiles)], mask_made(min(s + 2, NC), s))
                    with pool.Fori(0, NI) as it:
                        for z in range(2):
                            before = pack0[s] - 2 * TILES[s - 1] * (1 - z) if s else 0
                            here = pack0[s] + 2 * TILES[s] * (z + 1)
                            pool.wait_ge(pv, it * (here - before) + (before + 1))
                            pool.tensor_copy(Vg[:, z, :, :, :],
                                             Vaug[:, first:NKT, bass.ds(it * (2 * G) + z * G, G), :]).then_inc(vg, 1)

            def tensor(pe):
                pe.sem_inc(pv, 1)
                pe.sem_inc(m_tr, 1)
                pe.wait_ge(q_ones, 16)
                def max_piece(s, it, u, n):
                    q, pc, k0, w, diag = PIECES[s][n]
                    np_ = len(PIECES[s])
                    g = piece0[s] + u * np_ + n
                    total, local = 2 * G * np_, u * np_ + n
                    back = AB if local >= AB else local + total - max(m for m in range(total) if m % AB == local % AB)
                    pe.wait_ge(a_free, it * total + (g - back + AB + 2))
                    if local == AB - 1:
                        pe.wait_ge(m_sb, it + (NI * s + 1))
                    h = it * (2 * G) + u
                    ab = local % AB
                    out = psA[:, ab, 0:w]
                    mmi = pe.matmul(out, Qst[0:KA, s % QB, bass.ds(h * QC + q * P, P)],
                                    Kf[0:KA, bass.ds(h * SP_ + k0, w)], start=True,
                                    stop=diag is None and not masked)
                    if diag is not None:
                        dw = min(P, w - diag)
                        mmi = pe.matmul(psA[:, ab, diag:diag + dw], identb[:, :], causb[:, 0:dw],
                                        start=False, stop=True)
                    if masked:
                        mmi = pe.matmul(out, identb[:, :], mrow[:, q, k0:k0 + w], start=False, stop=True)
                    mmi.then_inc(a_done, 1)

                def score_pack(s, it, z, j, b):
                    k0, kw = tiles[j]
                    col = first_column(s, j)
                    n = pack0[s] + (z * TILES[s] + j) * 2 + b
                    pe.wait_ge(pr, it * (4 * TILES[s]) + (n + 1))
                    for y in range(2):
                        h = it * (2 * G) + (z * G + 2 * b + y)
                        mmi = pe.matmul(psC[0:kw, n % 2, y * 512 + col:y * 512 + QC],
                                        Kf[0:KC, bass.ds(h * SP_ + k0, kw)],
                                        Qst[0:KC, s % QB, bass.ds(h * QC + col, QC - col)],
                                        start=True, stop=not (masked or (causal and j >= s * QTC)))
                        if masked:
                            mmi = pe.matmul(psC[0:kw, n % 2, y * 512:y * 512 + QC], identb[0:kw, 0:kw],
                                            mcol[0:kw, j, :], start=False, stop=True)
                        elif causal and j >= s * QTC:
                            mmi = pe.matmul(psC[0:kw, n % 2, y * 512 + col:y * 512 + col + P],
                                            identb[0:kw, 0:kw], causbT[0:kw, :], start=False, stop=True)
                    mmi.then_inc(sc, 1)

                def value_pack(s, it, z, j, b):
                    kw = tiles[j][1]
                    col = first_column(s, j)
                    n = pack0[s] + (z * TILES[s] + j) * 2 + b
                    if j == 0 and b == 0:
                        pe.wait_ge(o_free, it * 2 + (s * NG + z + 1))
                        pe.wait_ge(vg, it * 2 + (s * NG + z + 1))
                    pe.wait_ge(pr, it * (4 * TILES[s]) + (n + 3))
                    for y in range(2):
                        u = 2 * b + y
                        mmi = pe.matmul(psO[32 * u:32 * u + NV, col:QC], Vg[0:kw, z, j, u, :],
                                        Pt[0:kw, n % SLOTS, y, col:QC],
                                        start=(j == 0), stop=(j == TILES[s] - 1),
                                        skip_group_check=True)
                    mmi.then_inc(pv, 1)

                def turn_maxima(stage, it):
                    pe.wait_ge(m_spl, it + NI * stage)
                    for q in range(QTC):
                        mmi = pe.transpose(psA[:, AB - 1, :].bitcast(BF16)[0:3 * HH, q * P:(q + 1) * P],
                                           mparts[:, q, :, :].rearrange("p a h -> p (a h)"), identb[:, :])
                    mmi.then_inc(m_tr, 1)

                for stage in range(NC + 1):
                    a, c = stage, stage - 1
                    if a < NC:
                        pe.wait_ge(q_ld[a], 16 * len(PAIRS))
                        if masked:
                            pe.wait_ge(mask_mk, mask_made(a + 1, max(a - 1, 0)))
                    if c >= 0:
                        if c == 0:
                            pe.wait_ge(o_zero, 1)
                        if masked:
                            pe.wait_ge(mask_mk, mask_made(min(c + 2, NC), c + 1))
                    with pe.Fori(0, NI) as it:
                        na = 2 * G * len(PIECES[a]) if a < NC else 0
                        steps = []
                        if c >= 0:
                            order = [(z, j, b) for z in range(2) for j in range(TILES[c]) for b in range(2)]
                            for i in range(len(order) + LAG):
                                if i < len(order):
                                    steps.append((score_pack, order[i]))
                                if i >= LAG:
                                    steps.append((value_pack, order[i - LAG]))
                        if c >= 0:
                            pe.wait_ge(m_ld[c], it * 48 + 48)
                        done = 0
                        for i, (step, where) in enumerate(steps):
                            step(c, it, *where)
                            if i == 1:
                                if c < NC - 1:
                                    turn_maxima(stage, it)
                                else:
                                    with pe.If(it < 1):
                                        turn_maxima(stage, it)
                            if i >= 1:
                                to = na * (i + 1) // len(steps)
                                for n in range(done, to):
                                    max_piece(a, it, n // len(PIECES[a]), n % len(PIECES[a]))
                                done = to
                        if not steps:
                            with pe.If(it > 0):
                                turn_maxima(stage, it)
                        for n in range(done, na):
                            max_piece(a, it, n // len(PIECES[a]), n % len(PIECES[a]))

            def scalar(act):
                act.sem_inc(pr, 2)
                act.sem_inc(o_free, 1)
                act.sem_inc(m_sb, 1)

                def maxima_out(stage, it):
                    act.wait_ge(m_tr, it + (NI * stage + 1))
                    act.activation(mT[:, bass.ds(it * QC, QC)], psA[:, AB - 1, :].bitcast(BF16)[0:3 * HH, 0:QC], ACT.Copy)\
                       .then_inc(m_sb, 1)

                for stage in range(NC + 1):
                    a, c = stage, stage - 1

                    def read_out(it, z):
                        act.wait_ge(pv, it * (4 * TILES[c]) + (pack0[c] + 2 * TILES[c] * (z + 1) + 1))
                        act.activation(OT[:, bass.ds(it * (2 * T) + (z * T + c * QC), QC)],
                                       psO[:, :], ACT.Copy).then_inc(o_free, 1)

                    with act.Fori(0, NI) as it:
                        if c < 0:
                            with act.If(it > 0):
                                maxima_out(stage, it)
                        else:
                            for z in range(2):
                                for j in range(TILES[c]):
                                    kw = tiles[j][1]
                                    col = first_column(c, j)
                                    for b in range(2):
                                        n = pack0[c] + (z * TILES[c] + j) * 2 + b
                                        act.wait_ge(sc, it * (4 * TILES[c]) + (n + 1))
                                        if n >= SLOTS:
                                            act.wait_ge(pv, it * (4 * TILES[c]) + (n + 2 - SLOTS))
                                        act.activation(
                                            Pt[0:kw, n % SLOTS, :, col:QC],
                                            psC[0:kw, n % 2, :].rearrange("p (y t) -> p y t", y=2)[:, :, col:QC],
                                            ACT.Exp).then_inc(pr, 1)
                                        if z == 0 and j == 0 and b == 0:
                                            if c < NC - 1:
                                                maxima_out(stage, it)
                                            else:
                                                with act.If(it < 1):
                                                    maxima_out(stage, it)
                                    if z == 1 and j == 0:
                                        read_out(it, 0)
                            read_out(it, 1)

            def vector(dve):
                dve.memset(psO[:, :], 0.0).then_inc(o_zero, 1)
                dve.sem_inc(a_free, AB + 1)
                mxf = mxp[:, :, :, :].rearrange("p q h n -> p (q h n)")
                for s in range(NC):
                    np_ = len(PIECES[s])
                    with dve.Fori(0, NI) as it:
                        for u in range(2 * G):
                            for i, (q, pc, k0, w, diag) in enumerate(PIECES[s]):
                                g = piece0[s] + u * np_ + i
                                dve.wait_ge(a_done, it * (2 * G * np_) + (g + 1))
                                dve.tensor_reduce(mxf[:, bass.ds(it * (2 * G * 4) + ((q * H + u) * 4 + pc), 1)],
                                                  psA[:, (u * np_ + i) % AB, 0:w], AX.X, ALU.max).then_inc(a_free, 1)
                        heads = bass.ds(it * HH, HH)
                        per_tile = np_ // QTC
                        links = 5 if live is None else 6
                        n = [0]

                        def link(ins):
                            n[0] += 1
                            ins.then_inc(chain, 1)
                            dve.wait_ge(chain, it * links + (s * NI * links + n[0]))

                        dve.wait_ge(a_free, it * (HH * np_) + (AB + 1 + piece0[s] + HH * np_))
                        dve.wait_ge(m_tr, it + (NI * s + 1))
                        m = mx[:, :, heads]
                        link(dve.tensor_reduce(m, mxp[:, :, heads, 0:per_tile], AX.X, ALU.max))
                        if live is not None:
                            link(dve.tensor_scalar(live[:, s * QTC:(s + 1) * QTC, heads], m, DEAD, None, ALU.is_ge))
                        link(dve.tensor_scalar(mparts[:, :, 0, :], m, -1.0, None, ALU.mult))
                        link(dve.scalar_tensor_tensor(out=m, in0=m, scalar=-1.0,
                                                      in1=mparts[:, :, 0, :], op0=ALU.mult, op1=ALU.subtract))
                        link(dve.tensor_scalar(mparts[:, :, 1, :], m, 1.0, None, ALU.mult))
                        link(dve.tensor_tensor(mparts[:, :, 2, :], m, mparts[:, :, 1, :], ALU.subtract))
                        assert n[0] == links
                        dve.sem_inc(m_spl, 1)

            return sync, gpsimd, tensor, scalar, vector

        def output_projection(L, OT, live):
            NG = H // G
            with ExitStack() as st:
                w = W[L]
                att = sb(st, f"att{L}", [P, NQT, D])
                rden = sb(st, f"rden{L}", [P, NC * NG, QTC, G])
                wo = sb(st, f"wo{L}", [P, KD, D])
                bob = sb(st, f"bob{L}", [P, D])
                aT = sb(st, f"aT{L}", [P, 2, KD, QC])
                ld, chain, att_s, bias_s = sem(f"o{L}_loaded"), sem(f"o{L}_chain"), sem(f"o{L}_att"), sem(f"o{L}_bias")
                ot, rd, stat = sem(f"o{L}_out_transposed"), sem(f"o{L}_sum_inverse"), sem(f"o{L}_stats")
                tr, tre, mm, up = (sem(f"o{L}_{n}") for n in ("transposed", "aT", "done", "residual"))
                with nc.Block() as block:
                    @block.sync
                    def _(sp):
                        sp.dma_start(wo[:, :, :], w["WoT"].rearrange("(k p) n -> p k n", p=P)).then_inc(ld, 16)
                        sp.dma_start(bob[:, :], w["bo"].rearrange("(a n) -> a n", a=1).to_broadcast([P, D]))\
                          .then_inc(ld, 16)

                    @block.gpsimd
                    def _(pool):
                        pool.wait_ge(ld, 32)
                        pool.tensor_scalar(bob[:, :], bob[:, :], gates[:, L:L + 1], 0.0, ALU.mult, ALU.add).then_inc(bias_s, 1)
                        pool.wait_ge(bias_s, 1)
                        for g in range(NC):
                            v = xres[:, g * QTC:(g + 1) * QTC, :]
                            pool.tensor_tensor(v, v, bob[:, :].unsqueeze(1).to_broadcast([P, QTC, D]), ALU.add).then_inc(bias_s, 1)

                    @block.vector
                    def _(dve):
                        def residual(g):
                            for i in (2 * g, 2 * g + 1):
                                dve.wait_ge(mm, i + 1)
                                v = xres[:, 2 * i:2 * i + 2, :].rearrange("p q d -> p (q d)")
                                dve.scalar_tensor_tensor(out=v, in0=bank(4 + i % 4), scalar=gates[:, L:L + 1], in1=v,
                                                         op0=ALU.mult, op1=ALU.add).then_inc(up, 1)
                                dve.wait_ge(up, i + 1)
                                for t in (2 * i, 2 * i + 1):
                                    dve.bn_stats(stats[:, t, :], xres[:, t, :]).then_inc(stat, 1)
                        nrd = 0
                        for c in range(NC):
                            for g in range(NG):
                                i = c * NG + g
                                dve.wait_ge(ot, i + 1)
                                o = bank(i % 2).rearrange("p (q u n) -> p q u n", q=QTC, u=G)
                                r = rden[:, i, :, :]
                                if live is not None:
                                    lv = live[:, c * QTC:(c + 1) * QTC, g * G:(g + 1) * G]
                                    dve.tensor_tensor(r, o[:, :, :, DH], lv, ALU.mult).then_inc(rd, 1)
                                    nrd += 1
                                    dve.wait_ge(rd, nrd)
                                    dve.reciprocal(r, r).then_inc(rd, 1)
                                    nrd += 1
                                    dve.wait_ge(rd, nrd)
                                    dve.tensor_tensor(r, r, lv, ALU.mult).then_inc(rd, 1)
                                else:
                                    dve.reciprocal(r, o[:, :, :, DH]).then_inc(rd, 1)
                                nrd += 1
                                dve.wait_ge(rd, nrd)
                                for q in range(QTC):
                                    last = dve.tensor_tensor(
                                        att[:, c * QTC + q, g * G * DH:(g + 1) * G * DH].rearrange("p (u d) -> p u d", u=G),
                                        o[:, q, :, 0:DH], r[:, q, :].unsqueeze(2).to_broadcast([P, G, DH]), ALU.mult)
                                last.then_inc(att_s, 1)
                            if c == 1:
                                dve.wait_ge(bias_s, 1 + NC)
                            if c:
                                residual(c - 1)
                        residual(NC - 1)

                    @block.scalar
                    def _(act):
                        for g in range(NC):
                            for k in range(KD):
                                act.wait_ge(tr, 2 * g + k + 1)
                                if g >= 2:
                                    act.wait_ge(mm, 2 * (g - 1))
                                act.activation(aT[:, g % 2, k, :], bank(2 + k)[:, :], ACT.Copy).then_inc(tre, 1)

                    @block.tensor
                    def _(pe):
                        def heads_back(c):
                            for g in range(NG):
                                i = c * NG + g
                                if i >= 2:
                                    pe.wait_ge(att_s, i - 1)
                                for q in range(QTC):
                                    at = g * T + (c * QTC + q) * P
                                    mmi = pe.transpose(bank(i % 2)[:, q * P:(q + 1) * P], OT[:, at:at + P], ident[:, :])
                                mmi.then_inc(ot, 1)

                        heads_back(0)
                        for g in range(NC):
                            if g + 1 < NC:
                                heads_back(g + 1)
                            pe.wait_ge(att_s, NG * (g + 1))
                            for k in range(KD):
                                if g:
                                    pe.wait_ge(tre, 2 * (g - 1) + k + 1)
                                for q in range(QTC):
                                    mmi = pe.transpose(bank(2 + k)[:, q * P:(q + 1) * P],
                                                       att[:, g * QTC + q, k * P:(k + 1) * P], ident[:, :])
                                mmi.then_inc(tr, 1)
                            pe.wait_ge(tre, 2 * (g + 1))
                            if g == 0:
                                pe.wait_ge(ld, 32)
                            for half in range(2):
                                i = 2 * g + half
                                if i >= 4:
                                    pe.wait_ge(up, i - 3)
                                for z in range(2):
                                    q = 2 * half + z
                                    for k in range(KD):
                                        mmi = pe.matmul(bank(4 + i % 4)[:, z * D:(z + 1) * D],
                                                        aT[:, g % 2, k, q * P:(q + 1) * P], wo[:, k, :],
                                                        start=(k == 0), stop=(k == KD - 1))
                                mmi.then_inc(mm, 1)

        def summarise_mask(st):
            k0 = TAIL * P
            cuts = [(c, min(512, k0 - c)) for c in range(0, k0, 512)] + [(k0, S - k0)]
            tail = len(cuts) - 1
            assert tail < 6 and S - k0 <= 512
            onesb = sb(st, "onesb", [P, P], BF16)
            some = sb(st, "some", [P, tail + 1])
            part = sb(st, "part", [P, 2, S - k0])
            bias = sb(st, "bias", [P, S - k0], BF16)
            made, summed, chain = sem("m_ones"), sem("m_summed"), sem("m_chain")
            def gpsimd(pool):
                pool.memset(onesb[:, :], 1.0).then_inc(made, 1)

            def tensor(pe):
                pe.wait_ge(made, 1)
                for i, (c0, cw) in enumerate(cuts):
                    pe.matmul(bank(i)[:, 0:cw], onesb[:, :], ignored[:, c0:c0 + cw], start=True, stop=True)\
                      .then_inc(summed, 1)

            def vector(dve):
                n = [0]

                def link(ins):
                    n[0] += 1
                    ins.then_inc(chain, 1)
                    dve.wait_ge(chain, n[0])

                dve.wait_ge(summed, tail + 1)
                for i, (c0, cw) in enumerate(cuts[:tail]):
                    link(dve.tensor_reduce(some[:, i:i + 1], bank(i)[:, 0:cw], AX.X, ALU.min))
                link(dve.tensor_scalar(some[:, 0:tail], some[:, 0:tail], -1.0, float(T), ALU.mult, ALU.add))
                last = bank(tail)[:, 0:S - k0]
                link(dve.tensor_scalar(part[:, 0, :], last, -1.0, float(T), ALU.mult, ALU.add))
                link(dve.tensor_tensor(part[:, 1, :], part[:, 0, :], last, ALU.mult))
                link(dve.tensor_reduce(some[:, tail:tail + 1], part[:, 1, :], AX.X, ALU.max))
                link(dve.tensor_reduce(part[:, 0, 0:1], some[:, :], AX.X, ALU.max))
                link(dve.tensor_scalar(tail_only[:, :], part[:, 0, 0:1], 0.0, None, ALU.is_equal))
                link(dve.tensor_scalar(bias[:, :], last, float(T), MASKED, ALU.is_equal, ALU.mult))
                link(dve.tensor_copy(Kst[RB:RB + 1, :, k0:S],
                                     bias[RB:RB + 1, :].unsqueeze(1).to_broadcast([1, H, S - k0])))

            return gpsimd, tensor, vector

        def attention_layer(L):
            with ExitStack() as st:
                Vaug = sb(st, f"Vaug{L}", [P, NKT, H, NV])
                Qs = scratch(f"q_parts{L}", [3, D, T], BF16)
                if L == 0:
                    projections("0", 0, 0, Vaug, Qs)
                else:
                    projections("1", 1, None, Vaug, Qs)
                OT = sb(st, f"OT{L}", [P, H // G * T])
                live = sb(st, f"live{L}", [P, NQT, H]) if L else None
                if L == 0:
                    with ExitStack() as at:
                        sync, gpsimd, tensor, scalar, vector = attention(at, True, False, 0, Vaug, OT, None, Qs, "0",
                                                                          zero_rows)
                        with nc.Block() as block:
                            block.sync(sync)
                            block.gpsimd(gpsimd)
                            block.tensor(tensor)
                            block.scalar(scalar)
                            block.vector(vector)
                else:
                    with ExitStack() as at:
                        tail = attention(at, False, False, TAIL, Vaug, OT, live, Qs, "t")
                    with ExitStack() as at:
                        every = attention(at, False, True, 0, Vaug, OT, live, Qs, "g")

                        def either(i):
                            def program(eng):
                                flag = eng.value_load(tail_only[0:1, 0:1], min_val=0, max_val=1)
                                with eng.If(flag > 0):
                                    tail[i](eng)
                                with eng.Else():
                                    every[i](eng)
                            return program
                        with nc.Block() as block:
                            block.sync(either(0))
                            block.gpsimd(either(1))
                            block.tensor(either(2))
                            block.scalar(either(3))
                            block.vector(either(4))
                output_projection(L, OT, live)

        def load_expert(queue, e, w1, w2, w_ld):
            z = e % 2
            queue.dma_start(w1[:, z, :, :], F["w1"][e].rearrange("(k p) n -> p k n", p=P)).then_inc(w_ld, 16)
            nf = F0 // P
            queue.dma_start(w2[:, z * nf * D:(z + 1) * nf * D].rearrange("p (k n) -> p k n", k=nf),
                            F["w2"][e].rearrange("(k p) n -> p k n", p=P)).then_inc(w_ld, 16)

        def route(L, E, wr_d, rb_d, xn, xT, gate, slot, xs, places):
            with ExitStack() as st:
                wr = sb(st, f"wr{L}", [P, KD, E])
                rb = sb(st, f"rb{L}", [P, E])
                lg = sb(st, f"lg{L}", [P, NQT, E])
                v8 = sb(st, f"v8{L}", [P, NQT, 8])
                i8 = sb(st, f"i8{L}", [P, NQT, 8], U32)
                idx = sb(st, f"idx{L}", [P, 2, NQT])
                small = sb(st, f"small{L}", [P, 6, NQT])
                ex = sb(st, f"ex{L}", [P, NQT, E])
                iota_i = sb(st, f"iota_i{L}", [P, E, NQT], I32)
                iota_e = sb(st, f"iota_e{L}", [P, E, NQT])
                again = sb(st, f"again{L}", [P, E, NQT])
                hot = sb(st, f"hot{L}", [P, 2, E, NQT])
                both = sb(st, f"both{L}", [P, E, NQT])
                upto = sb(st, f"upto{L}", [P, E, NQT])
                below = sb(st, f"below{L}", [P, E, NQT])
                row = sb(st, f"row{L}", [P, E, NQT])
                pick = sb(st, f"pick{L}", [P, E, NQT])
                srow = sb(st, f"srow{L}", [P, 2, NQT])
                lower = sb(st, f"lower{L}", [P, P])
                ones = sb(st, f"ones{L}", [P, P])
                ld = sem(f"r{L}_loaded")
                lnc, lns, lnv = sem(f"r{L}_ln"), sem(f"r{L}_ln_sqrt"), sem(f"r{L}_ln_var")
                tr, tre, lgt, pos = (sem(f"r{L}_{n}") for n in ("transposed", "xT", "logits", "positions"))
                chain, exps, exin, cst, csts = (sem(f"r{L}_{n}") for n in ("chain", "exp", "exp_in", "const", "const_steps"))
                slots_s, scat, sums_in = sem(f"r{L}_slots"), sem(f"r{L}_scattered"), sem(f"r{L}_counted")

                def scatter(pool):
                    for t in range(NQT):
                        for k in range(2):
                            pool.indirect_dma_start(
                                xs[:, :], bass.IndirectOffsetOnAxis(ap=slot[:, k, t:t + 1], axis=0),
                                xn[:, t, :], None, bounds_check=ROWS - 1, oob_is_err=False).then_inc(scat, 16)

                xn_done = NQT + 7
                with nc.Block() as block:
                    @block.sync
                    def _(sp):
                        sp.dma_start(wr[:, :, :], wr_d.rearrange("(k p) n -> p k n", p=P)).then_inc(ld, 16)
                        if rb_d is not None:
                            sp.dma_start(rb[:, :], rb_d.rearrange("(a n) -> a n", a=1).to_broadcast([P, E])).then_inc(ld, 16)
                        places["loads"](sp)

                    @block.gpsimd
                    def _(pool):
                        places["weights"](pool, 0)
                        pool.iota(iota_i[:, :, :], [[1, E], [0, NQT]], base=0, channel_multiplier=0).then_inc(cst, 1)
                        pool.memset(again[:, :, :], 1.0).then_inc(csts, 1)
                        pool.memset(lower[:, :], 1.0).then_inc(csts, 1)
                        pool.wait_ge(csts, 2)
                        pool.memset(again[:, :, 0:1], 0.0).then_inc(cst, 1)
                        pool.memset(ones[:, :], 1.0).then_inc(cst, 1)
                        pool.affine_select(out=lower[:, :], in_=lower[:, :], compare_op=ALU.is_ge, fill=0.0,
                                           base=-1, pattern=[[1, P]], channel_multiplier=-1).then_inc(cst, 1)
                        if L == 0:
                            places["consts"](pool, cst)
                        pool.wait_ge(slots_s, 1)
                        pool.wait_ge(zeroed, 48 * NC)

                    @block.scalar
                    def _(act):
                        act.wait_ge(lnv, 1)
                        act.activation(lnw[:, 3, :], lnw[:, 2, :], ACT.Sqrt).then_inc(lns, 1)
                        for i in range(8):
                            act.wait_ge(tr, i + 1)
                            k, g = i % 2, i // 2
                            act.activation(xT[:, k, g * 512:(g + 1) * 512], bank(i % 2)[:, :], ACT.Copy)\
                               .then_inc(tre, 1)
                        act.wait_ge(exin, 1)
                        if L == 0:
                            act.activation(small[:, 1, :], small[:, 0, :], ACT.Exp).then_inc(exps, 1)
                        else:
                            act.activation(ex[:, :, :], ex[:, :, :], ACT.Exp).then_inc(exps, 1)
                            act.activation(small[:, 1, :], small[:, 0, :], ACT.Exp).then_inc(exps, 1)

                    @block.tensor
                    def _(pe):
                        for i in range(8):
                            k, g = i % 2, i // 2
                            if i >= 2:
                                pe.wait_ge(tre, i - 1)
                            pe.wait_ge(lnc, xn_done - NQT + 4 * g + 4)
                            for q in range(4):
                                mmi = pe.transpose(bank(i % 2)[:, q * P:(q + 1) * P],
                                                   xn[:, 4 * g + q, k * P:(k + 1) * P], ident[:, :])
                            mmi.then_inc(tr, 1)
                        pe.wait_ge(ld, 16 if rb_d is None else 32)
                        pe.wait_ge(tre, 8)
                        for t in range(NQT):
                            for k in range(KD):
                                mmi = pe.matmul(bank(2)[:, t * E:(t + 1) * E], xT[:, k, t * P:(t + 1) * P], wr[:, k, :],
                                                start=(k == 0), stop=(k == KD - 1))
                        mmi.then_inc(lgt, 1)
                        pe.wait_ge(sums_in, 1)
                        pe.wait_ge(cst, 4)
                        pe.matmul(bank(3)[:, 0:E * NQT], lower[:, :], both[:, :, :].rearrange("p e t -> p (e t)"),
                                  start=True, stop=False)
                        pe.matmul(bank(3)[:, 0:E * NQT], ones[:, :], below[:, :, :].rearrange("p e t -> p (e t)"),
                                  start=False, stop=True)
                        pe.matmul(bank(4)[:, 0:E], ones[:, :], upto[:, :, NQT - 1], start=True, stop=True)\
                          .then_inc(pos, 1)

                    @block.vector
                    def _(dve):
                        got = norm_vector(dve, xn, lnc, lns, lnv, have_stats=True)
                        assert got == xn_done, got
                        n = [0]

                        def link(ins):
                            n[0] += 1
                            ins.then_inc(chain, 1)
                            dve.wait_ge(chain, n[0])

                        dve.wait_ge(lgt, 1)
                        logits = bank(2)[:, 0:NQT * E].rearrange("p (t e) -> p t e", e=E)
                        if rb_d is None:
                            link(dve.tensor_copy(lg[:, :, :], logits))
                        else:
                            dve.wait_ge(ld, 32)
                            link(dve.tensor_tensor(lg[:, :, :], logits, rb[:, :].unsqueeze(1).to_broadcast([P, NQT, E]), ALU.add))
                        for t in range(NQT):
                            dve.max(v8[:, t, :], lg[:, t, :]).then_inc(chain, 1)
                        n[0] += NQT
                        dve.wait_ge(chain, n[0])
                        for t in range(NQT):
                            dve.max_index(i8[:, t, :], v8[:, t, :], lg[:, t, :]).then_inc(chain, 1)
                        n[0] += NQT
                        dve.wait_ge(chain, n[0])
                        d, e2, s1, s2, r, w = (small[:, i, :] for i in range(6))
                        if L:
                            link(dve.tensor_tensor(ex[:, :, :], lg[:, :, :], v8[:, :, 0:1].to_broadcast([P, NQT, E]), ALU.subtract))
                        link(dve.tensor_tensor(d, v8[:, :, 1], v8[:, :, 0], ALU.subtract))
                        dve.sem_inc(exin, 1)
                        for k in range(2):
                            link(dve.tensor_copy(idx[:, k, :], i8[:, :, k]))
                        dve.wait_ge(cst, 2)
                        link(dve.tensor_copy(iota_e[:, :, :], iota_i[:, :, :]))
                        for k in range(2):
                            link(dve.tensor_tensor(hot[:, k, :, :], iota_e[:, :, :],
                                                   idx[:, k, :].unsqueeze(1).to_broadcast([P, E, NQT]), ALU.is_equal))
                        link(dve.tensor_tensor(both[:, :, :], hot[:, 0, :, :], hot[:, 1, :, :], ALU.add))
                        flat = lambda x: x[:, :, :].rearrange("p e t -> p (e t)")
                        link(dve.tensor_tensor_scan(flat(upto), flat(again), flat(both), 0.0, ALU.mult, ALU.add))
                        link(dve.tensor_tensor(below[:, :, :], upto[:, :, :], both[:, :, :], ALU.subtract))
                        dve.sem_inc(sums_in, 1)
                        if L == 0:
                            dve.wait_ge(exps, 1)
                            link(dve.tensor_scalar(s1, e2, 1.0, None, ALU.add))
                            link(dve.reciprocal(gate[:, 0, :], s1))
                            link(dve.tensor_tensor(gate[:, 1, :], gate[:, 0, :], e2, ALU.mult))
                        else:
                            dve.wait_ge(exps, 2)
                            link(dve.tensor_reduce(s1, ex[:, :, :], AX.X, ALU.add))
                            link(dve.reciprocal(s2, s1))
                            link(dve.tensor_tensor(r, s2, e2, ALU.mult))
                            link(dve.tensor_tensor(w, s2, r, ALU.add))
                            link(dve.tensor_scalar(w, w, 1e-9, None, ALU.add))
                            link(dve.reciprocal(w, w))
                            link(dve.tensor_tensor(gate[:, 0, :], s2, w, ALU.mult))
                            link(dve.tensor_tensor(gate[:, 1, :], r, w, ALU.mult))
                        dve.wait_ge(pos, 1)
                        place = bank(3)[:, 0:E * NQT].rearrange("p (e t) -> p e t", e=E)
                        places["rows"](dve, link, place, bank(4)[:, 0:E], row, iota_e, pick, cst)
                        for k in range(2):
                            link(dve.tensor_tensor(pick[:, :, :], row[:, :, :], hot[:, k, :, :], ALU.mult))
                            link(dve.tensor_reduce(srow[:, k, :], pick[:, :, :].rearrange("p e t -> p t e"), AX.X, ALU.add))
                        if L:
                            for k in range(2):
                                link(dve.tensor_scalar(w, srow[:, k, :], float(ROWS), None, ALU.is_lt))
                                link(dve.tensor_tensor(gate[:, k, :], gate[:, k, :], w, ALU.mult))
                        link(dve.tensor_scalar(gate[:, :, :], gate[:, :, :], gates[:, 2 + L:3 + L], None, ALU.mult))
                        link(dve.tensor_copy(slot[:, :, :], srow[:, :, :]))
                        dve.sem_inc(slots_s, 1)
                return scatter, scat

        def experts0(xs, ys, tile_e, ends, pairs, ws, w_ld, b_ld):
            w1, w2, b1r, b2 = ws
            NF = F0 // P
            NJ = NF // 2
            NW = 32
            with ExitStack() as st:
                b1 = sb(st, "b1", [P, P])
                xt = sb(st, "xt", [P, 2, D])
                xTt = sb(st, "xTt", [P, 2, KD, P])
                sil = sb(st, "sil", [P, NJ, 2, P])
                hT = sb(st, "hT", [P, 2, F0])
                yv = sb(st, "yv", [P, 2, D])
                mi = sb(st, "mi", [P, 2, S], I32)
                off = sb(st, "mask_off", [P, S], BF16)
                mask_ld = [sem(f"e0_mask_loaded{i}") for i in range(2)]
                seen, counted = sem("e0_mask_seen"), sem("e0_mask_counted")
                x_ld = [sem(f"e0_rows{i}") for i in range(2)]
                y_st = [sem(f"e0_stored{i}") for i in range(2)]
                xtr, xte, u, si, hd, y, ye = (
                    sem(f"e0_{n}") for n in ("x_transposed", "xT", "up", "silu", "hidden", "down", "down_read"))
                btr, bt, kload = sem("e0_bias_transposed"), sem("e0_bias"), sem("e0_kstack")

                def pair_count(eng):
                    return eng.value_load(pairs[0:1, 0:1], min_val=1, max_val=NT0 // 2)

                with nc.Block() as block:
                    @block.gpsimd
                    def _(pool):
                        def load_mask(t):
                            pool.dma_start(mi[:, t % 2, :], mask_d[t * P:(t + 1) * P, :]).then_inc(mask_ld[t % 2], 16)

                        def count_mask(t):
                            pool.wait_ge(mask_ld[t % 2], 16 * (t // 2 + 1))
                            pool.tensor_scalar(off[:, :], mi[:, t % 2, :], 0, None, ALU.is_equal).then_inc(seen, 1)
                            pool.wait_ge(seen, t + 1)
                            pool.tensor_tensor(ignored[:, :], ignored[:, :], off[:, :], ALU.add).then_inc(counted, 1)
                            pool.wait_ge(counted, t + 2)
                            if t + 2 < NQT:
                                load_mask(t + 2)

                        pool.memset(ignored[:, :], 0.0).then_inc(counted, 1)
                        pool.wait_ge(counted, 1)
                        load_mask(0)
                        load_mask(1)
                        for e in range(2, E0):
                            for t in range(NQT * (e - 2) // (E0 - 2), NQT * (e - 1) // (E0 - 2)):
                                count_mask(t)
                            last = pool.value_load(ends[0:1, e - 2:e - 1], min_val=2, max_val=NT0 + 2)
                            pool.wait_ge(w_ld, NW * e)
                            pool.wait_ge(ye, last)
                            load_expert(pool, e, w1, w2, w_ld)
                        pool.wait_ge(w_ld, NW * E0)
                        pool.wait_ge(kload, 16 * len(PAIRS))
                        count = pair_count(pool)
                        for z in range(2):
                            pool.wait_ge(y_st[z], count * 16 + 16)
                            pool.wait_ge(x_ld[z], count * 16 + 16)

                    @block.sync
                    def _(sp):
                        def load_rows(first, z):
                            sp.dma_start(xt[:, z, :], xs[bass.ds(first, P), :]).then_inc(x_ld[z], 16)

                        for z in range(2):
                            sp.sem_inc(y_st[z], 16)
                            load_rows(z * P, z)
                        load_key_stack(sp, 1, Ks, kload)
                        with sp.Fori(0, pair_count(sp)) as it:
                            for z in range(2):
                                sp.wait_ge(xtr, it * 2 + (z + 1))
                                load_rows(it * (2 * P) + (2 + z) * P, z)
                            for z in range(2):
                                sp.wait_ge(ye, it * 2 + (z + 3))
                                sp.dma_start(ys[bass.ds(it * (2 * P) + z * P, P), :], yv[:, z, :]).then_inc(y_st[z], 16)

                    @block.tensor
                    def _(pe):
                        pe.sem_inc(y, 2)
                        pe.wait_ge(b_ld, 32)
                        pe.transpose(bank(4)[:, 0:P], b1r[:, :], ident[:, :]).then_inc(btr, 1)

                        def turn_x(z):
                            for k in range(KD):
                                mmi = pe.transpose(bank(6 + z)[:, k * P:(k + 1) * P], xt[:, z, k * P:(k + 1) * P], ident[:, :])
                            mmi.then_inc(xtr, 1)

                        def up(it, z, side):
                            for j in range(NJ):
                                pe.wait_ge(hd, it * (2 * NJ) + (z * NJ + j + 1))
                                for i, f in enumerate((2 * j, 2 * j + 1, NF + 2 * j, NF + 2 * j + 1)):
                                    for k in range(KD):
                                        mmi = pe.matmul(bank(j)[:, i * P:(i + 1) * P], w1[:, side, k, f * P:(f + 1) * P],
                                                        xTt[:, z, k, :], start=(k == 0), stop=(k == KD - 1))
                                mmi.then_inc(u, 1)

                        def down(it, z, odd):
                            pe.wait_ge(ye, it * 2 + (z + 1))
                            for f in range(NF):
                                if f % 2 == 0:
                                    pe.wait_ge(hd, it * (2 * NJ) + (z * NJ + f // 2 + 5))
                                mmi = pe.matmul(bank(4 + z)[:, 0:D], hT[:, z, f * P:(f + 1) * P],
                                                w2[:, bass.ds(odd * (NF * D) + f * D, D)],
                                                start=(f == 0), stop=(f == NF - 1))
                            mmi.then_inc(y, 1)

                        for z in range(2):
                            pe.wait_ge(x_ld[z], 16)
                            turn_x(z)
                        pe.wait_ge(bt, 1)
                        with pe.Fori(0, pair_count(pe)) as it:
                            expert = [pe.value_load(tile_e[0:1, 0, bass.ds(it * 2 + z, 1)], min_val=0, max_val=E0 - 1)
                                      for z in range(2)]
                            odd = [pe.value_load(tile_e[0:1, 1, bass.ds(it * 2 + z, 1)], min_val=0, max_val=1)
                                   for z in range(2)]
                            for z in range(2):
                                pe.wait_ge(w_ld, expert[z] * NW + NW)
                                pe.wait_ge(xte, it * 2 + (z + 1))
                                with pe.If(odd[z] > 0):
                                    up(it, z, 1)
                                with pe.Else():
                                    up(it, z, 0)
                            for z in range(2):
                                pe.wait_ge(x_ld[z], it * 16 + 32)
                                turn_x(z)
                            for z in range(2):
                                down(it, z, odd[z])

                    @block.scalar
                    def _(act):
                        act.wait_ge(btr, 1)
                        act.activation(b1[:, :], bank(4)[:, 0:P], ACT.Copy).then_inc(bt, 1)

                        def x_out(n, z):
                            act.wait_ge(xtr, n + 1)
                            act.activation(xTt[:, z, :, :].rearrange("p k t -> p (k t)"), bank(6 + z)[:, 0:D], ACT.Copy)\
                               .then_inc(xte, 1)
                        x_out(0, 0)
                        x_out(1, 1)
                        act.wait_ge(bt, 1)
                        with act.Fori(0, pair_count(act)) as it:
                            for z in range(2):
                                e = act.value_load(tile_e[0:1, 0, bass.ds(it * 2 + z, 1)], min_val=0, max_val=E0 - 1)
                                for j in range(NJ):
                                    act.wait_ge(u, it * (2 * NJ) + (z * NJ + j + 1))
                                    for i in range(2):
                                        last = act.activation(sil[:, j, i, :], bank(j)[:, i * P:(i + 1) * P], ACT.Silu,
                                                              bias=b1[:, bass.ds(e * (2 * NF) + (2 * j + i), 1)])
                                    last.then_inc(si, 1)
                            for z in range(2):
                                x_out(it * 2 + (z + 2), z)

                    @block.vector
                    def _(dve):
                        dve.sem_inc(hd, NJ)
                        dve.sem_inc(ye, 2)
                        dve.wait_ge(bt, 1)
                        with dve.Fori(0, pair_count(dve)) as it:
                            experts = []
                            for z in range(2):
                                e = dve.value_load(tile_e[0:1, 0, bass.ds(it * 2 + z, 1)], min_val=0, max_val=E0 - 1)
                                experts.append(e)
                                dve.wait_ge(y, it * 2 + (z + 1))
                                for j in range(NJ):
                                    dve.wait_ge(si, it * (2 * NJ) + (z * NJ + j + 1))
                                    for i in range(2):
                                        f = 2 * j + i
                                        last = dve.scalar_tensor_tensor(
                                            out=hT[:, z, f * P:(f + 1) * P], in0=bank(j)[:, (2 + i) * P:(3 + i) * P],
                                            scalar=b1[:, bass.ds(e * (2 * NF) + (NF + f), 1)], in1=sil[:, j, i, :],
                                            op0=ALU.add, op1=ALU.mult)
                                    last.then_inc(hd, 1)
                            for z in range(2):
                                dve.wait_ge(y, it * 2 + (z + 3))
                                dve.wait_ge(y_st[z], it * 16 + 16)
                                dve.tensor_tensor(yv[:, z, :], bank(4 + z)[:, 0:D],
                                                  b2[:, bass.ds(experts[z] * D, D)], ALU.add).then_inc(ye, 1)

        MF = [(m * P, min(P, F1 - m * P)) for m in range(-(-F1 // P))]
        NM = len(MF)
        WB = 4
        SHARED = WB

        def load_mlp(queue, at, gate_d, up_d, down_d, wts, done):
            wg, wu, wd = wts
            full = F1 // P * P
            queue.dma_start(wg[:, at, :, :], gate_d.rearrange("(k p) n -> p k n", p=P)).then_inc(done, 16)
            queue.dma_start(wu[:, at, :, :], up_d.rearrange("(k p) n -> p k n", p=P)).then_inc(done, 16)
            queue.dma_start(wd[:, at, 0:F1 // P, :], down_d[0:full, :].rearrange("(m p) n -> p m n", p=P)).then_inc(done, 16)
            queue.dma_start(wd[0:F1 - full, at, F1 // P, :], down_d[full:F1, :]).then_inc(done, 16)

        def experts1(xs, ys, xn, xT, wts, w_ld, scatter, scat):
            wg, wu, wd = wts
            CT = [(i * P, min(P, CAP - i * P)) for i in range(-(-CAP // P))]
            full = CAP // P * P
            with ExitStack() as st:
                xe = sb(st, "xe", [P, 2, len(CT), D])
                xTe = sb(st, "xTe", [P, 2, KD, CAP])
                sil = sb(st, "sil1", [P, 2, 512])
                hT1 = sb(st, "hT1", [P, 2, NM, 512])
                ye1 = sb(st, "ye1", [P, 2, len(CT), D])
                xn_in = sem("s1_normed_added")
                x_ld = [sem(f"e1_rows{i}") for i in range(2)]
                y_st = [sem(f"e1_stored{i}") for i in range(2)]
                xtr, xte, gu, si, h, y, ye = (
                    sem(f"e1_{n}") for n in ("x_transposed", "xT", "gate_up", "silu", "hidden", "down", "down_read"))
                s_gu, s_si, s_h, s_y, s_ye = (sem(f"s1_{n}") for n in ("gate_up", "silu", "hidden", "down", "down_read"))
                NI1 = E1 // WB

                with nc.Block() as block:
                    @block.sync
                    def _(sp):
                        def load_rows(r, z):
                            sp.dma_start(xe[:, z, 0:CAP // P, :],
                                         xs[bass.ds(r, full), :].rearrange("(m p) n -> p m n", p=P)).then_inc(x_ld[z], 16)
                            sp.dma_start(xe[0:CAP - full, z, CAP // P, :],
                                         xs[bass.ds(r + full, CAP - full), :]).then_inc(x_ld[z], 16)

                        sp.wait_ge(scat, 16 * 2 * NQT)
                        for z in range(2):
                            sp.sem_inc(y_st[z], 32)
                            load_rows(z * CAP, z)
                        with sp.Fori(0, NI1) as it:
                            for q0 in range(0, WB, 2):
                                for z in range(2):
                                    sp.wait_ge(xtr, it * WB + (q0 + z + 1))
                                    load_rows(it * (WB * CAP) + (q0 + z + 2) * CAP, z)
                                for z in range(2):
                                    sp.wait_ge(ye, it * WB + (q0 + z + 2))
                                    r = it * (WB * CAP) + (q0 + z) * CAP
                                    sp.dma_start(ys[bass.ds(r, full), :].rearrange("(m p) n -> p m n", p=P),
                                                 ye1[:, z, 0:CAP // P, :]).then_inc(y_st[z], 16)
                                    sp.dma_start(ys[bass.ds(r + full, CAP - full), :],
                                                 ye1[0:CAP - full, z, CAP // P, :]).then_inc(y_st[z], 16)
                        for z in range(2):
                            sp.wait_ge(y_st[z], 32 + 32 * (E1 // 2))
                            sp.wait_ge(x_ld[z], 32 + 32 * (E1 // 2))

                    @block.gpsimd
                    def _(pool):
                        scatter(pool)
                        for e in range(WB, E1):
                            pool.wait_ge(y, 2 + e - WB + 1)
                            load_mlp(pool, e % WB, F["w_gate"][e], F["w_up"][e], F["w_down"][e], wts, w_ld[e % WB])

                    @block.tensor
                    def _(pe):
                        pe.wait_ge(w_ld[SHARED], 64)

                        def shared_down(c):
                            pe.wait_ge(s_h, (c + 1) * NM)
                            for q in range(QTC):
                                j = c * QTC + q
                                if j >= 2:
                                    pe.wait_ge(s_ye, j - 1)
                                for m, (f0, fw) in enumerate(MF):
                                    mmi = pe.matmul(bank(4 + j % 2)[:, 0:D], hT1[0:fw, c % 2, m, q * P:(q + 1) * P],
                                                    wd[0:fw, SHARED, m, :], start=(m == 0), stop=(m == NM - 1))
                                mmi.then_inc(s_y, 1)

                        for c in range(NC):
                            for m, (f0, fw) in enumerate(MF):
                                n = c * NM + m
                                if n >= 2:
                                    pe.wait_ge(s_h, n - 1)
                                for i, w in enumerate((wg, wu)):
                                    for k in range(KD):
                                        mmi = pe.matmul(bank(2 * (n % 2) + i)[0:fw, :], w[:, SHARED, k, f0:f0 + fw],
                                                        xT[:, k, c * QC:(c + 1) * QC], start=(k == 0), stop=(k == KD - 1))
                                mmi.then_inc(s_gu, 1)
                            if c:
                                shared_down(c - 1)
                        shared_down(NC - 1)

                        def turn_x(z):
                            for k in range(KD):
                                for i, (c0, cw) in enumerate(CT):
                                    mmi = pe.transpose(bank(6 + k)[:, c0:c0 + cw], xe[0:cw, z, i, k * P:(k + 1) * P],
                                                       ident[0:cw, 0:cw])
                            mmi.then_inc(xtr, 1)

                        def up(it, q):
                            z = q % 2
                            pe.wait_ge(w_ld[q], it * 64 + 64)
                            pe.wait_ge(xte, it * (2 * WB) + 2 * (q + 1))
                            for m, (f0, fw) in enumerate(MF):
                                pe.wait_ge(h, it * (WB * NM) + (NM * q + m + 1))
                                b = (NM * q + m) % 2
                                for i, w in enumerate((wg, wu)):
                                    for k in range(KD):
                                        mmi = pe.matmul(bank(2 * b + i)[0:fw, 0:CAP], w[:, q, k, f0:f0 + fw],
                                                        xTe[:, z, k, :], start=(k == 0), stop=(k == KD - 1))
                                mmi.then_inc(gu, 1)

                        def down(it, q):
                            z = q % 2
                            pe.wait_ge(h, it * (WB * NM) + (NM * q + NM + 2))
                            pe.wait_ge(ye, it * WB + (q + 1))
                            for i, (c0, cw) in enumerate(CT):
                                for m, (f0, fw) in enumerate(MF):
                                    mmi = pe.matmul(bank(4 + i // 2)[0:cw, (i % 2) * D:(i % 2 + 1) * D],
                                                    hT1[0:fw, z, m, c0:c0 + cw], wd[0:fw, q, m, :],
                                                    start=(m == 0), stop=(m == NM - 1))
                            mmi.then_inc(y, 1)

                        for z in range(2):
                            pe.wait_ge(x_ld[z], 32)
                            if z:
                                pe.wait_ge(xte, 2)
                            turn_x(z)
                        pe.wait_ge(s_ye, NQT)
                        pe.sem_inc(y, 2)
                        with pe.Fori(0, NI1) as it:
                            for q0 in range(0, WB, 2):
                                up(it, q0)
                                up(it, q0 + 1)
                                for q in (q0, q0 + 1):
                                    down(it, q)
                                    pe.wait_ge(x_ld[q % 2], it * (32 * WB // 2) + 32 * (q // 2 + 2))
                                    pe.wait_ge(xte, it * (2 * WB) + (2 * q + 4))
                                    turn_x(q % 2)

                    @block.scalar
                    def _(act):
                        act.sem_inc(ye, 1)
                        for n in range(NC * NM):
                            fw = MF[n % NM][1]
                            act.wait_ge(s_gu, n + 1)
                            if n >= 2:
                                act.wait_ge(s_h, n - 1)
                            act.activation(sil[0:fw, n % 2, :], bank(2 * (n % 2))[0:fw, :], ACT.Silu).then_inc(s_si, 1)
                        act.wait_ge(s_h, NC * NM)

                        def x_out(n, z):
                            act.wait_ge(xtr, n + 1)
                            for k in range(KD):
                                act.activation(xTe[:, z, k, :], bank(6 + k)[:, 0:CAP], ACT.Copy).then_inc(xte, 1)

                        for z in range(2):
                            x_out(z, z)
                        with act.Fori(0, NI1) as it:
                            for q0 in range(0, WB, 2):
                                for q in (q0, q0 + 1):
                                    for m, (f0, fw) in enumerate(MF):
                                        b = (NM * q + m) % 2
                                        act.wait_ge(gu, it * (WB * NM) + (NM * q + m + 1))
                                        act.wait_ge(h, it * (WB * NM) + (NM * q + m + 1))
                                        act.activation(sil[0:fw, b, 0:CAP], bank(2 * b)[0:fw, 0:CAP], ACT.Silu)\
                                           .then_inc(si, 1)
                                for q in (q0, q0 + 1):
                                    z = q % 2
                                    act.wait_ge(y, it * WB + (q + 3))
                                    act.wait_ge(y_st[z], it * (32 * WB // 2) + 32 * (q // 2 + 1))
                                    act.activation(ye1[:, z, 0:2, :].rearrange("p a d -> p (a d)"), bank(4), ACT.Copy)
                                    act.activation(ye1[0:CT[2][1], z, 2, :], bank(5)[0:CT[2][1], 0:D], ACT.Copy).then_inc(ye, 1)
                                    x_out(it * WB + (q + 2), z)

                    @block.vector
                    def _(dve):
                        dve.sem_inc(h, 2)
                        for j in range(NQT):
                            dve.scalar_tensor_tensor(out=xres[:, j, :], in0=xn[:, j, :], scalar=gates[:, 3:4],
                                                     in1=xres[:, j, :], op0=ALU.mult, op1=ALU.add).then_inc(xn_in, 1)

                        def shared_out(c):
                            for q in range(QTC):
                                j = c * QTC + q
                                dve.wait_ge(s_y, j + 1)
                                dve.wait_ge(xn_in, j + 1)
                                dve.scalar_tensor_tensor(out=xres[:, j, :], in0=bank(4 + j % 2)[:, 0:D], scalar=gates[:, 3:4],
                                                         in1=xres[:, j, :], op0=ALU.mult, op1=ALU.add).then_inc(s_ye, 1)
                        for c in range(NC):
                            for m, (f0, fw) in enumerate(MF):
                                n = c * NM + m
                                dve.wait_ge(s_si, n + 1)
                                dve.tensor_tensor(hT1[0:fw, c % 2, m, :], sil[0:fw, n % 2, :],
                                                  bank(2 * (n % 2) + 1)[0:fw, :], ALU.mult).then_inc(s_h, 1)
                            if c:
                                shared_out(c - 1)
                        shared_out(NC - 1)
                        with dve.Fori(0, NI1) as it:
                            for q in range(WB):
                                dve.wait_ge(y, it * WB + (q + 1))
                                for m, (f0, fw) in enumerate(MF):
                                    b = (NM * q + m) % 2
                                    dve.wait_ge(si, it * (WB * NM) + (NM * q + m + 1))
                                    dve.tensor_tensor(hT1[0:fw, q % 2, m, 0:CAP], sil[0:fw, b, 0:CAP],
                                                      bank(2 * b + 1)[0:fw, 0:CAP], ALU.mult).then_inc(h, 1)

        def combine(L, ys, gate, slot):
            with ExitStack() as st:
                NR = 8
                yg = sb(st, f"yg{L}", [P, NR, D])
                zs, used, stat = sem(f"c{L}_zeroed"), sem(f"c{L}_used"), sem(f"c{L}_stats")
                got = [sem(f"c{L}_gathered{i}") for i in range(NR)]
                if L == 0:
                    mask_gpsimd, mask_tensor, mask_vector = summarise_mask(st)
                stored = sem("out_stored") if L else None
                with nc.Block() as block:
                    @block.gpsimd
                    def _(pool):
                        pool.memset(yg[:, :, :], 0.0).then_inc(zs, 1)
                        if L == 0:
                            mask_gpsimd(pool)
                        pool.wait_ge(zs, 1)
                        for n in range(2 * NQT):
                            t, k = n // 2, n % 2
                            if n >= NR:
                                pool.wait_ge(used, n - NR + 1)
                            pool.indirect_dma_start(
                                yg[:, n % NR, :], None, ys[:, :],
                                bass.IndirectOffsetOnAxis(ap=slot[:, k, t:t + 1], axis=0),
                                bounds_check=ROWS - 1, oob_is_err=False).then_inc(got[n % NR], 16)

                    if L == 0:
                        block.tensor(mask_tensor)

                    @block.vector
                    def _(dve):
                        if L == 0:
                            mask_vector(dve)
                        for n in range(2 * NQT):
                            t, k = n // 2, n % 2
                            dve.wait_ge(got[n % NR], 16 * (n // NR + 1))
                            if k:
                                dve.wait_ge(used, n)
                            dve.scalar_tensor_tensor(out=xres[:, t, :], in0=yg[:, n % NR, :], scalar=gate[:, k, t:t + 1],
                                                     in1=xres[:, t, :], op0=ALU.mult, op1=ALU.add).then_inc(used, 1)
                            if L == 0 and k:
                                dve.wait_ge(used, n + 1)
                                dve.bn_stats(stats[:, t, :], xres[:, t, :]).then_inc(stat, 1)

                    if L:
                        @block.sync
                        def _(sp):
                            o = out_d.rearrange("(t p) d -> p t d", p=P)
                            for g in range(NC):
                                sp.wait_ge(used, 2 * QTC * (g + 1))
                                sp.dma_start(o[:, g * QTC:(g + 1) * QTC, :], xres[:, g * QTC:(g + 1) * QTC, :])\
                                  .then_inc(stored, 16)
                            sp.wait_ge(stored, 16 * NC)

        def ffn_layer(L):
            with ExitStack() as st:
                E = (E0, E1)[L]
                gate = sb(st, f"gate{L}", [P, 2, NQT])
                slot = sb(st, f"slot{L}", [P, 2, NQT], U32)
                xn = sb(st, f"fxn{L}", [P, NQT, D])
                places = {}
                if L == 0:
                    pairs = sb(st, "pairs", [P, 1], I32)
                    pairs_f = sb(st, "pairs_f", [P, 1])
                    w1 = sb(st, "w1", [P, 2, KD, 2 * F0])
                    w2 = sb(st, "w2", [P, 2 * (F0 // P) * D])
                    b1r = sb(st, "b1r", [P, P])
                    b2 = sb(st, "b2", [P, E0 * D])
                    w_ld, b_ld = sem("e0_weights"), sem("e0_biases_loaded")

                    def loads(sp):
                        sp.dma_start(b1r[:, :], F["b1"].rearrange("e (f p) -> (e f) p", p=P)).then_inc(b_ld, 16)
                        sp.dma_start(b2[:, :], F["b2"].rearrange("(a e) d -> a (e d)", a=1).to_broadcast([P, E0 * D]))\
                          .then_inc(b_ld, 16)

                    def first_weights(pool, e):
                        if e:
                            pool.wait_ge(w_ld, 32)
                        load_expert(pool, e, w1, w2, w_ld)
                    tile_e = sb(st, "tile_e", [P, 2, NT0], I32)
                    ends = sb(st, "ends", [P, E0], I32)
                    tile_f = sb(st, "tile_f", [P, 2, NT0])
                    cnt = sb(st, "cnt", [P, 4, E0])
                    thr_i = sb(st, "thr_i", [P, E0, NQT], I32)
                    thr = sb(st, "thr", [P, E0, NQT])
                    tno_i = sb(st, "tno_i", [P, NT0, E0 - 1], I32)
                    tno = sb(st, "tno", [P, NT0, E0 - 1])
                    sign = sb(st, "sign", [P, E0])
                    one8 = sb(st, "one8", [P, E0])

                    def consts(pool, cst):
                        pool.iota(thr_i[:, :, :], [[0, E0], [P, NQT]], base=0, channel_multiplier=0).then_inc(cst, 1)
                        pool.iota(tno_i[:, :, :], [[1, NT0], [0, E0 - 1]], base=0, channel_multiplier=0).then_inc(cst, 1)
                        pool.memset(one8[:, :], 1.0).then_inc(cst, 1)
                        pool.memset(sign[:, :].rearrange("p (a b) -> p a b", b=2)[:, :, 0], 1.0).then_inc(cst, 1)
                        pool.memset(sign[:, :].rearrange("p (a b) -> p a b", b=2)[:, :, 1], -1.0).then_inc(cst, 1)

                    def rows(dve, link, place, counts, row, iota_e, pick, cst):
                        dve.wait_ge(cst, 9)
                        link(dve.tensor_copy(thr[:, :, :], thr_i[:, :, :]))
                        link(dve.tensor_copy(tno[:, :, :], tno_i[:, :, :]))
                        n, nt, end, start = (cnt[:, i, :] for i in range(4))
                        link(dve.tensor_copy(n, counts))
                        link(dve.tensor_tensor(pick[:, :, :], thr[:, :, :], n.unsqueeze(2).to_broadcast([P, E0, NQT]), ALU.is_lt))
                        link(dve.tensor_reduce(nt, pick[:, :, :], AX.X, ALU.add))
                        link(dve.tensor_tensor_scan(end, one8[:, :], nt, 0.0, ALU.mult, ALU.add))
                        link(dve.tensor_tensor(start, end, nt, ALU.subtract))
                        link(dve.tensor_scalar(start, start, float(P), None, ALU.mult))
                        link(dve.tensor_tensor(row[:, :, :], place, start.unsqueeze(2).to_broadcast([P, E0, NQT]), ALU.add))
                        link(dve.tensor_scalar(ends[:, :], end, 2.0, None, ALU.add))
                        even = tno[:, :, 0].rearrange("p (a b) -> p a b", b=2)[:, :, 0]
                        tests = tile_f[:, 0, 0:NT0 // 2]
                        link(dve.tensor_tensor(tests, even, end[:, E0 - 1:E0].to_broadcast([P, NT0 // 2]), ALU.is_lt))
                        link(dve.tensor_reduce(pairs_f[:, :], tests, AX.X, ALU.add))
                        link(dve.tensor_copy(pairs[:, :], pairs_f[:, :]))
                        link(dve.tensor_tensor(tno[:, :, :], tno[:, :, :],
                                               end[:, 0:E0 - 1].unsqueeze(1).to_broadcast([P, NT0, E0 - 1]), ALU.is_ge))
                        link(dve.tensor_reduce(tile_f[:, 0, :], tno[:, :, :], AX.X, ALU.add))
                        link(dve.tensor_tensor(tno[:, :, :], tno[:, :, :],
                                               sign[:, 0:E0 - 1].unsqueeze(1).to_broadcast([P, NT0, E0 - 1]), ALU.mult))
                        link(dve.tensor_reduce(tile_f[:, 1, :], tno[:, :, :], AX.X, ALU.add))
                        link(dve.tensor_copy(tile_e[:, :, :], tile_f[:, :, :]))
                    places["consts"], places["rows"], places["loads"] = consts, rows, loads
                    places["weights"] = first_weights
                    with ExitStack() as rt:
                        xT = sb(rt, "fxT0", [P, KD, T])
                        scatter, scat = route(0, E, F["wrT"], None, xn, xT, gate, slot, xs0, places)

                    def rows_to_experts(pool):
                        scatter(pool)
                        first_weights(pool, 1)
                        pool.wait_ge(scat, 16 * 2 * NQT)
                    projections("c", None, 1, beside=rows_to_experts)
                    experts0(xs0, ys0, tile_e, ends, pairs, (w1, w2, b1r, b2), w_ld, b_ld)
                    combine(0, ys0, gate, slot)
                else:
                    def rows1(dve, link, place, counts, row, iota_e, pick, cst):
                        link(dve.tensor_scalar(pick[:, :, :], place, float(CAP), float(FAR), ALU.is_ge, ALU.mult))
                        link(dve.scalar_tensor_tensor(out=row[:, :, :], in0=iota_e[:, :, :], scalar=float(CAP), in1=pick[:, :, :],
                                                      op0=ALU.mult, op1=ALU.add))
                        link(dve.tensor_tensor(row[:, :, :], row[:, :, :], place, ALU.add))
                    wts = (sb(st, "wg", [P, WB + 1, KD, F1]), sb(st, "wu", [P, WB + 1, KD, F1]), sb(st, "wd", [P, WB + 1, NM, D]))
                    w_ld = [sem(f"e1_weights{i}") for i in range(WB + 1)]

                    def first_weights1(pool, e):
                        load_mlp(pool, SHARED, F["sw_gate"], F["sw_up"], F["sw_down"], wts, w_ld[SHARED])
                        for e in range(WB):
                            load_mlp(pool, e, F["w_gate"][e], F["w_up"][e], F["w_down"][e], wts, w_ld[e])
                    places["rows"], places["loads"] = rows1, lambda sp: None
                    places["weights"] = first_weights1
                    xT = sb(st, "fxT1", [P, KD, T])
                    scatter, scat = route(1, E, F["router_w"], F["router_b"], xn, xT, gate, slot, xs1, places)
                    experts1(xs1, ys1, xn, xT, wts, w_ld, scatter, scat)
                    combine(1, ys1, gate, slot)

        xs0, xs1 = scratch("rows0", [ROWS + 2 * P, D], F32), scratch("rows1", [ROWS + 2 * CAP, D], F32)
        ys0, ys1 = scratch("outs0", [ROWS, D], F32), scratch("outs1", [ROWS, D], F32)
        Ks, Vs = [scratch(f"k_parts{l}", [3, D, S], BF16) for l in range(2)], scratch("values1", [NKT, P, H * NV], F32)
        zeroed = ctx.enter_context(nc.semaphore("rows_zeroed"))

        def zero_rows(sp, s):
            for r in (xs0, xs1, ys0[2 * T:ROWS, :]):
                tiles = r.shape[0] // P
                r0, r1 = tiles * s // NC * P, tiles * (s + 1) // NC * P
                sp.dma_start(r[r0:r1, :].rearrange("(t p) d -> p t d", p=P),
                             zero[:, :].unsqueeze(1).to_broadcast([P, (r1 - r0) // P, D])).then_inc(zeroed, 16)

        for L in range(2):
            attention_layer(L)
            free_semaphores()
            ffn_layer(L)
            free_semaphores()


_NAMES = ["Wq", "bq", "Wk", "bk", "Wv", "bv", "Wo", "bo"]


def kernel(**inputs):
    import concourse.bacc as _bacc
    from concourse.bass_utils import run_bass_kernel_spmd as _run

    nc = _bacc.Bacc("TRN2", target_bir_lowering=False, num_devices=1)
    arrays = {}

    def give(name, a):
        a = np.ascontiguousarray(a)
        arrays[name] = a
        return nc.dram_tensor(name, a.shape, mybir.dt.from_np(a.dtype), kind="ExternalInput").ap()

    x = give("x", inputs["x"].reshape(T, D))
    ctxT = give("ctxT", inputs["ctx_1024"].reshape(S, D).T)
    mask = give("mask", inputs["mask_SxS2_ik0"])
    maskT = give("maskT", inputs["mask_SxS2_ik0"].T)
    gx, gf = give("g_xattn", inputs["g_xattn"]), give("g_ffn", inputs["g_ffn"])
    W = []
    for L in range(2):
        w = {}
        for n in _NAMES:
            a = inputs[f"L{L}_xattn_{n}"]
            if n[0] == "W":
                w[n + "T"] = give(f"L{L}_{n}T", a.T)
            else:
                w[n] = give(f"L{L}_{n}", a)
        W.append(w)
    out = nc.dram_tensor("out", (T, D), F32, kind="ExternalOutput").ap()
    F = {n: give(f"L0_{n}", inputs[f"L0_ffn_{n}"]) for n in ("w1", "b1", "w2", "b2")}
    F["wrT"] = give("L0_wrT", inputs["L0_ffn_wr"].T)
    for n in ("router_w", "router_b", "w_gate", "w_up", "w_down", "sw_gate", "sw_up", "sw_down"):
        F[n] = give(f"L1_{n}", inputs[f"L1_ffn_{n}"])
    build(nc, x, ctxT, mask, maskT, gx, gf, W, F, out)
    r = _run(nc, [arrays], core_ids=[0])
    return r.results[0]["out"].reshape(1, T, D)
```
